# Optimizing a Trainium2 kernel written in Bass

```python
import numpy as np
import jax
import jax.numpy as jnp

def _softmax(x, axis=-1):
    return jax.nn.softmax(x, axis=axis)

def _gelu(x):
    return jax.nn.gelu(x, approximate=True)

def _silu(x):
    return jax.nn.silu(x)

def _sigmoid(x):
    return jax.nn.sigmoid(x)

def _layernorm(x, axis=-1, eps=1e-05):
    m = jnp.mean(x, axis=axis, keepdims=True)
    v = jnp.var(x, axis=axis, keepdims=True)
    return (x - m) / jnp.sqrt(v + eps)

def _scatter_add(tgt, idx, src, axis=0):
    return tgt.at[idx].add(src)

def _segment_sum(src, seg, n):
    return jax.ops.segment_sum(src, seg, n)
kernel_name = 'mk_metaformer_d2_conv_nchw2048_r4_3d731f'

def setup_inputs(seed: int=0):
    np.random.seed(seed)
    _w = jnp.asarray

    def _rec_inputs():
        import jax
        import jax.numpy as jnp
        _gk = jax.random.key(seed)
        x = -9.26e-05 + 0.9999 * jax.random.normal(jax.random.fold_in(_gk, 1), (16, 512, 24, 12), jnp.float32)
        return x
    x = _rec_inputs()

    def _L0_conv_setup():
        import jax, jax.numpy as jnp
        import numpy as np
        B_, C_IN, H_, W_ = (16, 512, 24, 12)
        HID = 192
        INNER = 2 * HID
        N_STATE = 16
        DT_RANK = 48

        def _interp_axis(n_in, n_out):
            src = (jnp.arange(n_out, dtype=jnp.float32) + 0.5) * (n_in / n_out) - 0.5
            src = jnp.maximum(src, 0.0)
            i0 = jnp.minimum(jnp.floor(src).astype(jnp.int32), n_in - 1)
            i1 = jnp.minimum(i0 + 1, n_in - 1)
            w = src - i0.astype(jnp.float32)
            return (i0, i1, w)
        key = jax.random.key(seed)
        ks = jax.random.split(key, 8)
        s = 0.02
        return {'x': jax.random.normal(ks[0], (B_, C_IN, H_, W_), jnp.float32), 'pe_W': jax.random.normal(ks[1], (C_IN, HID), jnp.float32) * s, 'pe_b': jnp.zeros((HID,), jnp.float32), 'ln_g': jnp.ones((HID,), jnp.float32), 'ln_b': jnp.zeros((HID,), jnp.float32), 'in_W': jax.random.normal(ks[2], (HID, 2 * INNER), jnp.float32) * s, 'conv_w': jax.random.normal(ks[3], (INNER, 1, 3), jnp.float32) * s, 'conv_b': jnp.zeros((INNER,), jnp.float32), 'xproj_W': jax.random.normal(ks[4], (INNER, DT_RANK + 2 * N_STATE), jnp.float32) * s, 'dt_W': jax.random.normal(ks[5], (DT_RANK, INNER), jnp.float32) * s, 'dt_b': jnp.zeros((INNER,), jnp.float32), 'A_log': jnp.log(jnp.broadcast_to(jnp.arange(1, N_STATE + 1, dtype=jnp.float32), (INNER, N_STATE))), 'D_param': jnp.ones((INNER,), jnp.float32), 'out_W': jax.random.normal(ks[6], (INNER, C_IN), jnp.float32) * s}
    _L0_conv_all = _L0_conv_setup()
    _L0_conv_in = {k: v for k, v in _L0_conv_all.items() if k in ('pe_W', 'pe_b', 'ln_g', 'ln_b', 'in_W', 'conv_w', 'conv_b', 'xproj_W', 'dt_W', 'dt_b', 'A_log', 'D_param', 'out_W')}
    del _L0_conv_all

    def _L0_ffn_setup():
        import jax, jax.numpy as jnp
        import numpy as np
        NUM_EXPERTS = 4
        key = jax.random.key(seed)
        k1, k2, k3 = jax.random.split(key, 3)
        B, N, H = (8, 512, 512)
        E = NUM_EXPERTS
        I = H * 4 // E
        x = jax.random.normal(k1, (B, N, H), dtype=jnp.float32)
        gate_up_proj = jax.random.normal(k2, (E, H, 2 * I), dtype=jnp.float32) * 0.02
        down_proj = jax.random.normal(k3, (E, I, H), dtype=jnp.float32) * 0.02
        return {'x': x, 'gate_up_proj': gate_up_proj, 'down_proj': down_proj}
    _L0_ffn_all = _L0_ffn_setup()
    _L0_ffn_in = {k: v for k, v in _L0_ffn_all.items() if k in ('gate_up_proj', 'down_proj')}
    del _L0_ffn_all

    def _L1_conv_setup():
        import jax, jax.numpy as jnp
        import numpy as np
        B_, C_IN, H_, W_ = (16, 512, 24, 12)
        HID = 192
        INNER = 2 * HID
        N_STATE = 16
        DT_RANK = 48

        def _interp_axis(n_in, n_out):
            src = (jnp.arange(n_out, dtype=jnp.float32) + 0.5) * (n_in / n_out) - 0.5
            src = jnp.maximum(src, 0.0)
            i0 = jnp.minimum(jnp.floor(src).astype(jnp.int32), n_in - 1)
            i1 = jnp.minimum(i0 + 1, n_in - 1)
            w = src - i0.astype(jnp.float32)
            return (i0, i1, w)
        key = jax.random.key(seed)
        ks = jax.random.split(key, 8)
        s = 0.02
        return {'x': jax.random.normal(ks[0], (B_, C_IN, H_, W_), jnp.float32), 'pe_W': jax.random.normal(ks[1], (C_IN, HID), jnp.float32) * s, 'pe_b': jnp.zeros((HID,), jnp.float32), 'ln_g': jnp.ones((HID,), jnp.float32), 'ln_b': jnp.zeros((HID,), jnp.float32), 'in_W': jax.random.normal(ks[2], (HID, 2 * INNER), jnp.float32) * s, 'conv_w': jax.random.normal(ks[3], (INNER, 1, 3), jnp.float32) * s, 'conv_b': jnp.zeros((INNER,), jnp.float32), 'xproj_W': jax.random.normal(ks[4], (INNER, DT_RANK + 2 * N_STATE), jnp.float32) * s, 'dt_W': jax.random.normal(ks[5], (DT_RANK, INNER), jnp.float32) * s, 'dt_b': jnp.zeros((INNER,), jnp.float32), 'A_log': jnp.log(jnp.broadcast_to(jnp.arange(1, N_STATE + 1, dtype=jnp.float32), (INNER, N_STATE))), 'D_param': jnp.ones((INNER,), jnp.float32), 'out_W': jax.random.normal(ks[6], (INNER, C_IN), jnp.float32) * s}
    _L1_conv_all = _L1_conv_setup()
    _L1_conv_in = {k: v for k, v in _L1_conv_all.items() if k in ('pe_W', 'pe_b', 'ln_g', 'ln_b', 'in_W', 'conv_w', 'conv_b', 'xproj_W', 'dt_W', 'dt_b', 'A_log', 'D_param', 'out_W')}
    del _L1_conv_all

    def _L1_ffn_setup():
        import jax, jax.numpy as jnp
        import numpy as np
        NUM_EXPERTS = 8
        TOP_K = 2
        MODEL_DIM = 512
        INTER_DIM = 256
        GATE_SCALE = 1.0
        UP_SCALE = 0.0
        key = jax.random.key(seed)
        k1, k2, k3, k4 = jax.random.split(key, 4)
        hidden_states = jax.random.normal(k1, (2, 512, MODEL_DIM), jnp.float32)
        router_gate = jax.random.normal(k2, (NUM_EXPERTS, MODEL_DIM), jnp.float32) * 0.02
        expert_gate_up = jax.random.normal(k3, (NUM_EXPERTS, MODEL_DIM, 2 * INTER_DIM), jnp.float32) * 0.02
        expert_down = jax.random.normal(k4, (NUM_EXPERTS, INTER_DIM, MODEL_DIM), jnp.float32) * 0.02
        return {'hidden_states': hidden_states, 'router_gate': router_gate, 'expert_gate_up': expert_gate_up, 'expert_down': expert_down}
    _L1_ffn_all = _L1_ffn_setup()
    _L1_ffn_in = {k: v for k, v in _L1_ffn_all.items() if k in ('router_gate', 'expert_gate_up', 'expert_down')}
    del _L1_ffn_all
    return {'x': x, 'L0_conv_pe_W': _L0_conv_in['pe_W'], 'L0_conv_pe_b': _L0_conv_in['pe_b'], 'L0_conv_ln_g': _L0_conv_in['ln_g'], 'L0_conv_ln_b': _L0_conv_in['ln_b'], 'L0_conv_in_W': _L0_conv_in['in_W'], 'L0_conv_conv_w': _L0_conv_in['conv_w'], 'L0_conv_conv_b': _L0_conv_in['conv_b'], 'L0_conv_xproj_W': _L0_conv_in['xproj_W'], 'L0_conv_dt_W': _L0_conv_in['dt_W'], 'L0_conv_dt_b': _L0_conv_in['dt_b'], 'L0_conv_A_log': _L0_conv_in['A_log'], 'L0_conv_D_param': _L0_conv_in['D_param'], 'L0_conv_out_W': _L0_conv_in['out_W'], 'L0_ffn_gate_up_proj': _L0_ffn_in['gate_up_proj'], 'L0_ffn_down_proj': _L0_ffn_in['down_proj'], 'L1_conv_pe_W': _L1_conv_in['pe_W'], 'L1_conv_pe_b': _L1_conv_in['pe_b'], 'L1_conv_ln_g': _L1_conv_in['ln_g'], 'L1_conv_ln_b': _L1_conv_in['ln_b'], 'L1_conv_in_W': _L1_conv_in['in_W'], 'L1_conv_conv_w': _L1_conv_in['conv_w'], 'L1_conv_conv_b': _L1_conv_in['conv_b'], 'L1_conv_xproj_W': _L1_conv_in['xproj_W'], 'L1_conv_dt_W': _L1_conv_in['dt_W'], 'L1_conv_dt_b': _L1_conv_in['dt_b'], 'L1_conv_A_log': _L1_conv_in['A_log'], 'L1_conv_D_param': _L1_conv_in['D_param'], 'L1_conv_out_W': _L1_conv_in['out_W'], 'L1_ffn_router_gate': _L1_ffn_in['router_gate'], 'L1_ffn_expert_gate_up': _L1_ffn_in['expert_gate_up'], 'L1_ffn_expert_down': _L1_ffn_in['expert_down']}

def reference(x, L0_conv_pe_W, L0_conv_pe_b, L0_conv_ln_g, L0_conv_ln_b, L0_conv_in_W, L0_conv_conv_w, L0_conv_conv_b, L0_conv_xproj_W, L0_conv_dt_W, L0_conv_dt_b, L0_conv_A_log, L0_conv_D_param, L0_conv_out_W, L0_ffn_gate_up_proj, L0_ffn_down_proj, L1_conv_pe_W, L1_conv_pe_b, L1_conv_ln_g, L1_conv_ln_b, L1_conv_in_W, L1_conv_conv_w, L1_conv_conv_b, L1_conv_xproj_W, L1_conv_dt_W, L1_conv_dt_b, L1_conv_A_log, L1_conv_D_param, L1_conv_out_W, L1_ffn_router_gate, L1_ffn_expert_gate_up, L1_ffn_expert_down):
    import jax
    import jax.numpy as jnp

    def _L0_conv_ref(x, pe_W, pe_b, ln_g, ln_b, in_W, conv_w, conv_b, xproj_W, dt_W, dt_b, A_log, D_param, out_W):
        import jax, jax.numpy as jnp
        import numpy as np
        B_, C_IN, H_, W_ = (16, 512, 24, 12)
        HID = 192
        INNER = 2 * HID
        N_STATE = 16
        DT_RANK = 48

        def _interp_axis(n_in, n_out):
            src = (jnp.arange(n_out, dtype=jnp.float32) + 0.5) * (n_in / n_out) - 0.5
            src = jnp.maximum(src, 0.0)
            i0 = jnp.minimum(jnp.floor(src).astype(jnp.int32), n_in - 1)
            i1 = jnp.minimum(i0 + 1, n_in - 1)
            w = src - i0.astype(jnp.float32)
            return (i0, i1, w)
        B, C, H, W = x.shape
        D_in = conv_w.shape[0]
        dt_rank = dt_W.shape[0]
        nstate = A_log.shape[1]
        p = x.reshape(B, C, 3, H // 3, 3, W // 3).mean(axis=(3, 5))
        tok = p.reshape(B, C, 9).transpose(0, 2, 1) @ pe_W + pe_b
        mu = tok.mean(-1, keepdims=True)
        var = jnp.mean((tok - mu) ** 2, axis=-1, keepdims=True)
        t = (tok - mu) / jnp.sqrt(var + 1e-05) * ln_g + ln_b
        xz = t @ in_W
        xc, z = jnp.split(xz, [D_in], axis=-1)
        xdl = xc.transpose(0, 2, 1)
        xdl = jax.lax.conv_general_dilated(xdl, conv_w, (1,), [(1, 1)], dimension_numbers=('NCH', 'OIH', 'NCH'), feature_group_count=D_in) + conv_b[None, :, None]
        u = jax.nn.silu(xdl.transpose(0, 2, 1))
        A = -jnp.exp(A_log)
        dBC = u @ xproj_W
        dlt, Bp, Cp = jnp.split(dBC, [dt_rank, dt_rank + nstate], axis=-1)
        delta = jax.nn.softplus(dlt @ dt_W + dt_b)

        def step(state, inp):
            u_l, d_l, B_l, C_l = inp
            k1 = A[None] * state + B_l[:, None, :] * u_l[:, :, None]
            state = state + d_l[:, :, None] * k1
            y_l = jnp.einsum('bdn,bn->bd', state, C_l)
            return (state, y_l)
        st0 = jnp.zeros((B, D_in, nstate), u.dtype)
        _, ys = jax.lax.scan(step, st0, (u.transpose(1, 0, 2), delta.transpose(1, 0, 2), Bp.transpose(1, 0, 2), Cp.transpose(1, 0, 2)))
        y = ys.transpose(1, 0, 2) + u * D_param
        y = y * jax.nn.silu(z)
        out_tok = y @ out_W
        g = out_tok.transpose(0, 2, 1).reshape(B, out_W.shape[1], 3, 3)
        i0y, i1y, wy = _interp_axis(3, H)
        i0x, i1x, wx = _interp_axis(3, W)
        top = g[:, :, i0y, :]
        bot = g[:, :, i1y, :]
        v00 = top[:, :, :, i0x]
        v01 = top[:, :, :, i1x]
        v10 = bot[:, :, :, i0x]
        v11 = bot[:, :, :, i1x]
        wy_ = wy[None, None, :, None]
        wx_ = wx[None, None, None, :]
        out = (1 - wy_) * ((1 - wx_) * v00 + wx_ * v01) + wy_ * ((1 - wx_) * v10 + wx_ * v11)
        return out

    def _L0_ffn_ref(x, gate_up_proj, down_proj):
        import jax, jax.numpy as jnp
        import numpy as np
        NUM_EXPERTS = 4
        B, N, H = x.shape
        E, _, two_I = gate_up_proj.shape
        I = two_I // 2
        G = N // E
        x4 = x.reshape(B, G, E, H)
        gu = jnp.einsum('bgeh,ehd->bged', x4, gate_up_proj)
        gate, up = (gu[..., :I], gu[..., I:])
        inter = jax.nn.silu(gate) * up
        out = jnp.einsum('bgei,eih->bgeh', inter, down_proj)
        return out.reshape(B, N, H)

    def _L1_conv_ref(x, pe_W, pe_b, ln_g, ln_b, in_W, conv_w, conv_b, xproj_W, dt_W, dt_b, A_log, D_param, out_W):
        import jax, jax.numpy as jnp
        import numpy as np
        B_, C_IN, H_, W_ = (16, 512, 24, 12)
        HID = 192
        INNER = 2 * HID
        N_STATE = 16
        DT_RANK = 48

        def _interp_axis(n_in, n_out):
            src = (jnp.arange(n_out, dtype=jnp.float32) + 0.5) * (n_in / n_out) - 0.5
            src = jnp.maximum(src, 0.0)
            i0 = jnp.minimum(jnp.floor(src).astype(jnp.int32), n_in - 1)
            i1 = jnp.minimum(i0 + 1, n_in - 1)
            w = src - i0.astype(jnp.float32)
            return (i0, i1, w)
        B, C, H, W = x.shape
        D_in = conv_w.shape[0]
        dt_rank = dt_W.shape[0]
        nstate = A_log.shape[1]
        p = x.reshape(B, C, 3, H // 3, 3, W // 3).mean(axis=(3, 5))
        tok = p.reshape(B, C, 9).transpose(0, 2, 1) @ pe_W + pe_b
        mu = tok.mean(-1, keepdims=True)
        var = jnp.mean((tok - mu) ** 2, axis=-1, keepdims=True)
        t = (tok - mu) / jnp.sqrt(var + 1e-05) * ln_g + ln_b
        xz = t @ in_W
        xc, z = jnp.split(xz, [D_in], axis=-1)
        xdl = xc.transpose(0, 2, 1)
        xdl = jax.lax.conv_general_dilated(xdl, conv_w, (1,), [(1, 1)], dimension_numbers=('NCH', 'OIH', 'NCH'), feature_group_count=D_in) + conv_b[None, :, None]
        u = jax.nn.silu(xdl.transpose(0, 2, 1))
        A = -jnp.exp(A_log)
        dBC = u @ xproj_W
        dlt, Bp, Cp = jnp.split(dBC, [dt_rank, dt_rank + nstate], axis=-1)
        delta = jax.nn.softplus(dlt @ dt_W + dt_b)

        def step(state, inp):
            u_l, d_l, B_l, C_l = inp
            k1 = A[None] * state + B_l[:, None, :] * u_l[:, :, None]
            state = state + d_l[:, :, None] * k1
            y_l = jnp.einsum('bdn,bn->bd', state, C_l)
            return (state, y_l)
        st0 = jnp.zeros((B, D_in, nstate), u.dtype)
        _, ys = jax.lax.scan(step, st0, (u.transpose(1, 0, 2), delta.transpose(1, 0, 2), Bp.transpose(1, 0, 2), Cp.transpose(1, 0, 2)))
        y = ys.transpose(1, 0, 2) + u * D_param
        y = y * jax.nn.silu(z)
        out_tok = y @ out_W
        g = out_tok.transpose(0, 2, 1).reshape(B, out_W.shape[1], 3, 3)
        i0y, i1y, wy = _interp_axis(3, H)
        i0x, i1x, wx = _interp_axis(3, W)
        top = g[:, :, i0y, :]
        bot = g[:, :, i1y, :]
        v00 = top[:, :, :, i0x]
        v01 = top[:, :, :, i1x]
        v10 = bot[:, :, :, i0x]
        v11 = bot[:, :, :, i1x]
        wy_ = wy[None, None, :, None]
        wx_ = wx[None, None, None, :]
        out = (1 - wy_) * ((1 - wx_) * v00 + wx_ * v01) + wy_ * ((1 - wx_) * v10 + wx_ * v11)
        return out

    def _L1_ffn_ref(hidden_states, router_gate, expert_gate_up, expert_down):
        import jax, jax.numpy as jnp
        import numpy as np
        NUM_EXPERTS = 8
        TOP_K = 2
        MODEL_DIM = 512
        INTER_DIM = 256
        GATE_SCALE = 1.0
        UP_SCALE = 0.0
        orig_shape = hidden_states.shape
        hs = hidden_states.reshape(-1, orig_shape[-1])
        T = hs.shape[0]
        logits = hs @ router_gate.T
        probs = jax.nn.softmax(logits.astype(jnp.float32), axis=-1)
        topk_scores, topk_idx = jax.lax.top_k(probs, TOP_K)
        topk_scores = topk_scores / jnp.sum(topk_scores, axis=-1, keepdims=True)
        scores_f = topk_scores.T.reshape(-1).astype(hs.dtype)
        ids_f = topk_idx.T.reshape(-1)
        order = jnp.argsort(ids_f)
        sorted_ids = ids_f[order]
        scores_sorted = scores_f[order]
        token_slots = order % T
        x = hs[token_slots]
        inter = jnp.zeros((x.shape[0], 2 * INTER_DIM), x.dtype)
        for e in range(NUM_EXPERTS):
            m = (sorted_ids == e)[:, None]
            inter = inter + jnp.where(m, x, 0) @ expert_gate_up[e]
        gate = inter[..., 0::2]
        up = inter[..., 1::2]
        h = (up + UP_SCALE) * jax.nn.silu(gate * GATE_SCALE)
        out_rows = jnp.zeros((x.shape[0], MODEL_DIM), x.dtype)
        for e in range(NUM_EXPERTS):
            m = (sorted_ids == e)[:, None]
            out_rows = out_rows + jnp.where(m, h, 0) @ expert_down[e]
        out = jnp.zeros_like(hs).at[token_slots].add(out_rows * scores_sorted[:, None])
        return out.reshape(orig_shape)

    def _gn(v, G=32, eps=1e-05):
        B_, C_, H_, W_ = v.shape
        g = v.reshape(B_, G, C_ // G, H_, W_)
        m = jnp.mean(g, axis=(2, 3, 4), keepdims=True)
        s = jnp.var(g, axis=(2, 3, 4), keepdims=True)
        return ((g - m) / jnp.sqrt(s + eps)).reshape(v.shape)

    def _ln_c(v, eps=1e-06):
        m = jnp.mean(v, axis=1, keepdims=True)
        s = jnp.var(v, axis=1, keepdims=True)
        return (v - m) / jnp.sqrt(s + eps)

    def _ln_t(v, eps=1e-05):
        m = jnp.mean(v, axis=-1, keepdims=True)
        s = jnp.var(v, axis=-1, keepdims=True)
        return (v - m) / jnp.sqrt(s + eps)

    def _to_tokens(v):
        B_, C_, H_, W_ = v.shape
        return v.reshape(B_, C_, H_ * W_).transpose(0, 2, 1)

    def _from_tokens(t, like):
        B_, C_, H_, W_ = like.shape
        return t.transpose(0, 2, 1).reshape(B_, C_, H_, W_)
    x = x + _L0_conv_ref(_ln_c(x), L0_conv_pe_W, L0_conv_pe_b, L0_conv_ln_g, L0_conv_ln_b, L0_conv_in_W, L0_conv_conv_w, L0_conv_conv_b, L0_conv_xproj_W, L0_conv_dt_W, L0_conv_dt_b, L0_conv_A_log, L0_conv_D_param, L0_conv_out_W)
    t = _to_tokens(x)
    t = t + _L0_ffn_ref(_ln_t(t), L0_ffn_gate_up_proj, L0_ffn_down_proj)
    x = _from_tokens(t, x)
    x = x + _L1_conv_ref(_ln_c(x), L1_conv_pe_W, L1_conv_pe_b, L1_conv_ln_g, L1_conv_ln_b, L1_conv_in_W, L1_conv_conv_w, L1_conv_conv_b, L1_conv_xproj_W, L1_conv_dt_W, L1_conv_dt_b, L1_conv_A_log, L1_conv_D_param, L1_conv_out_W)
    t = _to_tokens(x)
    t = t + _L1_ffn_ref(_ln_t(t), L1_ffn_router_gate, L1_ffn_expert_gate_up, L1_ffn_expert_down)
    x = _from_tokens(t, x)
    return x

_drawn_inputs = setup_inputs


def setup_inputs(seed=0):
    import zlib

    import numpy as np

    out = dict(_drawn_inputs(seed))
    spreads = {'L0_conv_pe_b': (0.0, 0.1),
     'L0_conv_ln_g': (1.0, 0.2),
     'L0_conv_ln_b': (0.0, 0.1),
     'L0_conv_conv_b': (0.0, 0.1),
     'L0_conv_dt_b': (0.0, 0.1),
     'L0_conv_D_param': (1.0, 0.6),
     'L1_conv_pe_b': (0.0, 0.1),
     'L1_conv_ln_g': (1.0, 0.2),
     'L1_conv_ln_b': (0.0, 0.1),
     'L1_conv_conv_b': (0.0, 0.1),
     'L1_conv_dt_b': (0.0, 0.1),
     'L1_conv_D_param': (1.0, 0.6)}
    factors = {'L0_ffn_gate_up_proj': 8.0,
     'L0_ffn_down_proj': 8.0,
     'L1_conv_dt_W': 4.296,
     'L1_ffn_router_gate': 8.0,
     'L1_ffn_expert_gate_up': 8.0,
     'L1_ffn_expert_down': 8.0}
    for name, (base, spread) in spreads.items():
        noise = np.random.default_rng([zlib.crc32(name.encode()), seed]).standard_normal(out[name].shape)
        drawn = base * np.exp(spread * noise) if base else spread * noise
        out[name] = jnp.asarray(drawn.astype(out[name].dtype))
    for name, factor in factors.items():
        out[name] = (out[name] * factor).astype(out[name].dtype)
    return out
```

```python
from contextlib import ExitStack

import concourse.bass as bass
import numpy as np
from concourse import mybir

P = 128
B, CH, H, W = 16, 512, 24, 12
S = H * W
T = B * S
KC = CH // P
HID, INNER, NS, RANK = 192, 384, 16, 48
HH = HID // 2
JC = INNER // P
L = 9
NT = B * L
TT = NT // 2
IB = B // 2
ROWT = S // 3
NROW = T // ROWT
XG = 8
GR = 6
NG = NROW // GR
XR = 2 * GR
TILES = T // P
E0, I0 = 4, 512
E1, I1 = 8, 256
CN = 288
NC = T // E0 // CN
EJ = TILES // E0
PIECE = 1024
PE0 = KC * (2 * I0 + CH) // PIECE
PE1 = (KC * 2 * I1 + 2 * CH) // PIECE
NP0, NP1 = E0 * PE0, E1 * PE1
MT = 2 * TILES + E1
ZT = 4
XSR = 4
GRING = 4
TB = (6, 7, 0)


def metaformer(nc, x, c_mat, c_ind, c_up, c_rout, pe_W, vec_hid, in_W, vec_inner, a_log, xproj, dt_W, out_W,
               w_ffn, router, out):
    f32, f32r, i32 = mybir.dt.float32, mybir.dt.float32r, mybir.dt.int32
    ALU, ACT, AX = mybir.AluOpType, mybir.ActivationFunctionType, mybir.AxisListType
    ds = bass.ds

    bc_dram = nc.dram_tensor("bc_dram", (2, 2 * NS, NT), f32, kind="Internal").ap()
    stat_dram = nc.dram_tensor("stat_dram", (2, E0, EJ * P), f32, kind="Internal").ap()
    xs_dram = nc.dram_tensor("xs_dram", (MT * P, CH), f32, kind="Internal").ap()
    y_dram = nc.dram_tensor("y_dram", (MT * P, CH), f32, kind="Internal").ap()

    ctx = ExitStack()
    with ctx:
        def sb(name, shape, dt=f32, life=ctx):
            return life.enter_context(nc.sbuf_tensor("sb_" + name, shape, dt))

        def sem(name):
            return ctx.enter_context(nc.semaphore(name))

        X = sb("X", [P, KC, T])
        mats = sb("mats", [P, 3, P])
        ident, ones, triu = mats[:, 0, :], mats[:, 1, :], mats[:, 2, :]
        eps = sb("eps", [P, 2])
        zero = sb("zero", [P, P])
        raw = sb("raw", [P, 2, PIECE])
        MV = sb("MV", [P, NROW, 2])
        ST6 = sb("ST6", [P, 6])
        SD = sb("SD", [P, NROW])
        RS = sb("RS", [P, NROW])
        score = sb("score", [P, 2, TILES])
        pos = sb("pos", [P, 2, TILES], i32)
        tile_expert = sb("tile_expert", [P, MT], i32)
        tile_end = sb("tile_end", [P, E1], i32)
        PS = ctx.enter_context(nc.psum_tensor("ps", [P, 8, 512], f32))

        mix = ExitStack()
        gH = sb("gH", [TT, 2, CH], f32r, mix)
        gL = sb("gL", [TT, 2, CH], f32r, mix)
        upM = sb("upM", [TT, IB, S], f32r, mix)
        MR = sb("MR", [P, 2 * TILES], f32, mix)
        statT = sb("statT", [2 * TILES, P], f32, mix)
        rw = sb("rw", [P, KC, E1], f32, mix)
        wbar = sb("wbar", [P, E1], f32, mix)
        body = ExitStack()
        mterm = sb("mterm", [P, NT], f32, body)
        pT = sb("pT", [P, KC, NT], f32, body)
        peW = sb("peW", [P, KC, HID], f32, body)
        vhid = sb("vhid", [TT, 3, HID], f32, body)
        inW = sb("inW", [HH, 2, 2 * INNER], f32, body)
        vinn = sb("vinn", [P, JC, 6], f32, body)
        alog = sb("alog", [P, JC, NS], f32, body)
        xpW = sb("xpW", [P, JC, RANK + 2 * NS], f32, body)
        dtW = sb("dtW", [RANK, INNER], f32, body)
        outW = sb("outW", [P, JC, CH], f32, body)
        tk = sb("tk", [TT, 2, HID], f32, body)
        mvh = sb("mvh", [TT, 2, 2], f32, body)
        sth = sb("sth", [TT, 2, 6], f32, body)
        sdh = sb("sdh", [TT, 2], f32, body)
        rsh = sb("rsh", [TT, 2], f32, body)
        tT = sb("tT", [HH, 2, NT], f32, body)
        acc = sb("acc", [P, JC, NT], f32, body)
        uu = sb("uu", [P, JC, NT], f32, body)
        sz = sb("sz", [P, JC, NT], f32, body)
        bc = sb("bc", [2 * NS, NT], f32, body)
        dl = sb("dl", [RANK, NT], f32, body)
        dx = sb("dx", [P, JC, NT], f32, body)
        ab = sb("ab", [P, JC, NT], f32, body)
        delta = sb("delta", [P, JC, NT], f32, body)
        du = sb("du", [P, JC, NT], f32, body)
        negA = sb("negA", [P, JC, NS], f32, body)
        yy = sb("yy", [P, JC, NT], f32, body)
        patch = ExitStack()
        xtok = sb("xtok", [ROWT, XR, CH], f32, patch)
        ind = sb("ind", [ROWT, 3], f32, patch)
        RI = sb("RI", [ROWT, NROW, 3], f32, patch)
        RM = sb("RM", [ROWT, NROW, 3], f32, patch)
        upS = sb("upS", [TT, IB, S], f32, patch)
        patch.close()
        da = sb("da", [P, NS, NT], f32, body)
        db = sb("db", [P, NS, NT], f32, body)
        hs = sb("hs", [P, NS, NT], f32, body)
        Bb = sb("Bb", [P, 2 * NS, NT], f32, body)
        a1 = sb("a1", [P, NS, NT], f32, body)
        body.close()
        moe_in = ExitStack()
        XN = sb("XN", [P, TILES, CH], f32, moe_in)
        R = {n: sb("R_" + n, [P, TILES, E1], f32, moe_in)
             for n in ("log", "e", "p", "oh1", "oh2", "t", "O", "pe")}
        q36 = {n: sb("q_" + n, [P, TILES], f32, moe_in) for n in ("mx", "sm", "rs", "m1", "m2", "k", "den", "pf")}
        rout = sb("rout", [P, E1 + TILES + MT + E1 * TILES], f32, moe_in)
        scT = {n: sb("s_" + n, [P, E1, TILES], f32, moe_in) for n in ("tot", "inc", "exc", "cmp")}
        e8 = {n: sb("e_" + n, [P, E1], f32, moe_in) for n in ("nt", "end", "base")}
        tcmp = sb("tcmp", [P, MT, E1 - 1], f32, moe_in)
        texp = sb("texp", [P, MT], f32, moe_in)
        nmr = sb("nmr", [P, TILES], f32, moe_in)
        moe_in.close()
        mix.close()
        ffn0 = ExitStack()
        w0H = sb("w0H", [P, 2, PE0 * PIECE], f32r, ffn0)
        w0L = sb("w0L", [P, 2, PE0 * PIECE], f32r, ffn0)
        xnH = sb("xnH", [P, KC, CN], f32r, ffn0)
        xnL = sb("xnL", [P, KC, CN], f32r, ffn0)
        itH = sb("itH", [P, KC, CN], f32r, ffn0)
        itL = sb("itL", [P, KC, CN], f32r, ffn0)
        rmb = sb("rmb", [P, 2, CN], f32, ffn0)
        xr = sb("xr", [P, KC, CN], f32, ffn0)
        sg = sb("sg", [P, 2, CN], f32, ffn0)
        ffn0.close()
        ffn1 = ExitStack()
        w1H = sb("w1H", [P, 2, PE1 * 2, 512], f32r, ffn1)
        w1L = sb("w1L", [P, 2, PE1 * 2, 512], f32r, ffn1)
        xs = sb("xs", [P, XSR, CH], f32, ffn1)
        xtH = sb("xtH", [P, 2, KC, P], f32r, ffn1)
        xtL = sb("xtL", [P, 2, KC, P], f32r, ffn1)
        sgt = sb("sgt", [P, 2, I1], f32, ffn1)
        hh = sb("hh", [P, 2, I1], f32, ffn1)
        htH = sb("htH", [P, 2, 2, P], f32r, ffn1)
        htL = sb("htL", [P, 2, 2, P], f32r, ffn1)
        ysb = sb("ysb", [P, 2, CH], f32, ffn1)
        g1 = sb("g1", [P, GRING, CH], f32, ffn1)
        g2 = sb("g2", [P, GRING, CH], f32, ffn1)
        gs = sb("gs", [P, 2, CH], f32, ffn1)
        gt = sb("gt", [P, 2, CH], f32, ffn1)
        ffn1.close()

        Xe = X[:, :, :].rearrange("p k (t e) -> p k e t", e=E0)
        w8 = rout[:, 0:E1]
        j128 = rout[:, E1:E1 + TILES]
        iMT = rout[:, E1 + TILES:E1 + TILES + MT]
        jmask = rout[:, E1 + TILES + MT:]
        one8 = ones[:, 0:E1]

        consts, filled = sem("consts"), sem("filled")
        x_loaded = [sem(f"x_loaded_{g}") for g in range(XG)]
        mixw, upm = sem("mix_weights"), sem("up_matrix")
        tp_ready, xtok_ready = sem("tp_ready"), sem("xtok_ready")
        st_done, mv_done, sd_ready = sem("st_done"), sem("mv_done"), sem("sd_ready")
        ri_ready, pooled = sem("ri_ready"), sem("pooled")
        mterm_ready, p_ready, tok_ready = sem("mterm_ready"), sem("p_ready"), sem("tok_ready")
        var_h, sd_h, tk_ready, tkT = sem("var_h"), sem("sd_h"), sem("tk_ready"), sem("tkT")
        tT_ready, xz_ready, acc_ready = sem("tT_ready"), sem("xz_ready"), sem("acc_ready")
        u_ready, z_ready, dbc_ready = sem("u_ready"), sem("z_ready"), sem("dbc_ready")
        bc_ready, bc_out, bc_in, dl_ready = sem("bc_ready"), sem("bc_out"), sem("bc_in"), sem("dl_ready")
        dt_ready, ab_ready, ex_done, sp_ready = sem("dt_ready"), sem("ab_ready"), sem("ex_done"), sem("sp_ready")
        ea_ready, na_ready, du_ready = sem("ea_ready"), sem("na_ready"), sem("du_ready")
        da_ready, db_ready, a1_ready = sem("da_ready"), sem("db_ready"), sem("a1_ready")
        a1_zero, scanned = sem("a1_zero"), sem("scanned")
        y_ready, og_ready, gh_ready, g_ready = sem("y_ready"), sem("og_ready"), sem("gh_ready"), sem("g_ready")
        up_ready, up_added = sem("up_ready"), sem("up_added")
        lt_ready, lt_free, lst_done, lmv_done = sem("lt_ready"), sem("lt_free"), sem("lst_done"), sem("lmv_done")
        lsd_ready, mr_ready = sem("lsd_ready"), sem("mr_ready")
        mrT, statT_ready, stats_out = sem("mrT"), sem("statT_ready"), sem("stats_out")
        dve = sem("dve_step")
        raw_loaded, split_step = [sem(f"raw_loaded_{r}") for r in range(2)], sem("split_step")
        w0_ready = sem("w0_ready")
        rm_loaded, rm_free, xr_done = sem("rm_loaded"), sem("rm_free"), sem("xr_done")
        xn_ready = sem("xn_ready")
        gu_ready, gu_free, sg_ready, sg_free = sem("gu_ready"), sem("gu_free"), sem("sg_ready"), sem("sg_free")
        it_step, it_ready = sem("it_step"), sem("it_ready")
        dn_ready, dn_free = sem("dn_ready"), sem("dn_free")
        wb_ready, wb_sb, rw_ready = sem("wb_ready"), sem("wb_sb"), sem("rw_ready")
        logit_ready, r_e, r_O, r_pre, r_tot = (sem("logit_ready"), sem("router_exp"), sem("router_onehot"),
                                               sem("router_prefix"), sem("router_totals"))
        routed, rexp_in, xnorm, nmr_ready = sem("routed"), sem("rexp_in"), sem("xnorm"), sem("nmr_ready")
        scattered = sem("scattered")
        w1_ready, slot_free = sem("w1_ready"), sem("slot_free")
        xs_loaded = [sem(f"xs_loaded_{r}") for r in range(XSR)]
        t_ready, xt_hi, xt_ready = sem("t_ready"), sem("xt_hi"), sem("xt_ready")
        g_up, sgt_ready, h_ready = sem("g_up"), sem("sgt_ready"), sem("h_ready")
        th_ready, ht_hi, ht_ready = sem("th_ready"), sem("ht_hi"), sem("ht_ready")
        d_ready, y_out, y_stored = sem("d_ready"), sem("y_out"), [sem("y_stored_0"), sem("y_stored_1")]
        g_loaded = [sem(f"g_loaded_{r}") for r in range(GRING)]
        gs_ready, gt_ready = sem("gs_ready"), sem("gt_ready")
        f_ready, f_added, stored = sem("f_ready"), sem("f_added"), sem("stored")

        def behind(engine, signal, i):
            if not isinstance(i, int) or i >= 2:
                engine.wait_ge(signal, i - 1)

        def images_before(tokens):
            return -(-tokens // S)

        block = ctx.enter_context(nc.Block())

        @block.sync
        def _(sp):
            sp.dma_start(mats[:, :, :], c_mat).then_inc(consts, 16)

            def load_mix_weights(l):
                for dst, src in ((ind[:, :], c_ind), (peW[:, :, :], pe_W[l]), (inW[:, :, :], in_W[l]),
                                 (vinn[:, :, :], vec_inner[l]), (alog[:, :, :], a_log[l]),
                                 (xpW[:, :, :], xproj[l]), (dtW[:, :], dt_W[l]), (outW[:, :, :], out_W[l])):
                    sp.dma_start(dst, src).then_inc(mixw, 16)
                sp.dma_start(vhid[:, :, :], vec_hid[l:l + 1].broadcast_to((TT, 3, HID))).then_inc(mixw, 16)
                sp.dma_start(upS[:, :, :], c_up).then_inc(mixw, 16)

            def exchange(l):
                sp.wait_ge(bc_ready, l + 1)
                sp.dma_start(bc_dram[l], bc[:, :]).then_inc(bc_out, 16)
                sp.wait_ge(bc_out, l * 16 + 16)
                sp.wait_ge(p_ready, l * 2 + 2)
                sp.dma_start(Bb[:, :, :], bc_dram[l:l + 1].broadcast_to((P, 2 * NS, NT))).then_inc(bc_in, 16)

            for b in range(B):
                if b == 2:
                    load_mix_weights(0)
                sp.dma_start(X[:, :, b * S:(b + 1) * S], x[b].rearrange("(k p) s -> p k s", p=P))\
                    .then_inc(x_loaded[b // (B // XG)], 16)
            sp.wait_ge(dve, 2)
            exchange(0)
            zrow = xs_dram.rearrange("(m p z) c -> m p (z c)", z=ZT, p=P)
            with sp.Fori(0, MT // ZT) as m:
                sp.dma_start(zrow[ds(m, 1)].rearrange("m p (a c) -> p (m a) c", c=P),
                             zero[:, :].unsqueeze(1).broadcast_to((P, ZT * CH // P, P))).then_inc(filled, 16)
            sp.wait_ge(statT_ready, 1)
            sp.dma_start(stat_dram.rearrange("a e (j t) -> (a e j) t", t=P), statT[:, :]).then_inc(stats_out, 16)
            sp.wait_ge(stats_out, 16)
            with sp.Fori(0, E0) as e:
                for c in range(NC):
                    sp.wait_ge(rm_free, e * NC + c + 1)
                    sp.dma_start(rmb[:, :, :],
                                 stat_dram[:, ds(e, 1), c * CN:(c + 1) * CN].rearrange("a e n -> e a n")
                                 .broadcast_to((P, 2, CN))).then_inc(rm_loaded, 16)
            sp.wait_ge(dn_free, E0 * NC + 1)
            load_mix_weights(1)
            sp.dma_start(rw[:, :, :], router).then_inc(upm, 16)
            exchange(1)
            sp.wait_ge(up_added, 2 * B + 2 * B)
            sp.wait_ge(g_ready, 2 + 2)
            sp.dma_start(rout[:, :], c_rout).then_inc(upm, 16)
            sp.wait_ge(scattered, 16 * 2 * TILES)
            xs_t = xs_dram.rearrange("(m p) c -> m p c", p=P)
            y_t = y_dram.rearrange("(m p) c -> m p c", p=P)

            def load(i, r):
                if not isinstance(i, int):
                    sp.wait_ge(t_ready, i - (XSR - 1))
                sp.dma_start(xs[:, r:r + 1, :], xs_t[i:i + 1].rearrange("m p c -> p m c") if isinstance(i, int)
                             else xs_t[ds(i, 1)].rearrange("m p c -> p m c")).then_inc(xs_loaded[r], 16)

            def store(i, r):
                sp.wait_ge(y_out, i + 1)
                sp.dma_start(y_t[ds(i, 1)].rearrange("m p c -> p m c"), ysb[:, r:r + 1, :]).then_inc(y_stored[r], 16)

            for i in range(XSR):
                load(i, i)
            with sp.Fori(0, MT // XSR - 1) as g:
                for r in range(XSR):
                    load(g * XSR + (r + XSR), r)
                    store(g * XSR + r, r % 2)
            for r in range(XSR):
                store(MT - XSR + r, r % 2)
            for b in range(B):
                sp.wait_ge(f_added, -(-S * (b + 1) // P))
                sp.dma_start(out[b].rearrange("(k p) s -> p k s", p=P), X[:, :, b * S:(b + 1) * S])\
                    .then_inc(stored, 16)
            sp.wait_ge(stored, 16 * B)

        @block.gpsimd
        def _(pool):
            steps = [0]

            def split(p, dst_h, dst_l):
                r = p % 2
                pool.wait_ge(raw_loaded[r], 16 * (p // 2 + 1))
                pool.tensor_copy(dst_h, raw[:, r, :]).then_inc(split_step, 1)
                pool.wait_ge(split_step, 2 * p + 1)
                pool.tensor_tensor(dst_l, raw[:, r, :], dst_h.bitcast(f32), ALU.subtract).then_inc(split_step, 1)
                pool.wait_ge(split_step, 2 * p + 2)
                if p + 2 < NP0 + NP1:
                    pool.dma_start(raw[:, r, :], w_ffn[p + 2]).then_inc(raw_loaded[r], 16)

            def scan_inputs(l):
                pool.wait_ge(na_ready, l + 1)
                pool.wait_ge(sp_ready, l + 1)
                for j in range(JC):
                    if j:
                        pool.wait_ge(a1_ready, l * JC + j)
                    pool.tensor_tensor(da[:, :, :], delta[:, j:j + 1, :].broadcast_to((P, NS, NT)),
                                       negA[:, j, :].unsqueeze(2).broadcast_to((P, NS, NT)), ALU.mult)\
                        .then_inc(da_ready, 1)
                    if not j:
                        pool.wait_ge(du_ready, l + 1)
                        pool.wait_ge(bc_in, l * 16 + 16)
                    else:
                        pool.wait_ge(scanned, l * JC + j)
                    pool.tensor_tensor(db[:, :, :], du[:, j:j + 1, :].broadcast_to((P, NS, NT)),
                                       Bb[:, 0:NS, :], ALU.mult).then_inc(db_ready, 1)

            pool.dma_start(raw[:, 0, :], w_ffn[0]).then_inc(raw_loaded[0], 16)
            pool.dma_start(raw[:, 1, :], w_ffn[1]).then_inc(raw_loaded[1], 16)
            scan_inputs(0)
            pool.wait_ge(stats_out, 16)
            pool.wait_ge(up_added, 2 * B)
            pool.wait_ge(lmv_done, TILES)
            for e in range(E0):
                if e >= 2:
                    pool.wait_ge(dn_ready, (e - 1) * NC)
                for q in range(PE0):
                    p = e * PE0 + q
                    split(p, w0H[:, e % 2, q * PIECE:(q + 1) * PIECE], w0L[:, e % 2, q * PIECE:(q + 1) * PIECE])
                pool.sem_inc(w0_ready, 1)
            scan_inputs(1)
            pool.wait_ge(routed, 2)
            pool.wait_ge(filled, 16 * (MT // ZT))
            for t in range(TILES):
                pool.wait_ge(xnorm, t + 1)
                for k in range(2):
                    pool.indirect_dma_start(
                        xs_dram, bass.IndirectOffsetOnAxis(ap=pos[:, k, t:t + 1], axis=0), XN[:, t, :], None)\
                        .then_inc(scattered, 16)
            pool.wait_ge(scattered, 16 * 2 * TILES)
            for e in range(E1):
                if e >= 2:
                    end = pool.value_load(tile_end[0:1, e - 2:e - 1], min_val=1, max_val=MT)
                    pool.wait_ge(d_ready, end)
                    pool.sem_inc(slot_free, 1)
                for q in range(PE1):
                    p = NP0 + e * PE1 + q
                    split(p, w1H[:, e % 2, 2 * q:2 * q + 2, :].rearrange("p a n -> p (a n)"),
                          w1L[:, e % 2, 2 * q:2 * q + 2, :].rearrange("p a n -> p (a n)"))
                pool.sem_inc(w1_ready, 1)
            for r in range(2):
                pool.wait_ge(y_stored[r], 16 * (MT // 2))
            for t in range(TILES):
                if t >= GRING:
                    pool.wait_ge(gt_ready, t - GRING + 1)
                for k, g in enumerate((g1, g2)):
                    pool.indirect_dma_start(
                        g[:, t % GRING, :], None, y_dram, bass.IndirectOffsetOnAxis(ap=pos[:, k, t:t + 1], axis=0))\
                        .then_inc(g_loaded[t % GRING], 16)

        @block.tensor
        def _(pe):
            def pool_patches(l, g):
                pe.wait_ge(ri_ready, l * 2 * NG + 2 * (g + 1))
                for t in range(g * GR, (g + 1) * GR):
                    for k in range(KC):
                        pe.matmul(PS[:, 4 + k // 2, (k % 2) * NT + 3 * t:(k % 2) * NT + 3 * t + 3],
                                  xtok[:, t % XR, k * P:(k + 1) * P], RI[:, t, :], start=True, stop=True)
                pe.matmul(PS[:, 3, 3 * g * GR:3 * (g + 1) * GR], ones[0:ROWT, :],
                          RM[:, g * GR:(g + 1) * GR, :].rearrange("p t a -> p (t a)"), start=True, stop=True)\
                    .then_inc(pooled, 1)

            def patches(l):
                for g in range(NG):
                    for t in range(g * GR, (g + 1) * GR):
                        if l == 0:
                            if t % (NROW // XG) == 0:
                                pe.wait_ge(x_loaded[t // (NROW // XG)], 16 * (B // XG))
                        elif t == 0:
                            pe.wait_ge(dn_free, E0 * NC + 1)
                        if t >= 3:
                            pe.wait_ge(xtok_ready, l * NROW + t - 2)
                        for k in range(KC):
                            last = pe.transpose(PS[0:ROWT, t % 3, k * P:(k + 1) * P],
                                                X[:, k, t * ROWT:(t + 1) * ROWT], ident)
                        last.then_inc(tp_ready, 1)
                    if g:
                        pool_patches(l, g - 1)
                pool_patches(l, NG - 1)

            def mixer(l):
                pe.wait_ge(mixw, l * 160 + 160)
                pe.wait_ge(p_ready, l * 2 + 2)
                for tt in range(2):
                    for k in range(KC):
                        last = pe.matmul(PS[0:TT, tt, 0:HID], pT[:, k, tt * TT:(tt + 1) * TT], peW[:, k, :],
                                         start=k == 0, stop=k == KC - 1)
                last.then_inc(tok_ready, 1)
                pe.wait_ge(tk_ready, l + 1)
                for tt in range(2):
                    for h in range(2):
                        last = pe.transpose(PS[0:HH, 2, h * NT + tt * TT:h * NT + (tt + 1) * TT],
                                            tk[:, tt, h * HH:(h + 1) * HH], ident[0:TT, 0:TT])
                last.then_inc(tkT, 1)
                pe.wait_ge(tT_ready, l + 1)
                pe.wait_ge(mterm_ready, l + 1)
                pe.wait_ge(p_ready, l * 2 + 2)
                for m in range(2 * JC):
                    for h in range(2):
                        last = pe.matmul(PS[:, 3 + m // JC, (m % JC) * NT:(m % JC + 1) * NT],
                                         inW[:, h, m * P:(m + 1) * P], tT[:, h, :], start=h == 0, stop=h == 1)
                    if m % JC == JC - 1:
                        last.then_inc(xz_ready, 1)
                pe.wait_ge(u_ready, l + 1)
                for j in range(JC):
                    last = pe.matmul(PS[0:2 * NS, 5, 0:NT], xpW[:, j, RANK:], uu[:, j, :],
                                     start=j == 0, stop=j == JC - 1)
                last.then_inc(dbc_ready, 1)
                for j in range(JC):
                    last = pe.matmul(PS[0:RANK, 6, 0:NT], xpW[:, j, 0:RANK], uu[:, j, :],
                                     start=j == 0, stop=j == JC - 1)
                last.then_inc(dbc_ready, 1)
                pe.wait_ge(dl_ready, l + 1)
                for j in range(JC):
                    last = pe.matmul(PS[:, 7, j * NT:(j + 1) * NT], dtW[:, j * P:(j + 1) * P], dl[:, :],
                                     start=True, stop=True)
                last.then_inc(dt_ready, 1)
                pe.wait_ge(y_ready, l + 1)
                for tt in range(2):
                    for j in range(JC):
                        last = pe.matmul(PS[0:TT, tt, :], yy[:, j, tt * TT:(tt + 1) * TT], outW[:, j, :],
                                         start=j == 0, stop=j == JC - 1)
                last.then_inc(og_ready, 1)

            def upsample(l, b):
                for half in range(2):
                    if b:
                        pe.wait_ge(up_added, l * 2 * B + 2 * (b - 1) + half + 1)
                    for k in (2 * half, 2 * half + 1):
                        for g, first in ((gH, True), (gL, False)):
                            last = pe.matmul(PS[:, 2 + k, 0:S], g[:, b // IB, k * P:(k + 1) * P],
                                             upM[:, b % IB, :], start=first, stop=not first)
                    last.then_inc(up_ready, 1)

            def tile_transposes(l, q, view):
                if q >= len(TB):
                    pe.wait_ge(lt_free, l * TILES + q - len(TB) + 1)
                for k in range(KC):
                    last = pe.transpose(PS[:, TB[q % len(TB)], k * P:(k + 1) * P], view(k), ident)
                last.then_inc(lt_ready, 1)

            pe.wait_ge(consts, 16)
            patches(0)
            mixer(0)
            pe.wait_ge(g_ready, 2)
            q = 0
            for b in range(B):
                upsample(0, b)
                while q < TILES and images_before(E0 * P * (q // E0 + 1)) <= b:
                    pe.wait_ge(up_added, 2 * images_before(E0 * P * (q // E0 + 1)))
                    tile_transposes(0, q, lambda k: Xe[:, k, q % E0, (q // E0) * P:(q // E0 + 1) * P])
                    q += 1
            while q < TILES:
                pe.wait_ge(up_added, 2 * images_before(E0 * P * (q // E0 + 1)))
                tile_transposes(0, q, lambda k: Xe[:, k, q % E0, (q // E0) * P:(q // E0 + 1) * P])
                q += 1
            pe.wait_ge(mr_ready, 2)
            pe.transpose(PS[0:2 * TILES, 2, 0:P], MR[:, :], ident).then_inc(mrT, 1)

            def three(out_ap, wl, wh, xl, xh, start, stop):
                pe.matmul(out_ap, wh, xh, start=start, stop=False)
                pe.matmul(out_ap, wl, xh, start=False, stop=False)
                return pe.matmul(out_ap, wh, xl, start=False, stop=stop)

            pe.wait_ge(statT_ready, 1)
            with pe.Fori(0, E0 // 2) as ee:
                for s in range(2):
                    with pe.Fori(0, NC) as c:
                        n = ee * (2 * NC) + c + s * NC
                        pe.wait_ge(w0_ready, ee * 2 + s + 1)
                        pe.wait_ge(xn_ready, n + 1)
                        for m in range(KC):
                            pe.wait_ge(gu_free, n * KC + m + 1)
                            for u in range(2):
                                for k in range(KC):
                                    o = k * 2 * I0 + u * I0 + m * P
                                    last = three(PS[:, 2 * (m % 2) + u, 0:CN], w0L[:, s, o:o + P],
                                                 w0H[:, s, o:o + P], xnL[:, k, :], xnH[:, k, :],
                                                 k == 0, k == KC - 1)
                            last.then_inc(gu_ready, 1)
                        pe.wait_ge(dn_free, n + 1)
                        for k in range(KC):
                            pe.wait_ge(it_ready, n * KC + k + 1)
                            for h in range(KC):
                                o = KC * 2 * I0 + k * CH + h * P
                                last = three(PS[:, 4 + h, 0:CN], w0L[:, s, o:o + P], w0H[:, s, o:o + P],
                                             itL[:, k, :], itH[:, k, :], k == 0, k == KC - 1)
                        last.then_inc(dn_ready, 1)

            patches(1)
            mixer(1)
            pe.wait_ge(upm, 16)
            pe.wait_ge(gh_ready, 1 + 1)
            pe.wait_ge(g_ready, 2 + 2)
            for k in range(KC):
                last = pe.matmul(PS[:, 1, 0:E1], ones, rw[:, k, :], start=k == 0, stop=k == KC - 1)
            last.then_inc(wb_ready, 1)
            pe.wait_ge(rw_ready, 1)
            pe.wait_ge(g_ready, 2 + 2)

            def router_tile(t):
                pe.wait_ge(up_added, 2 * B + 2 * images_before(P * (t + 1)))
                tile_transposes(1, t, lambda k: X[:, k, t * P:(t + 1) * P])
                for k in range(KC):
                    last = pe.matmul(PS[:, 1, t * E1:(t + 1) * E1], X[:, k, t * P:(t + 1) * P], rw[:, k, :],
                                     start=k == 0, stop=k == KC - 1)
                return last

            t = 0
            for b in range(B):
                upsample(1, b)
                while t < TILES and images_before(P * (t + 1)) <= b:
                    router_tile(t)
                    t += 1
            while t < TILES:
                last = router_tile(t)
                t += 1
            last.then_inc(logit_ready, 1)
            pe.wait_ge(r_O, 1)
            O = R["O"][:, :, :].rearrange("p t e -> p (t e)")
            pe.matmul(PS[:, 2, 0:TILES * E1], triu, O, start=True, stop=True).then_inc(r_pre, 1)
            pe.matmul(PS[:, 3, 0:TILES * E1], ones, O, start=True, stop=True).then_inc(r_pre, 1)
            pe.wait_ge(routed, 2)

            def transposes(i, turn, r, s):
                pe.wait_ge(xs_loaded[r], 16 * turn + 16)
                behind(pe, xt_ready, i)
                for k in range(KC):
                    last = pe.transpose(PS[:, s, k * P:(k + 1) * P], xs[:, r, k * P:(k + 1) * P], ident)
                last.then_inc(t_ready, 1)

            def slot_of(i):
                e = pe.value_load(tile_expert[0:1, i:i + 1] if isinstance(i, int) else tile_expert[0:1, ds(i, 1)],
                                  min_val=0, max_val=E1 - 1)
                return e, e % 2

            def gate_up(i, s, slot, ks):
                for k in ks:
                    wh = w1H[:, ds(slot, 1), k, :]
                    wl = w1L[:, ds(slot, 1), k, :]
                    pe.matmul(PS[:, 2 + s, :], xtH[:, s, k, :], wh, start=k == 0, stop=False)
                    pe.matmul(PS[:, 2 + s, :], xtL[:, s, k, :], wh, start=False, stop=False)
                    last = pe.matmul(PS[:, 2 + s, :], xtH[:, s, k, :], wl, start=False, stop=k == KC - 1)
                return last

            def hidden_transposes(i, s):
                pe.wait_ge(h_ready, i + 1)
                behind(pe, ht_ready, i)
                for k in range(2):
                    last = pe.transpose(PS[:, 4 + s, k * P:(k + 1) * P], hh[:, s, k * P:(k + 1) * P], ident)
                last.then_inc(th_ready, 1)

            def down(i, s, slot):
                pe.wait_ge(ht_ready, i + 1)
                behind(pe, y_out, i)
                for k in range(2):
                    wh = w1H[:, ds(slot, 1), KC + k, :]
                    wl = w1L[:, ds(slot, 1), KC + k, :]
                    pe.matmul(PS[:, 6 + s, :], htH[:, s, k, :], wh, start=k == 0, stop=False)
                    pe.matmul(PS[:, 6 + s, :], htL[:, s, k, :], wh, start=False, stop=False)
                    last = pe.matmul(PS[:, 6 + s, :], htH[:, s, k, :], wl, start=False, stop=k == 1)
                last.then_inc(d_ready, 1)

            def step(i, s, r_next, turn_next, first=False, last=False):
                if not last:
                    transposes(i + 1, turn_next, r_next, 1 - s)
                e, slot = slot_of(i)
                pe.wait_ge(w1_ready, e + 1)
                pe.wait_ge(xt_ready, i + 1)
                behind(pe, h_ready, i)
                gate_up(i, s, slot, (0, 1))
                if not first:
                    hidden_transposes(i - 1, 1 - s)
                gate_up(i, s, slot, (2, 3)).then_inc(g_up, 1)
                if not first:
                    _, before = slot_of(i - 1)
                    down(i - 1, 1 - s, before)

            transposes(0, 0, 0, 0)
            step(0, 0, 1, 0, first=True)
            for i in (1, 2, 3):
                step(i, i % 2, (i + 1) % XSR, (i + 1) // XSR)
            with pe.Fori(1, MT // XSR - 1) as g:
                for r in range(XSR):
                    step(g * XSR + r, r % 2, (r + 1) % XSR, g + (r + 1) // XSR)
            for i in range(MT - XSR, MT):
                step(i, i % 2, (i + 1) % XSR, (i + 1) // XSR, last=i == MT - 1)
            hidden_transposes(MT - 1, 1)
            down(MT - 1, 1, slot_of(MT - 1)[1])

            for t in range(TILES):
                pe.wait_ge(gt_ready, t + 1)
                if t >= 4:
                    pe.wait_ge(f_added, t - 3)
                for k in range(KC):
                    last = pe.transpose(PS[:, t % 4, k * P:(k + 1) * P], gt[:, t % 2, k * P:(k + 1) * P], ident)
                last.then_inc(f_ready, 1)

        @block.scalar
        def _(act):
            def patches(l):
                for g in range(NG):
                    for t in range(g * GR, (g + 1) * GR):
                        act.wait_ge(tp_ready, l * NROW + t + 1)
                        if t >= XR and t % GR == 0:
                            act.wait_ge(pooled, l * NG + g - 1)
                        act.activation(xtok[:, t % XR, :], PS[0:ROWT, t % 3, :], ACT.Copy).then_inc(xtok_ready, 1)
                    act.wait_ge(mv_done, l * NROW + GR * (g + 1))
                    act.activation(SD[0:ROWT, g * GR:(g + 1) * GR], MV[0:ROWT, g * GR:(g + 1) * GR, 1], ACT.Sqrt,
                                   bias=eps[0:ROWT, 0:1]).then_inc(sd_ready, 1)
                act.wait_ge(pooled, l * NG + NG)
                act.activation(mterm[:, :], PS[:, 3, 0:NT], ACT.Copy).then_inc(mterm_ready, 1)

            def mixer(l):
                act.wait_ge(var_h, l * 2 + 2)
                act.activation(sdh[:, :], mvh[:, :, 1], ACT.Sqrt, bias=eps[0:TT, 1:2]).then_inc(sd_h, 1)
                act.wait_ge(tkT, l + 1)
                act.activation(tT[:, :, :], PS[0:HH, 2, 0:2 * NT].rearrange("p (h t) -> p h t", h=2), ACT.Copy)\
                    .then_inc(tT_ready, 1)
                act.wait_ge(acc_ready, l + 1)
                act.activation(uu[:, :, :], acc[:, :, :], ACT.Silu).then_inc(u_ready, 1)
                act.wait_ge(xz_ready, l * 2 + 2)
                act.activation(sz[:, :, :], PS[:, 4, 0:JC * NT].rearrange("p (j t) -> p j t", j=JC), ACT.Silu)\
                    .then_inc(z_ready, 1)
                act.wait_ge(mixw, l * 160 + 160)
                act.activation(negA[:, :, :], alog[:, :, :], ACT.Exp).then_inc(ea_ready, 1)
                act.wait_ge(ab_ready, l + 1)
                act.activation(ab[:, :, :], ab[:, :, :], ACT.Exp, scale=-1.0).then_inc(ex_done, 1)
                act.wait_ge(ex_done, l * 2 + 1)
                act.activation(ab[:, :, :], ab[:, :, :], ACT.Ln, bias=1.0).then_inc(ex_done, 1)
                for j in range(JC):
                    act.wait_ge(da_ready, l * JC + j + 1)
                    if j:
                        act.wait_ge(scanned, l * JC + j)
                    else:
                        act.wait_ge(a1_zero, l + 1)
                    act.activation(a1[:, :, :].rearrange("p n (b t) -> p (n b) t", t=L)[:, :, 1:],
                                   da[:, :, :].rearrange("p n (b t) -> p (n b) t", t=L)[:, :, 1:],
                                   ACT.Identity, bias=1.0).then_inc(a1_ready, 1)
                act.wait_ge(og_ready, l + 1)
                act.activation(gH[:, :, :], PS[0:TT, 0:2, :], ACT.Copy).then_inc(gh_ready, 1)

            patches(0)
            mixer(0)
            act.wait_ge(lmv_done, TILES)
            act.activation(SD[:, 0:TILES], MV[:, 0:TILES, 1], ACT.Sqrt, bias=eps[:, 1:2]).then_inc(lsd_ready, 1)
            act.wait_ge(mrT, 1)
            act.activation(statT[:, :], PS[0:2 * TILES, 2, 0:P], ACT.Copy).then_inc(statT_ready, 1)
            act.wait_ge(statT_ready, 1)
            act.wait_ge(stats_out, 16)

            with act.Fori(0, E0 * NC) as n:
                for m in range(KC):
                    act.wait_ge(gu_ready, n * KC + m + 1)
                    act.wait_ge(sg_free, n * KC + m + 1)
                    act.activation(sg[:, m % 2, :], PS[:, 2 * (m % 2), 0:CN], ACT.Silu).then_inc(sg_ready, 1)

            patches(1)
            mixer(1)
            act.wait_ge(wb_ready, 1)
            act.activation(wbar[:, :], PS[:, 1, 0:E1], ACT.Copy, scale=1.0 / CH).then_inc(wb_sb, 1)
            act.wait_ge(g_ready, 2 + 2)
            for t in range(TILES):
                act.wait_ge(lt_ready, TILES + t + 1)
                act.activation(XN[:, t, :], PS[:, TB[t % len(TB)], :], ACT.Copy).then_inc(lt_free, 1)
            act.wait_ge(lmv_done, TILES + TILES)
            act.activation(SD[:, 0:TILES], MV[:, 0:TILES, 1], ACT.Sqrt, bias=eps[:, 1:2]).then_inc(lsd_ready, 1)
            act.wait_ge(rexp_in, 1)
            act.activation(R["e"][:, :, :], R["t"][:, :, :], ACT.Exp).then_inc(r_e, 1)
            act.wait_ge(r_pre, 2)
            act.activation(scT["tot"][:, :, :], PS[:, 3, 0:TILES * E1].rearrange("p (t e) -> p e t", e=E1), ACT.Copy)\
                .then_inc(r_tot, 1)
            act.wait_ge(nmr_ready, 1)
            for t in range(TILES):
                act.activation(XN[:, t, :], XN[:, t, :], ACT.Identity, scale=RS[:, t:t + 1], bias=nmr[:, t:t + 1])\
                    .then_inc(xnorm, 1)

            def x_hi(i, s):
                act.wait_ge(t_ready, i + 1)
                behind(act, g_up, i)
                act.activation(xtH[:, s, :, :], PS[:, s, :].rearrange("p (k n) -> p k n", n=P), ACT.Copy)\
                    .then_inc(xt_hi, 1)

            def silu(i, s):
                act.wait_ge(g_up, i + 1)
                behind(act, h_ready, i)
                act.activation(sgt[:, s, :], PS[:, 2 + s, 0:512:2], ACT.Silu).then_inc(sgt_ready, 1)

            def h_hi(i, s):
                act.wait_ge(th_ready, i + 1)
                behind(act, d_ready, i)
                act.activation(htH[:, s, :, :], PS[:, 4 + s, 0:2 * P].rearrange("p (k n) -> p k n", n=P), ACT.Copy)\
                    .then_inc(ht_hi, 1)

            def y_copy(i, s, turn):
                act.wait_ge(d_ready, i + 1)
                if turn is not None:
                    act.wait_ge(y_stored[s], turn * 16)
                act.activation(ysb[:, s, :], PS[:, 6 + s, :], ACT.Copy).then_inc(y_out, 1)

            def step(i, s, turn, first=False, last=False):
                if not last:
                    x_hi(i + 1, 1 - s)
                if not first:
                    h_hi(i - 1, 1 - s)
                silu(i, s)
                if not first:
                    y_copy(i - 1, 1 - s, turn)

            act.wait_ge(scattered, 16 * 2 * TILES)
            x_hi(0, 0)
            step(0, 0, None, first=True)
            step(1, 1, None)
            step(2, 0, None)
            step(3, 1, 1)
            with act.Fori(2, MT // 2 - 1) as g:
                step(g * 2, 0, g - 1)
                step(g * 2 + 1, 1, g)
            step(MT - 2, 0, MT // 2 - 2)
            step(MT - 1, 1, MT // 2 - 1, last=True)
            h_hi(MT - 1, 1)
            y_copy(MT - 1, 1, MT // 2 - 1)

            for t in range(TILES):
                act.wait_ge(g_loaded[t % GRING], 32 * (t // GRING + 1))
                if t >= 2:
                    act.wait_ge(gt_ready, t - 1)
                act.activation(gs[:, t % 2, :], g1[:, t % GRING, :], ACT.Copy, scale=score[:, 0, t:t + 1])\
                    .then_inc(gs_ready, 1)

        @block.vector
        def _(v):
            steps = [0]

            def link(ins):
                steps[0] += 1
                ins.then_inc(dve, 1)
                v.wait_ge(dve, steps[0])

            def count(ins):
                steps[0] += 1
                return ins.then_inc(dve, 1)

            link(v.memset(zero[:, :], 0.0))
            link(v.memset(eps[:, 0:1], 1e-6))
            link(v.memset(eps[:, 1:2], 1e-5))

            def patch_weights(l, g):
                sl = slice(g * GR, (g + 1) * GR)
                v.wait_ge(sd_ready, l * NG + g + 1)
                link(v.reciprocal(RS[0:ROWT, sl], SD[0:ROWT, sl]))
                ins = v.tensor_tensor(RI[:, sl, :], RS[0:ROWT, sl].unsqueeze(2).broadcast_to((ROWT, GR, 3)),
                                      ind[:, :].unsqueeze(1).broadcast_to((ROWT, GR, 3)), ALU.mult)
                ins.then_inc(ri_ready, 1)
                v.wait_ge(ri_ready, l * 2 * NG + 2 * g + 1)
                v.tensor_tensor(RM[:, sl, :], RI[:, sl, :],
                                MV[0:ROWT, sl, 0].unsqueeze(2).broadcast_to((ROWT, GR, 3)), ALU.mult)\
                    .then_inc(ri_ready, 1)

            def patches(l):
                v.wait_ge(mixw, l * 160 + 160)
                v.tensor_copy(upM[:, :, :], upS[:, :, :]).then_inc(g_ready, 1)
                for g in range(NG):
                    for t in range(g * GR, (g + 1) * GR):
                        v.wait_ge(xtok_ready, l * NROW + t + 1)
                        v.bn_stats(ST6[0:ROWT, :], xtok[:, t % XR, :]).then_inc(st_done, 1)
                        v.wait_ge(st_done, l * NROW + t + 1)
                        v.bn_aggr(MV[0:ROWT, t, :], ST6[0:ROWT, :]).then_inc(mv_done, 1)
                        v.wait_ge(mv_done, l * NROW + t + 1)
                    if g:
                        patch_weights(l, g - 1)
                patch_weights(l, NG - 1)
                v.wait_ge(mterm_ready, l + 1)
                for a in range(2):
                    v.tensor_tensor(pT[:, 2 * a:2 * a + 2, :],
                                    PS[:, 4 + a, 0:2 * NT].rearrange("p (k t) -> p k t", k=2),
                                    mterm[:, :].unsqueeze(1).broadcast_to((P, 2, NT)), ALU.subtract)\
                        .then_inc(p_ready, 1)

            def mixer(l):
                v.wait_ge(tok_ready, l + 1)
                link(v.tensor_tensor(tk[:, :, :], PS[0:TT, 0:2, 0:HID],
                                     vhid[:, 0:1, :].broadcast_to((TT, 2, HID)), ALU.add))
                for tt in range(2):
                    link(v.bn_stats(sth[:, tt, :], tk[:, tt, :]))
                    v.bn_aggr(mvh[:, tt, :], sth[:, tt, :]).then_inc(var_h, 1)
                v.wait_ge(var_h, l * 2 + 2)
                v.wait_ge(sd_h, l + 1)
                link(v.reciprocal(rsh[:, :], sdh[:, :]))
                for tt in range(2):
                    link(v.tensor_scalar(tk[:, tt, :], tk[:, tt, :], mvh[:, tt, 0:1], rsh[:, tt:tt + 1],
                                         ALU.subtract, ALU.mult))
                link(v.tensor_tensor(tk[:, :, :], tk[:, :, :], vhid[:, 1:2, :].broadcast_to((TT, 2, HID)), ALU.mult))
                v.tensor_tensor(tk[:, :, :], tk[:, :, :], vhid[:, 2:3, :].broadcast_to((TT, 2, HID)), ALU.add)\
                    .then_inc(tk_ready, 1)
                v.memset(a1[:, :, :].rearrange("p n (b t) -> p (n b) t", t=L)[:, :, 0:1], 0.0).then_inc(a1_zero, 1)
                v.wait_ge(xz_ready, l * 2 + 1)
                img = lambda ap: ap.rearrange("p (b t) -> p b t", t=L)
                for j in range(JC):
                    src = PS[:, 3, j * NT:(j + 1) * NT]
                    link(v.tensor_scalar(acc[:, j, :], src, vinn[:, j, 1:2], vinn[:, j, 3:4], ALU.mult, ALU.add))
                    link(v.scalar_tensor_tensor(img(acc[:, j, :])[:, :, 1:], img(src)[:, :, :L - 1], vinn[:, j, 0:1],
                                                img(acc[:, j, :])[:, :, 1:], ALU.mult, ALU.add))
                    last = v.scalar_tensor_tensor(img(acc[:, j, :])[:, :, :L - 1], img(src)[:, :, 1:], vinn[:, j, 2:3],
                                                  img(acc[:, j, :])[:, :, :L - 1], ALU.mult, ALU.add)
                    if j < JC - 1:
                        link(last)
                last.then_inc(acc_ready, 1)
                v.wait_ge(dbc_ready, l * 2 + 1)
                v.tensor_copy(bc[:, :], PS[0:2 * NS, 5, 0:NT]).then_inc(bc_ready, 1)
                v.wait_ge(dbc_ready, l * 2 + 2)
                v.tensor_copy(dl[:, :], PS[0:RANK, 6, 0:NT]).then_inc(dl_ready, 1)
                v.wait_ge(ea_ready, l + 1)
                v.tensor_scalar(negA[:, :, :], negA[:, :, :], -1.0, None, ALU.mult).then_inc(na_ready, 1)
                v.wait_ge(dt_ready, l + 1)
                for j in range(JC):
                    link(v.tensor_scalar(dx[:, j, :], PS[:, 7, j * NT:(j + 1) * NT], vinn[:, j, 4:5], None, ALU.add))
                v.scalar_tensor_tensor(ab[:, :, :], dx[:, :, :], -1.0, dx[:, :, :], ALU.mult, ALU.max)\
                    .then_inc(ab_ready, 1)
                v.wait_ge(ex_done, l * 2 + 2)
                v.scalar_tensor_tensor(delta[:, :, :], dx[:, :, :], 0.0, ab[:, :, :], ALU.max, ALU.add)\
                    .then_inc(sp_ready, 1)
                v.wait_ge(sp_ready, l + 1)
                v.wait_ge(u_ready, l + 1)
                v.tensor_tensor(du[:, :, :], delta[:, :, :], uu[:, :, :], ALU.mult).then_inc(du_ready, 1)
                v.wait_ge(bc_in, l * 16 + 16)
                v.wait_ge(a1_zero, l + 1)
                flat = lambda ap: ap.rearrange("p n t -> p (n t)")
                for j in range(JC):
                    v.wait_ge(a1_ready, l * JC + j + 1)
                    v.wait_ge(db_ready, l * JC + j + 1)
                    v.tensor_tensor_scan(flat(hs[:, :, :]), flat(a1[:, :, :]), flat(db[:, :, :]), 0.0,
                                         ALU.mult, ALU.add).then_inc(scanned, 1)
                    v.wait_ge(scanned, l * JC + j + 1)
                    link(v.tensor_tensor(hs[:, :, :], hs[:, :, :], Bb[:, NS:, :], ALU.mult))
                    link(v.tensor_reduce(yy[:, j, :], hs[:, :, :].rearrange("p n t -> p t n"), AX.X, ALU.add))
                for j in range(JC):
                    link(v.scalar_tensor_tensor(yy[:, j, :], uu[:, j, :], vinn[:, j, 5:6], yy[:, j, :],
                                                ALU.mult, ALU.add))
                v.wait_ge(z_ready, l + 1)
                v.tensor_tensor(yy[:, :, :], yy[:, :, :], sz[:, :, :], ALU.mult).then_inc(y_ready, 1)
                v.wait_ge(gh_ready, l + 1)
                v.tensor_tensor(gL[:, :, :], PS[0:TT, 0:2, :], gH[:, :, :].bitcast(f32), ALU.subtract)\
                    .then_inc(g_ready, 1)
                v.wait_ge(g_ready, l * 2 + 2)

            def add_upsampled(l, b):
                for half in range(2):
                    v.wait_ge(up_ready, l * 2 * B + 2 * b + half + 1)
                    dst = X[:, 2 * half:2 * half + 2, b * S:(b + 1) * S]
                    v.tensor_tensor(dst, dst, PS[:, 2 + 2 * half:4 + 2 * half, 0:S], ALU.add).then_inc(up_added, 1)

            def token_stats(l, q, src, at, frees):
                v.bn_stats(ST6[:, :], src).then_inc(lst_done if not frees else lt_free, 1)
                v.wait_ge(lst_done if not frees else lt_free, q + 1)
                v.bn_aggr(MV[:, at, :], ST6[:, :]).then_inc(lmv_done, 1)
                v.wait_ge(lmv_done, l * TILES + q + 1)

            def first_stats(q):
                v.wait_ge(lt_ready, q + 1)
                token_stats(0, q, PS[:, TB[q % len(TB)], :], (q % E0) * EJ + q // E0, True)

            patches(0)
            mixer(0)
            q = 0
            for b in range(B):
                add_upsampled(0, b)
                while q < TILES and images_before(E0 * P * (q // E0 + 1)) <= b:
                    first_stats(q)
                    q += 1
            while q < TILES:
                first_stats(q)
                q += 1
            v.wait_ge(lsd_ready, 1)
            v.reciprocal(MR[:, 0:TILES], SD[:, 0:TILES]).then_inc(mr_ready, 1)
            v.wait_ge(mr_ready, 1)
            v.tensor_tensor(MR[:, TILES:], MR[:, 0:TILES], MV[:, 0:TILES, 0], ALU.mult).then_inc(mr_ready, 1)

            v.wait_ge(stats_out, 16)
            for free, n in ((gu_free, 2), (sg_free, 2), (rm_free, 1), (dn_free, 1)):
                v.sem_inc(free, n)

            def normalise(n, r):
                v.wait_ge(rm_loaded, n * 16 + 16)
                e, c = n // NC, n % NC
                src = Xe[:, :, ds(e, 1), ds(c * CN, CN)].rearrange("p k e n -> p k (e n)") \
                    if not isinstance(n, int) else Xe[:, :, e, c * CN:(c + 1) * CN]
                v.tensor_tensor(xr[:, :, :], src, rmb[:, 0:1, :].broadcast_to((P, KC, CN)), ALU.mult)\
                    .then_inc(xr_done, 1)
                v.wait_ge(xr_done, n * 2 + 1)
                v.tensor_tensor(xr[:, :, :], xr[:, :, :], rmb[:, 1:2, :].broadcast_to((P, KC, CN)), ALU.subtract)\
                    .then_inc(xr_done, 1)
                v.wait_ge(xr_done, n * 2 + 2)
                v.sem_inc(rm_free, 1)
                if not isinstance(n, int) or n:
                    v.wait_ge(gu_ready, n * KC)
                v.tensor_copy(xnH[:, :, :], xr[:, :, :]).then_inc(it_step, 1)
                v.wait_ge(it_step, n * (2 * KC + 1) + 1)
                v.tensor_tensor(xnL[:, :, :], xr[:, :, :], xnH[:, :, :].bitcast(f32), ALU.subtract)\
                    .then_inc(xn_ready, 1)
                v.wait_ge(xn_ready, n + 1)

            def chunk(n, r, last=False):
                e, c = n // NC, n % NC
                for m in range(KC):
                    v.wait_ge(sg_ready, n * KC + m + 1)
                    v.tensor_tensor(sg[:, m % 2, :], sg[:, m % 2, :], PS[:, 2 * (m % 2) + 1, 0:CN], ALU.mult)\
                        .then_inc(gu_free, 1)
                    v.wait_ge(gu_free, n * KC + m + 3)
                    v.tensor_copy(itH[:, m, :], sg[:, m % 2, :]).then_inc(it_step, 1)
                    v.wait_ge(it_step, n * (2 * KC + 1) + (2 * m + 2))
                    v.tensor_tensor(itL[:, m, :], sg[:, m % 2, :], itH[:, m, :].bitcast(f32), ALU.subtract)\
                        .then_inc(it_step, 1)
                    v.wait_ge(it_step, n * (2 * KC + 1) + (2 * m + 3))
                    v.sem_inc(it_ready, 1)
                    v.sem_inc(sg_free, 1)
                if not last:
                    normalise(n + 1, 1 - r)
                v.wait_ge(dn_ready, n + 1)
                dst = Xe[:, :, ds(e, 1), ds(c * CN, CN)].rearrange("p k e n -> p k (e n)") \
                    if not isinstance(n, int) else Xe[:, :, e, c * CN:(c + 1) * CN]
                v.tensor_tensor(dst, dst, PS[:, 4:8, 0:CN], ALU.add).then_inc(dn_free, 1)

            normalise(0, 0)
            with v.Fori(0, E0 * NC // 2 - 1) as nn:
                for r in range(2):
                    chunk(nn * 2 + r, r)
            chunk(E0 * NC - 2, 0)
            chunk(E0 * NC - 1, 1, last=True)
            v.wait_ge(dn_free, E0 * NC + 1)

            patches(1)
            mixer(1)
            v.wait_ge(wb_sb, 1)
            v.wait_ge(upm, 16)
            v.tensor_tensor(rw[:, :, :], rw[:, :, :], wbar[:, :].unsqueeze(1).broadcast_to((P, KC, E1)), ALU.subtract)\
                .then_inc(rw_ready, 1)
            t = 0
            for b in range(B):
                add_upsampled(1, b)
                while t < TILES and images_before(P * (t + 1)) <= b:
                    v.wait_ge(lt_free, TILES + t + 1)
                    token_stats(1, t, XN[:, t, :], t, False)
                    t += 1
            while t < TILES:
                v.wait_ge(lt_free, TILES + t + 1)
                token_stats(1, t, XN[:, t, :], t, False)
                t += 1
            v.wait_ge(lsd_ready, 1 + 1)
            link(v.reciprocal(RS[:, 0:TILES], SD[:, 0:TILES]))
            v.scalar_tensor_tensor(nmr[:, :], MV[:, 0:TILES, 0], -1.0, RS[:, 0:TILES], ALU.mult, ALU.mult)\
                .then_inc(nmr_ready, 1)

            full = (P, TILES, E1)
            by_tile = lambda ap: ap.unsqueeze(2).broadcast_to(full)
            by_expert = lambda ap: ap.unsqueeze(1).broadcast_to(full)
            A = {n: ap[:, :, :] for n, ap in R.items()}
            Q = {n: ap[:, :] for n, ap in q36.items()}
            v.wait_ge(logit_ready, 1)
            v.wait_ge(upm, 32)
            link(v.tensor_tensor(A["log"], PS[:, 1, 0:TILES * E1].rearrange("p (t e) -> p t e", e=E1),
                                 by_tile(RS[:, 0:TILES]), ALU.mult))
            link(v.tensor_reduce(Q["mx"], A["log"], AX.X, ALU.max))
            v.tensor_tensor(A["t"], A["log"], by_tile(Q["mx"]), ALU.subtract).then_inc(rexp_in, 1)
            v.wait_ge(r_e, 1)
            link(v.tensor_reduce(Q["sm"], A["e"], AX.X, ALU.add))
            link(v.reciprocal(Q["rs"], Q["sm"]))
            link(v.tensor_tensor(A["p"], A["e"], by_tile(Q["rs"]), ALU.mult))

            def best(m, onehot):
                link(v.tensor_reduce(m, A["p"], AX.X, ALU.max))
                link(v.tensor_tensor(A["t"], A["p"], by_tile(m), ALU.is_equal))
                link(v.tensor_tensor(A["t"], A["t"], by_expert(w8), ALU.mult))
                link(v.tensor_reduce(Q["k"], A["t"], AX.X, ALU.max))
                link(v.tensor_tensor(onehot, by_expert(w8), by_tile(Q["k"]), ALU.is_equal))

            best(Q["m1"], A["oh1"])
            link(v.scalar_tensor_tensor(A["p"], A["oh1"], -2.0, A["p"], ALU.mult, ALU.add))
            best(Q["m2"], A["oh2"])
            v.tensor_tensor(A["O"], A["oh1"], A["oh2"], ALU.add).then_inc(r_O, 1)
            link(v.tensor_tensor(Q["den"], Q["m1"], Q["m2"], ALU.add))
            link(v.reciprocal(Q["den"], Q["den"]))
            link(v.tensor_tensor(score[:, 0, :], Q["m1"], Q["den"], ALU.mult))
            link(v.tensor_tensor(score[:, 1, :], Q["m2"], Q["den"], ALU.mult))
            v.wait_ge(r_tot, 1)
            tot, inc, exc, cmp = (scT[n][:, :, :] for n in ("tot", "inc", "exc", "cmp"))
            nt, end, base = (e8[n][:, :] for n in ("nt", "end", "base"))
            flat = lambda ap: ap.rearrange("p e t -> p (e t)")
            link(v.tensor_tensor_scan(flat(inc), jmask, flat(tot), 0.0, ALU.mult, ALU.add))
            link(v.tensor_tensor(exc, inc, tot, ALU.subtract))
            link(v.tensor_tensor(cmp, inc[:, :, TILES - 1:TILES].broadcast_to((P, E1, TILES)),
                                 j128.unsqueeze(1).broadcast_to((P, E1, TILES)), ALU.is_gt))
            link(v.tensor_reduce(nt, cmp, AX.X, ALU.add))
            link(v.tensor_tensor_scan(end, one8, nt, 0.0, ALU.mult, ALU.add))
            link(v.tensor_tensor(base, end, nt, ALU.subtract))
            link(v.tensor_scalar(base, base, float(P), None, ALU.mult))
            link(v.tensor_scalar(tile_end[:, :], end, 1.0, None, ALU.max))
            link(v.tensor_tensor(tcmp[:, :, :], end[:, 0:E1 - 1].unsqueeze(1).broadcast_to((P, MT, E1 - 1)),
                                 iMT.unsqueeze(2).broadcast_to((P, MT, E1 - 1)), ALU.is_le))
            link(v.tensor_reduce(texp[:, :], tcmp[:, :, :], AX.X, ALU.add))
            link(v.tensor_copy(tile_expert[:, :], texp[:, :]))
            v.wait_ge(r_pre, 2)
            link(v.tensor_tensor(A["pe"], PS[:, 2, 0:TILES * E1].rearrange("p (t e) -> p t e", e=E1),
                                 exc.rearrange("p e t -> p t e"), ALU.add))
            link(v.tensor_tensor(A["pe"], A["pe"], by_expert(base), ALU.add))
            for k, oh in enumerate(("oh1", "oh2")):
                link(v.tensor_tensor(A["t"], A["pe"], A[oh], ALU.mult))
                link(v.tensor_reduce(Q["pf"], A["t"], AX.X, ALU.add))
                link(v.tensor_copy(pos[:, k, :], Q["pf"]))
                v.sem_inc(routed, 1)

            def x_lo(i, s):
                v.wait_ge(xt_hi, i + 1)
                v.tensor_tensor(xtL[:, s, :, :], PS[:, s, :].rearrange("p (k n) -> p k n", n=P),
                                xtH[:, s, :, :].bitcast(f32), ALU.subtract).then_inc(xt_ready, 1)

            def hidden(i, s):
                v.wait_ge(sgt_ready, i + 1)
                behind(v, th_ready, i)
                v.tensor_tensor(hh[:, s, :], sgt[:, s, :], PS[:, 2 + s, 1:512:2], ALU.mult).then_inc(h_ready, 1)

            def h_lo(i, s):
                v.wait_ge(ht_hi, i + 1)
                v.tensor_tensor(htL[:, s, :, :], PS[:, 4 + s, 0:2 * P].rearrange("p (k n) -> p k n", n=P),
                                htH[:, s, :, :].bitcast(f32), ALU.subtract).then_inc(ht_ready, 1)

            def step(i, s, first=False, last=False):
                if not last:
                    x_lo(i + 1, 1 - s)
                if not first:
                    h_lo(i - 1, 1 - s)
                hidden(i, s)

            v.wait_ge(scattered, 16 * 2 * TILES)
            x_lo(0, 0)
            step(0, 0, first=True)
            step(1, 1)
            with v.Fori(1, MT // 2 - 1) as g:
                for s in range(2):
                    step(g * 2 + s, s)
            step(MT - 2, 0)
            step(MT - 1, 1, last=True)
            h_lo(MT - 1, 1)

            def add_out(t):
                v.wait_ge(f_ready, t + 1)
                dst = X[:, :, t * P:(t + 1) * P]
                v.tensor_tensor(dst, dst, PS[:, t % 4, :].rearrange("p (k n) -> p k n", n=P), ALU.add)\
                    .then_inc(f_added, 1)

            for t in range(TILES):
                v.wait_ge(gs_ready, t + 1)
                if t >= 2:
                    v.wait_ge(f_ready, t - 1)
                v.scalar_tensor_tensor(gt[:, t % 2, :], g2[:, t % GRING, :], score[:, 1, t:t + 1], gs[:, t % 2, :],
                                       ALU.mult, ALU.add).then_inc(gt_ready, 1)
                if t:
                    add_out(t - 1)
            add_out(TILES - 1)


def bilinear():
    def axis(n):
        at = np.maximum((np.arange(n, dtype=np.float32) + np.float32(0.5)) * np.float32(3 / n) - np.float32(0.5), 0)
        i0 = np.minimum(np.floor(at).astype(np.int32), 2)
        i1 = np.minimum(i0 + 1, 2)
        w = at - i0.astype(np.float32)
        m = np.zeros((3, n), np.float32)
        for o in range(n):
            m[i0[o], o] += 1 - w[o]
            m[i1[o], o] += w[o]
        return m
    return np.einsum("ay,bx->abyx", axis(H), axis(W)).reshape(L, S)


def constants():
    mats = np.stack([np.eye(P), np.ones((P, P)), np.triu(np.ones((P, P)), 1)], 1).astype(np.float32)
    token = np.arange(ROWT)
    ind = (((token % W) // (W // 3))[:, None] == np.arange(3)).astype(np.float32) / (H // 3 * W // 3)
    up = np.zeros((IB, L, IB, S), np.float32)
    for b in range(IB):
        up[b, :, b] = bilinear()
    mask = np.ones((E1, TILES), np.float32)
    mask[:, 0] = 0
    row = np.concatenate([E1 - np.arange(E1), P * np.arange(TILES), np.arange(MT), mask.ravel()]).astype(np.float32)
    return {"c_mat": mats, "c_ind": ind, "c_up": up.reshape(TT, IB, S), "c_rout": np.tile(row, (P, 1))}


def kernel(**inputs):
    import concourse.bacc as bacc
    from concourse.bass_utils import run_bass_kernel_spmd

    def both(name):
        return [np.asarray(inputs[f"L{l}_conv_{name}"]) for l in range(2)]

    def rows(a, n):
        return a.reshape(n, a.shape[0] // n, *a.shape[1:]).swapaxes(0, 1)

    arrays = {"x": np.asarray(inputs["x"]).reshape(B, CH, S)}
    arrays |= constants()
    arrays["pe_W"] = np.stack([rows(a, KC) for a in both("pe_W")])
    arrays["vec_hid"] = np.stack([np.stack(v) for v in zip(both("pe_b"), both("ln_g"), both("ln_b"))])
    arrays["in_W"] = np.stack([rows(a, 2) for a in both("in_W")])
    arrays["vec_inner"] = np.stack([
        rows(np.concatenate([w.reshape(INNER, 3), cb[:, None], tb[:, None], d[:, None]], 1), JC)
        for w, cb, tb, d in zip(both("conv_w"), both("conv_b"), both("dt_b"), both("D_param"))])
    arrays["a_log"] = np.stack([rows(a, JC) for a in both("A_log")])
    arrays["xproj"] = np.stack([rows(a, JC) for a in both("xproj_W")])
    arrays["dt_W"] = np.stack(both("dt_W"))
    arrays["out_W"] = np.stack([rows(a, JC) for a in both("out_W")])
    gu0, dn0 = np.asarray(inputs["L0_ffn_gate_up_proj"]), np.asarray(inputs["L0_ffn_down_proj"])
    gu1, dn1 = np.asarray(inputs["L1_ffn_expert_gate_up"]), np.asarray(inputs["L1_ffn_expert_down"])

    def pieces(a, n):
        e, r, c = a.shape
        return a.reshape(e, n, r // (n * P), P, c).swapaxes(2, 3).reshape(e, n, P, PIECE)

    w0 = np.concatenate([pieces(gu0, KC), pieces(dn0, 2)], 1).reshape(NP0, P, PIECE)
    w1 = np.concatenate([pieces(gu1, 2), pieces(dn1, 1)], 1).reshape(NP1, P, PIECE)
    arrays["w_ffn"] = np.concatenate([w0, w1])
    arrays["router"] = rows(np.asarray(inputs["L1_ffn_router_gate"]).T, KC)

    nc = bacc.Bacc("TRN2", target_bir_lowering=False, num_devices=1)
    data, args = {}, []
    for name, a in arrays.items():
        a = np.ascontiguousarray(a)
        data[f"in_{name}"] = a
        args.append(nc.dram_tensor(f"in_{name}", a.shape, mybir.dt.from_np(a.dtype), kind="ExternalInput").ap())
    args.append(nc.dram_tensor("out_x", (B, CH, S), mybir.dt.float32, kind="ExternalOutput").ap())
    metaformer(nc, *args)
    r = run_bass_kernel_spmd(nc, [data], core_ids=[0])
    return r.results[0]["out_x"].reshape(B, CH, H, W)
```

```python
from contextlib import ExitStack

import concourse.bass as bass
import numpy as np
from concourse import mybir

P = 128
B, CH, H, W = 16, 512, 24, 12
S = H * W
T = B * S
KC = CH // P
HID, INNER, NS, RANK = 192, 384, 16, 48
HH = HID // 2
JC = INNER // P
L = 9
NT = B * L
TT = NT // 2
IB = B // 2
ROWT = S // 3
NROW = T // ROWT
XG = 8
GR = 6
NG = NROW // GR
XR = 3 * GR
TILES = T // P
E0, I0 = 4, 512
E1, I1 = 8, 256
CN = 288
NC = T // E0 // CN
EJ = TILES // E0
PIECE = 1024
PE0 = KC * (2 * I0 + CH) // PIECE
PE1 = (KC * 2 * I1 + 2 * CH) // PIECE
NP0, NP1 = E0 * PE0, E1 * PE1
MT = 2 * TILES + E1
ZT = 4
XSR = 4
GRING = 4
TB = (6, 7, 0)
RB = (6, 0)
RC = 256


def metaformer(nc, x, c_mat, c_ind, c_up, c_rout, pe_W, vec_hid, in_W, vec_inner, a_log, xproj, dt_W, out_W,
               w_ffn, router, out):
    f32, f32r, i32 = mybir.dt.float32, mybir.dt.float32r, mybir.dt.int32
    ALU, ACT, AX = mybir.AluOpType, mybir.ActivationFunctionType, mybir.AxisListType
    ds = bass.ds

    bc_dram = nc.dram_tensor("bc_dram", (2, 2 * NS, NT), f32, kind="Internal").ap()
    stat_dram = nc.dram_tensor("stat_dram", (2, E0, EJ * P), f32, kind="Internal").ap()
    xs_dram = nc.dram_tensor("xs_dram", (MT * P, CH), f32, kind="Internal").ap()
    y_dram = nc.dram_tensor("y_dram", (MT * P, CH), f32, kind="Internal").ap()

    ctx = ExitStack()
    with ctx:
        def sb(name, shape, dt=f32, life=ctx):
            return life.enter_context(nc.sbuf_tensor("sb_" + name, shape, dt))

        def sem(name):
            return ctx.enter_context(nc.semaphore(name))

        X = sb("X", [P, KC, T])
        mats = sb("mats", [P, 3, P])
        ident, ones, triu = mats[:, 0, :], mats[:, 1, :], mats[:, 2, :]
        eps = sb("eps", [P, 2])
        zero = sb("zero", [P, P])
        raw = sb("raw", [P, 2, PIECE])
        MV = sb("MV", [P, NROW, 2])
        ST6 = sb("ST6", [P, 2, GR, 6])
        SD = sb("SD", [P, NROW])
        RS = sb("RS", [P, NROW])
        PS = ctx.enter_context(nc.psum_tensor("ps", [P, 8, 512], f32))

        mix = ExitStack()
        before = nc.sbuf_bytes_remaining
        score = sb("score", [P, 2, TILES], f32, mix)
        pos = sb("pos", [P, 2, TILES], i32, mix)
        tile_expert = sb("tile_expert", [P, MT], i32, mix)
        tile_end = sb("tile_end", [P, E1], i32, mix)
        kept = before - nc.sbuf_bytes_remaining
        tables = ExitStack()
        R = {n: sb("R_" + n, [P, TILES, E1], f32, tables)
             for n in ("log", "e", "p", "oh1", "oh2", "t", "O", "pe")}
        q36 = {n: sb("q_" + n, [P, TILES], f32, tables) for n in ("mx", "sm", "rs", "m1", "m2", "k", "den", "pf")}
        scT = {n: sb("s_" + n, [P, E1, TILES], f32, tables) for n in ("tot", "inc", "exc", "cmp")}
        tables_end = nc.sbuf_bytes_remaining
        tables.close()
        gH = sb("gH", [TT, 2, CH], f32r, mix)
        gL = sb("gL", [TT, 2, CH], f32r, mix)
        upM = sb("upM", [TT, IB, S], f32r, mix)
        assert nc.sbuf_bytes_remaining <= tables_end
        MR = sb("MR", [P, 2 * TILES], f32, mix)
        statT = sb("statT", [2 * TILES, P], f32, mix)
        wbar = sb("wbar", [P, E1], f32, mix)
        body = ExitStack()
        mterm = sb("mterm", [P, NT], f32, body)
        pT = sb("pT", [P, KC, NT], f32, body)
        peW = sb("peW", [P, KC, HID], f32, body)
        vhid = sb("vhid", [TT, 3, HID], f32, body)
        inW = sb("inW", [HH, 2, 2 * INNER], f32, body)
        vinn = sb("vinn", [P, JC, 6], f32, body)
        alog = sb("alog", [P, JC, NS], f32, body)
        xpW = sb("xpW", [P, JC, RANK + 2 * NS], f32, body)
        dtW = sb("dtW", [RANK, INNER], f32, body)
        outW = sb("outW", [P, JC, CH], f32, body)
        tk = sb("tk", [TT, 2, HID], f32, body)
        mvh = sb("mvh", [TT, 2, 2], f32, body)
        sth = sb("sth", [TT, 2, 6], f32, body)
        sdh = sb("sdh", [TT, 2], f32, body)
        rsh = sb("rsh", [TT, 2], f32, body)
        tT = sb("tT", [HH, 2, NT], f32, body)
        acc = sb("acc", [P, JC, NT], f32, body)
        uu = sb("uu", [P, JC, NT], f32, body)
        sz = sb("sz", [P, JC, NT], f32, body)
        bc = sb("bc", [2 * NS, NT], f32, body)
        dl = sb("dl", [RANK, NT], f32, body)
        dx = sb("dx", [P, JC, NT], f32, body)
        ab = sb("ab", [P, JC, NT], f32, body)
        delta = sb("delta", [P, JC, NT], f32, body)
        du = dx
        negA = sb("negA", [P, JC, NS], f32, body)
        yy = sb("yy", [P, JC, NT], f32, body)
        patch = ExitStack()
        xtok = sb("xtok", [ROWT, XR, CH], f32, patch)
        ind = sb("ind", [ROWT, 3], f32, patch)
        RI = sb("RI", [ROWT, NROW, 3], f32, patch)
        RM = sb("RM", [ROWT, NROW, 3], f32, patch)
        upS = sb("upS", [TT, IB, S], f32, patch)
        patch.close()
        scan_at = nc.sbuf_bytes_remaining
        db = sb("db", [P, 2, NS, NT], f32, body)
        hs = sb("hs", [P, NS, NT], f32, body)
        Bb = sb("Bb", [P, 2 * NS, NT], f32, body)
        a1 = sb("a1", [P, 2, NS, NT], f32, body)
        body.close()
        moe_in = ExitStack()
        XN = sb("XN", [P, TILES, CH], f32, moe_in)
        rout = sb("rout", [P, E1 + TILES + MT + E1 * TILES], f32, moe_in)
        e8 = {n: sb("e_" + n, [P, E1], f32, moe_in) for n in ("nt", "end", "base")}
        tcmp = sb("tcmp", [P, MT, E1 - 1], f32, moe_in)
        texp = sb("texp", [P, MT], f32, moe_in)
        nmr = sb("nmr", [P, TILES], f32, moe_in)
        eyeR = sb("eyeR", [P, KC, P + E1], f32, moe_in)
        rw = eyeR[:, :, P:]
        logits = sb("logits", [P, TILES, E1], f32, moe_in)
        moe_in_end = nc.sbuf_bytes_remaining
        moe_in.close()
        mix.close()
        ffn0 = ExitStack()
        w0 = [None, sb("w0_1", [P, 2, PE0 * PIECE], f32r, ffn0)]
        rmb = sb("rmb", [P, 2, CN], f32, ffn0)
        xr = sb("xr", [P, KC, CN], f32, ffn0)
        sg = sb("sg", [P, 2, CN], f32, ffn0)
        sb("pad0", [P, (nc.sbuf_bytes_remaining - scan_at) // 4], f32, ffn0)
        w0[0] = sb("w0_0", [P, 2, PE0 * PIECE], f32r, ffn0)
        xnH = sb("xnH", [P, KC, CN], f32r, ffn0)
        xnL = sb("xnL", [P, KC, CN], f32r, ffn0)
        itH = sb("itH", [P, KC, CN], f32r, ffn0)
        itL = sb("itL", [P, KC, CN], f32r, ffn0)
        ffn0.close()
        ffn1 = ExitStack()
        sb("pad2", [P, kept // 4], f32, ffn1)
        xs = sb("xs", [P, XSR, CH], f32, ffn1)
        xtH = sb("xtH", [P, 2, KC, P], f32r, ffn1)
        xtL = sb("xtL", [P, 2, KC, P], f32r, ffn1)
        sgt = sb("sgt", [P, 2, I1], f32, ffn1)
        hh = sb("hh", [P, 2, I1], f32, ffn1)
        htH = sb("htH", [P, 2, 2, P], f32r, ffn1)
        htL = sb("htL", [P, 2, 2, P], f32r, ffn1)
        ysb = sb("ysb", [P, 2, CH], f32, ffn1)
        g1 = sb("g1", [P, GRING, CH], f32, ffn1)
        g2 = sb("g2", [P, GRING, CH], f32, ffn1)
        gs = sb("gs", [P, 2, CH], f32, ffn1)
        gt = sb("gt", [P, 2, CH], f32, ffn1)
        W1B = 2 * 2 * PE1 * PIECE * 4
        assert moe_in_end >= W1B // 2 and nc.sbuf_bytes_remaining >= W1B
        sb("pad1", [P, (nc.sbuf_bytes_remaining - W1B) // 4], f32, ffn1)
        w1 = sb("w1", [P, 2, 2, 2 * PE1, 512], f32r, ffn1)
        ffn1.close()

        Xe = X[:, :, :].rearrange("p k (t e) -> p k e t", e=E0)
        w8 = rout[:, 0:E1]
        j128 = rout[:, E1:E1 + TILES]
        iMT = rout[:, E1 + TILES:E1 + TILES + MT]
        jmask = rout[:, E1 + TILES + MT:]
        one8 = ones[:, 0:E1]

        consts, filled = sem("consts"), sem("filled")
        x_loaded = [sem(f"x_loaded_{g}") for g in range(XG)]
        mixw, upm = sem("mix_weights"), sem("up_matrix")
        tp_ready, xtok_ready = sem("tp_ready"), sem("xtok_ready")
        st_done, mv_done, sd_ready = sem("st_done"), sem("mv_done"), sem("sd_ready")
        ri_ready, pooled = sem("ri_ready"), sem("pooled")
        mterm_ready, p_ready, tok_ready = sem("mterm_ready"), sem("p_ready"), sem("tok_ready")
        var_h, sd_h, tk_ready, tkT = sem("var_h"), sem("sd_h"), sem("tk_ready"), sem("tkT")
        tT_ready, xz_ready, acc_ready = sem("tT_ready"), sem("xz_ready"), sem("acc_ready")
        u_ready, z_ready, dbc_ready = sem("u_ready"), sem("z_ready"), sem("dbc_ready")
        bc_ready, bc_out, bc_in, dl_ready = sem("bc_ready"), sem("bc_out"), sem("bc_in"), sem("dl_ready")
        dt_ready, ab_ready, ex_done, sp_ready = sem("dt_ready"), sem("ab_ready"), sem("ex_done"), sem("sp_ready")
        ea_ready, na_ready, du_ready = sem("ea_ready"), sem("na_ready"), sem("du_ready")
        db_ready, a1_ready, hc_ready, ysum = sem("db_ready"), sem("a1_ready"), sem("hc_ready"), sem("ysum")
        a1_zero, scanned = sem("a1_zero"), sem("scanned")
        y_ready, og_ready, gh_ready, g_ready = sem("y_ready"), sem("og_ready"), sem("gh_ready"), sem("g_ready")
        up_ready, up_added = sem("up_ready"), sem("up_added")
        lt_ready, lt_free, lst_done, lmv_done = sem("lt_ready"), sem("lt_free"), sem("lst_done"), sem("lmv_done")
        lsd_ready, mr_ready = sem("lsd_ready"), sem("mr_ready")
        mrT, statT_ready, stats_out = sem("mrT"), sem("statT_ready"), sem("stats_out")
        dve = sem("dve_step")
        raw_loaded, split_step = [sem(f"raw_loaded_{r}") for r in range(2)], sem("split_step")
        w0_ready = sem("w0_ready")
        rm_loaded, rm_free, xr_done = sem("rm_loaded"), sem("rm_free"), sem("xr_done")
        xn_ready = sem("xn_ready")
        gu_ready, gu_free, sg_ready, sg_free = sem("gu_ready"), sem("gu_free"), sem("sg_ready"), sem("sg_free")
        it_step, it_ready = sem("it_step"), sem("it_ready")
        dn_ready, dn_free = sem("dn_ready"), sem("dn_free")
        wb_ready, wb_sb, rw_ready = sem("wb_ready"), sem("wb_sb"), sem("rw_ready")
        logits_ready, r_e, r_O, r_pre, r_tot = (sem("logits_ready"), sem("router_exp"), sem("router_onehot"),
                                               sem("router_prefix"), sem("router_totals"))
        routed, rexp_in, xnorm, nmr_ready = sem("routed"), sem("rexp_in"), sem("xnorm"), sem("nmr_ready")
        scattered = sem("scattered")
        w1_ready, slot_free = sem("w1_ready"), sem("slot_free")
        xs_loaded = [sem(f"xs_loaded_{r}") for r in range(XSR)]
        t_ready, xt_hi, xt_ready = sem("t_ready"), sem("xt_hi"), sem("xt_ready")
        g_up, sgt_ready, h_ready = sem("g_up"), sem("sgt_ready"), sem("h_ready")
        th_ready, ht_hi, ht_ready = sem("th_ready"), sem("ht_hi"), sem("ht_ready")
        d_ready, y_out, y_stored = sem("d_ready"), sem("y_out"), [sem("y_stored_0"), sem("y_stored_1")]
        g_loaded = [sem(f"g_loaded_{r}") for r in range(GRING)]
        gs_ready, gt_ready = sem("gs_ready"), sem("gt_ready")
        f_ready, f_added, stored = sem("f_ready"), sem("f_added"), sem("stored")

        def behind(engine, signal, i):
            if not isinstance(i, int) or i >= 2:
                engine.wait_ge(signal, i - 1)

        def router_banks(t):
            return PS[:, RB[t % 2]:RB[t % 2] + 2, :].rearrange("p b (h n) -> p (b h) n", n=RC)

        def images_before(tokens):
            return -(-tokens // S)

        block = ctx.enter_context(nc.Block())

        @block.sync
        def _(sp):
            sp.dma_start(mats[:, :, :], c_mat).then_inc(consts, 16)

            def load_mix_weights(l):
                for dst, src in ((ind[:, :], c_ind), (peW[:, :, :], pe_W[l]), (inW[:, :, :], in_W[l]),
                                 (vinn[:, :, :], vec_inner[l]), (alog[:, :, :], a_log[l]),
                                 (xpW[:, :, :], xproj[l]), (dtW[:, :], dt_W[l]), (outW[:, :, :], out_W[l])):
                    sp.dma_start(dst, src).then_inc(mixw, 16)
                sp.dma_start(vhid[:, :, :], vec_hid[l:l + 1].broadcast_to((TT, 3, HID))).then_inc(mixw, 16)
                sp.dma_start(upS[:, :, :], c_up).then_inc(mixw, 16)

            def exchange(l):
                sp.wait_ge(bc_ready, l + 1)
                sp.dma_start(bc_dram[l], bc[:, :]).then_inc(bc_out, 16)
                sp.wait_ge(bc_out, l * 16 + 16)
                sp.wait_ge(p_ready, l * 2 + 2)
                sp.dma_start(Bb[:, :, :], bc_dram[l:l + 1].broadcast_to((P, 2 * NS, NT))).then_inc(bc_in, 16)

            for b in range(B):
                if b == 2:
                    load_mix_weights(0)
                sp.dma_start(X[:, :, b * S:(b + 1) * S], x[b].rearrange("(k p) s -> p k s", p=P))\
                    .then_inc(x_loaded[b // (B // XG)], 16)
            sp.wait_ge(dve, 2)
            exchange(0)
            zrow = xs_dram.rearrange("(m p z) c -> m p (z c)", z=ZT, p=P)
            with sp.Fori(0, MT // ZT) as m:
                sp.dma_start(zrow[ds(m, 1)].rearrange("m p (a c) -> p (m a) c", c=P),
                             zero[:, :].unsqueeze(1).broadcast_to((P, ZT * CH // P, P))).then_inc(filled, 16)
            sp.wait_ge(statT_ready, 1)
            sp.dma_start(stat_dram.rearrange("a e (j t) -> (a e j) t", t=P), statT[:, :]).then_inc(stats_out, 16)
            sp.wait_ge(stats_out, 16)
            with sp.Fori(0, E0) as e:
                for c in range(NC):
                    sp.wait_ge(rm_free, e * NC + c + 1)
                    sp.dma_start(rmb[:, :, :],
                                 stat_dram[:, ds(e, 1), c * CN:(c + 1) * CN].rearrange("a e n -> e a n")
                                 .broadcast_to((P, 2, CN))).then_inc(rm_loaded, 16)
            sp.wait_ge(dn_free, E0 * NC + 1)
            load_mix_weights(1)
            exchange(1)
            sp.wait_ge(y_ready, 2)
            sp.dma_start(rw, router).then_inc(upm, 16)
            sp.wait_ge(up_added, 2 * B + 2 * B)
            sp.wait_ge(g_ready, 2 + 2)
            sp.dma_start(rout[:, :], c_rout).then_inc(upm, 16)
            sp.wait_ge(scattered, 16 * 2 * TILES)
            xs_t = xs_dram.rearrange("(m p) c -> m p c", p=P)
            y_t = y_dram.rearrange("(m p) c -> m p c", p=P)

            def load(i, r):
                if not isinstance(i, int):
                    sp.wait_ge(t_ready, i - (XSR - 1))
                sp.dma_start(xs[:, r:r + 1, :], xs_t[i:i + 1].rearrange("m p c -> p m c") if isinstance(i, int)
                             else xs_t[ds(i, 1)].rearrange("m p c -> p m c")).then_inc(xs_loaded[r], 16)

            def store(i, r):
                sp.wait_ge(y_out, i + 1)
                sp.dma_start(y_t[ds(i, 1)].rearrange("m p c -> p m c"), ysb[:, r:r + 1, :]).then_inc(y_stored[r], 16)

            for i in range(XSR):
                load(i, i)
            with sp.Fori(0, MT // XSR - 1) as g:
                for r in range(XSR):
                    load(g * XSR + (r + XSR), r)
                    store(g * XSR + r, r % 2)
            for r in range(XSR):
                store(MT - XSR + r, r % 2)
            for b in range(B):
                sp.wait_ge(f_added, -(-S * (b + 1) // P))
                sp.dma_start(out[b].rearrange("(k p) s -> p k s", p=P), X[:, :, b * S:(b + 1) * S])\
                    .then_inc(stored, 16)
            sp.wait_ge(stored, 16 * B)

        @block.gpsimd
        def _(pool):
            def split(p, dst_h, dst_l):
                r = p % 2
                pool.wait_ge(raw_loaded[r], 16 * (p // 2 + 1))
                pool.tensor_copy(dst_h, raw[:, r, :]).then_inc(split_step, 1)
                pool.wait_ge(split_step, 2 * p + 1)
                pool.tensor_tensor(dst_l, raw[:, r, :], dst_h.bitcast(f32), ALU.subtract).then_inc(split_step, 1)
                pool.wait_ge(split_step, 2 * p + 2)
                if p + 2 < NP0 + NP1:
                    pool.dma_start(raw[:, r, :], w_ffn[p + 2]).then_inc(raw_loaded[r], 16)

            def scan_inputs(l):
                pool.wait_ge(du_ready, l + 1)
                pool.wait_ge(bc_in, l * 16 + 16)
                for j in range(JC):
                    if j >= 2:
                        pool.wait_ge(scanned, l * JC + j - 1)
                    pool.tensor_tensor(db[:, j % 2, :, :], du[:, j:j + 1, :].broadcast_to((P, NS, NT)),
                                       Bb[:, 0:NS, :], ALU.mult).then_inc(db_ready, 1)

            pool.dma_start(raw[:, 0, :], w_ffn[0]).then_inc(raw_loaded[0], 16)
            pool.dma_start(raw[:, 1, :], w_ffn[1]).then_inc(raw_loaded[1], 16)
            scan_inputs(0)
            pool.wait_ge(y_ready, 1)
            for e in range(E0):
                if e == 1:
                    pool.wait_ge(stats_out, 16)
                if e >= 2:
                    pool.wait_ge(dn_ready, (e - 1) * NC)
                for q in range(PE0):
                    p = e * PE0 + q
                    split(p, *(w0[e % 2][:, a, q * PIECE:(q + 1) * PIECE] for a in range(2)))
                pool.sem_inc(w0_ready, 1)
            scan_inputs(1)
            def split_expert(e):
                for q in range(PE1):
                    split(NP0 + e * PE1 + q, *(w1[:, 1 - e % 2, a, 2 * q:2 * q + 2, :].rearrange("p k n -> p (k n)")
                                               for a in range(2)))
                pool.sem_inc(w1_ready, 1)

            pool.wait_ge(y_ready, 2)
            split_expert(0)
            pool.wait_ge(routed, 2)
            pool.wait_ge(filled, 16 * (MT // ZT))
            for t in range(TILES):
                pool.wait_ge(xnorm, t + 1)
                for k in range(2):
                    pool.indirect_dma_start(
                        xs_dram, bass.IndirectOffsetOnAxis(ap=pos[:, k, t:t + 1], axis=0), XN[:, t, :], None)\
                        .then_inc(scattered, 16)
            pool.wait_ge(scattered, 16 * 2 * TILES)
            for e in range(1, E1):
                if e >= 2:
                    end = pool.value_load(tile_end[0:1, e - 2:e - 1], min_val=1, max_val=MT)
                    pool.wait_ge(d_ready, end)
                    pool.sem_inc(slot_free, 1)
                split_expert(e)
            for r in range(2):
                pool.wait_ge(y_stored[r], 16 * (MT // 2))
            for t in range(TILES):
                if t >= GRING:
                    pool.wait_ge(gt_ready, t - GRING + 1)
                for k, g in enumerate((g1, g2)):
                    pool.indirect_dma_start(
                        g[:, t % GRING, :], None, y_dram, bass.IndirectOffsetOnAxis(ap=pos[:, k, t:t + 1], axis=0))\
                        .then_inc(g_loaded[t % GRING], 16)

        @block.tensor
        def _(pe):
            def pool_patches(l, g):
                pe.wait_ge(ri_ready, l * 2 * NG + 2 * (g + 1))
                for t in range(g * GR, (g + 1) * GR):
                    for k in range(KC):
                        pe.matmul(PS[:, 4 + k // 2, (k % 2) * NT + 3 * t:(k % 2) * NT + 3 * t + 3],
                                  xtok[:, t % XR, k * P:(k + 1) * P], RI[:, t, :], start=True, stop=True)
                pe.matmul(PS[:, 3, 3 * g * GR:3 * (g + 1) * GR], ones[0:ROWT, :],
                          RM[:, g * GR:(g + 1) * GR, :].rearrange("p t a -> p (t a)"), start=True, stop=True)\
                    .then_inc(pooled, 1)

            def patches(l):
                for g in range(NG):
                    for t in range(g * GR, (g + 1) * GR):
                        if l == 0:
                            if t % (NROW // XG) == 0:
                                pe.wait_ge(x_loaded[t // (NROW // XG)], 16 * (B // XG))
                        elif t == 0:
                            pe.wait_ge(dn_free, E0 * NC + 1)
                        if t >= 3:
                            pe.wait_ge(xtok_ready, l * NROW + t - 2)
                        for k in range(KC):
                            last = pe.transpose(PS[0:ROWT, t % 3, k * P:(k + 1) * P],
                                                X[:, k, t * ROWT:(t + 1) * ROWT], ident)
                        last.then_inc(tp_ready, 1)
                    if g >= 2:
                        pool_patches(l, g - 2)
                pool_patches(l, NG - 2)
                pool_patches(l, NG - 1)

            def mixer(l):
                pe.wait_ge(mixw, l * 160 + 160)
                pe.wait_ge(p_ready, l * 2 + 2)
                for tt in range(2):
                    for k in range(KC):
                        last = pe.matmul(PS[0:TT, tt, 0:HID], pT[:, k, tt * TT:(tt + 1) * TT], peW[:, k, :],
                                         start=k == 0, stop=k == KC - 1)
                last.then_inc(tok_ready, 1)
                pe.wait_ge(tk_ready, l + 1)
                for tt in range(2):
                    for h in range(2):
                        last = pe.transpose(PS[0:HH, 2, h * NT + tt * TT:h * NT + (tt + 1) * TT],
                                            tk[:, tt, h * HH:(h + 1) * HH], ident[0:TT, 0:TT])
                last.then_inc(tkT, 1)
                pe.wait_ge(tT_ready, l + 1)
                pe.wait_ge(mterm_ready, l + 1)
                pe.wait_ge(p_ready, l * 2 + 2)
                for m in range(2 * JC):
                    for h in range(2):
                        last = pe.matmul(PS[:, 3 + m // JC, (m % JC) * NT:(m % JC + 1) * NT],
                                         inW[:, h, m * P:(m + 1) * P], tT[:, h, :], start=h == 0, stop=h == 1)
                    if m % JC == JC - 1:
                        last.then_inc(xz_ready, 1)
                pe.wait_ge(u_ready, l + 1)
                for j in range(JC):
                    last = pe.matmul(PS[0:2 * NS, 5, 0:NT], xpW[:, j, RANK:], uu[:, j, :],
                                     start=j == 0, stop=j == JC - 1)
                last.then_inc(dbc_ready, 1)
                for j in range(JC):
                    last = pe.matmul(PS[0:RANK, 6, 0:NT], xpW[:, j, 0:RANK], uu[:, j, :],
                                     start=j == 0, stop=j == JC - 1)
                last.then_inc(dbc_ready, 1)
                pe.wait_ge(dl_ready, l + 1)
                for j in range(JC):
                    last = pe.matmul(PS[:, 7, j * NT:(j + 1) * NT], dtW[:, j * P:(j + 1) * P], dl[:, :],
                                     start=True, stop=True)
                last.then_inc(dt_ready, 1)
                for j in range(JC):
                    pe.wait_ge(hc_ready, l * JC + j + 1)
                    for n in range(NS):
                        last = pe.matmul(PS[:, 2, j * NT:(j + 1) * NT], ident, a1[:, j % 2, n, :],
                                         start=n == 0, stop=n == NS - 1)
                    last.then_inc(ysum, 1)
                pe.wait_ge(y_ready, l + 1)
                for tt in range(2):
                    for j in range(JC):
                        last = pe.matmul(PS[0:TT, tt, :], yy[:, j, tt * TT:(tt + 1) * TT], outW[:, j, :],
                                         start=j == 0, stop=j == JC - 1)
                last.then_inc(og_ready, 1)

            def upsample(l, b):
                for half in range(2):
                    if b:
                        pe.wait_ge(up_added, l * 2 * B + 2 * (b - 1) + half + 1)
                    for k in (2 * half, 2 * half + 1):
                        for g, first in ((gH, True), (gL, False)):
                            last = pe.matmul(PS[:, 2 + k, 0:S], g[:, b // IB, k * P:(k + 1) * P],
                                             upM[:, b % IB, :], start=first, stop=not first)
                    last.then_inc(up_ready, 1)

            def tile_transposes(l, q, view):
                if q >= len(TB):
                    pe.wait_ge(lt_free, l * TILES + q - len(TB) + 1)
                for k in range(KC):
                    last = pe.transpose(PS[:, TB[q % len(TB)], k * P:(k + 1) * P], view(k), ident)
                last.then_inc(lt_ready, 1)

            pe.wait_ge(consts, 16)
            patches(0)
            mixer(0)
            pe.wait_ge(g_ready, 2)
            q = 0
            for b in range(B):
                upsample(0, b)
                while q < TILES and images_before(E0 * P * (q // E0 + 1)) <= b:
                    pe.wait_ge(up_added, 2 * images_before(E0 * P * (q // E0 + 1)))
                    tile_transposes(0, q, lambda k: Xe[:, k, q % E0, (q // E0) * P:(q // E0 + 1) * P])
                    q += 1
            while q < TILES:
                pe.wait_ge(up_added, 2 * images_before(E0 * P * (q // E0 + 1)))
                tile_transposes(0, q, lambda k: Xe[:, k, q % E0, (q // E0) * P:(q // E0 + 1) * P])
                q += 1
            pe.wait_ge(mr_ready, 2)
            pe.transpose(PS[0:2 * TILES, 2, 0:P], MR[:, :], ident).then_inc(mrT, 1)

            def three(out_ap, wl, wh, xl, xh, start, stop):
                pe.matmul(out_ap, wh, xh, start=start, stop=False)
                pe.matmul(out_ap, wl, xh, start=False, stop=False)
                return pe.matmul(out_ap, wh, xl, start=False, stop=stop)

            pe.wait_ge(statT_ready, 1)
            with pe.Fori(0, E0 // 2) as ee:
                for s in range(2):
                    with pe.Fori(0, NC) as c:
                        n = ee * (2 * NC) + c + s * NC
                        pe.wait_ge(w0_ready, ee * 2 + s + 1)
                        pe.wait_ge(xn_ready, n + 1)
                        for m in range(KC):
                            pe.wait_ge(gu_free, n * KC + m + 1)
                            for u in range(2):
                                for k in range(KC):
                                    o = k * 2 * I0 + u * I0 + m * P
                                    last = three(PS[:, 2 * (m % 2) + u, 0:CN], w0[s][:, 1, o:o + P],
                                                 w0[s][:, 0, o:o + P], xnL[:, k, :], xnH[:, k, :],
                                                 k == 0, k == KC - 1)
                            last.then_inc(gu_ready, 1)
                        pe.wait_ge(dn_free, n + 1)
                        for k in range(KC):
                            pe.wait_ge(it_ready, n * KC + k + 1)
                            for h in range(KC):
                                o = KC * 2 * I0 + k * CH + h * P
                                last = three(PS[:, 4 + h, 0:CN], w0[s][:, 1, o:o + P], w0[s][:, 0, o:o + P],
                                             itL[:, k, :], itH[:, k, :], k == 0, k == KC - 1)
                        last.then_inc(dn_ready, 1)

            patches(1)
            mixer(1)
            pe.wait_ge(upm, 16)
            pe.wait_ge(gh_ready, 1 + 1)
            pe.wait_ge(g_ready, 2 + 2)
            for k in range(KC):
                last = pe.matmul(PS[:, 1, 0:E1], ones, rw[:, k, :], start=k == 0, stop=k == KC - 1)
            last.then_inc(wb_ready, 1)
            pe.wait_ge(rw_ready, 1)
            pe.wait_ge(g_ready, 2 + 2)

            def router_tile(t):
                pe.wait_ge(up_added, 2 * B + 2 * images_before(P * (t + 1)))
                if t >= 2:
                    pe.wait_ge(logits_ready, t - 1)
                for k in range(KC):
                    at = k % 2 * RC
                    last = pe.matmul(PS[:, RB[t % 2] + k // 2, at:at + P + E1], X[:, k, t * P:(t + 1) * P],
                                     eyeR[:, k, :], start=True, stop=True)
                last.then_inc(lt_ready, 1)

            t = 0
            for b in range(B):
                upsample(1, b)
                while t < TILES and images_before(P * (t + 1)) <= b:
                    router_tile(t)
                    t += 1
            while t < TILES:
                router_tile(t)
                t += 1
            pe.wait_ge(r_O, 1)
            O = R["O"][:, :, :].rearrange("p t e -> p (t e)")
            pe.matmul(PS[:, 2, 0:TILES * E1], triu, O, start=True, stop=True).then_inc(r_pre, 1)
            pe.matmul(PS[:, 3, 0:TILES * E1], ones, O, start=True, stop=True).then_inc(r_pre, 1)
            pe.wait_ge(routed, 2)

            def transposes(i, turn, r, s):
                pe.wait_ge(xs_loaded[r], 16 * turn + 16)
                behind(pe, xt_ready, i)
                for k in range(KC):
                    last = pe.transpose(PS[:, s, k * P:(k + 1) * P], xs[:, r, k * P:(k + 1) * P], ident)
                last.then_inc(t_ready, 1)

            def slot_of(i):
                e = pe.value_load(tile_expert[0:1, i:i + 1] if isinstance(i, int) else tile_expert[0:1, ds(i, 1)],
                                  min_val=0, max_val=E1 - 1)
                return e, (e + 1) % 2

            def gate_up(i, s, slot, ks):
                for k in ks:
                    wh = w1[:, ds(slot, 1), 0, k, :]
                    wl = w1[:, ds(slot, 1), 1, k, :]
                    pe.matmul(PS[:, 2 + s, :], xtH[:, s, k, :], wh, start=k == 0, stop=False)
                    pe.matmul(PS[:, 2 + s, :], xtL[:, s, k, :], wh, start=False, stop=False)
                    last = pe.matmul(PS[:, 2 + s, :], xtH[:, s, k, :], wl, start=False, stop=k == KC - 1)
                return last

            def hidden_transposes(i, s):
                pe.wait_ge(h_ready, i + 1)
                behind(pe, ht_ready, i)
                for k in range(2):
                    last = pe.transpose(PS[:, 4 + s, k * P:(k + 1) * P], hh[:, s, k * P:(k + 1) * P], ident)
                last.then_inc(th_ready, 1)

            def down(i, s, slot):
                pe.wait_ge(ht_ready, i + 1)
                behind(pe, y_out, i)
                for k in range(2):
                    wh = w1[:, ds(slot, 1), 0, KC + k, :]
                    wl = w1[:, ds(slot, 1), 1, KC + k, :]
                    pe.matmul(PS[:, 6 + s, :], htH[:, s, k, :], wh, start=k == 0, stop=False)
                    pe.matmul(PS[:, 6 + s, :], htL[:, s, k, :], wh, start=False, stop=False)
                    last = pe.matmul(PS[:, 6 + s, :], htH[:, s, k, :], wl, start=False, stop=k == 1)
                last.then_inc(d_ready, 1)

            def step(i, s, r_next, turn_next, first=False, last=False):
                if not last:
                    transposes(i + 1, turn_next, r_next, 1 - s)
                e, slot = slot_of(i)
                pe.wait_ge(w1_ready, e + 1)
                pe.wait_ge(xt_ready, i + 1)
                behind(pe, h_ready, i)
                gate_up(i, s, slot, (0, 1))
                if not first:
                    hidden_transposes(i - 1, 1 - s)
                gate_up(i, s, slot, (2, 3)).then_inc(g_up, 1)
                if not first:
                    _, before = slot_of(i - 1)
                    down(i - 1, 1 - s, before)

            transposes(0, 0, 0, 0)
            step(0, 0, 1, 0, first=True)
            for i in (1, 2, 3):
                step(i, i % 2, (i + 1) % XSR, (i + 1) // XSR)
            with pe.Fori(1, MT // XSR - 1) as g:
                for r in range(XSR):
                    step(g * XSR + r, r % 2, (r + 1) % XSR, g + (r + 1) // XSR)
            for i in range(MT - XSR, MT):
                step(i, i % 2, (i + 1) % XSR, (i + 1) // XSR, last=i == MT - 1)
            hidden_transposes(MT - 1, 1)
            down(MT - 1, 1, slot_of(MT - 1)[1])

            for t in range(TILES):
                pe.wait_ge(gt_ready, t + 1)
                if t >= 4:
                    pe.wait_ge(f_added, t - 3)
                for k in range(KC):
                    last = pe.transpose(PS[:, t % 4, k * P:(k + 1) * P], gt[:, t % 2, k * P:(k + 1) * P], ident)
                last.then_inc(f_ready, 1)

        @block.scalar
        def _(act):
            def patch_sd(l, g):
                act.wait_ge(mv_done, l * NROW + GR * (g + 1))
                act.activation(SD[0:ROWT, g * GR:(g + 1) * GR], MV[0:ROWT, g * GR:(g + 1) * GR, 1], ACT.Sqrt,
                               bias=eps[0:ROWT, 0:1]).then_inc(sd_ready, 1)

            def patches(l):
                for g in range(NG):
                    for t in range(g * GR, (g + 1) * GR):
                        act.wait_ge(tp_ready, l * NROW + t + 1)
                        if t >= XR and t % GR == 0:
                            act.wait_ge(pooled, l * NG + g - 2)
                        act.activation(xtok[:, t % XR, :], PS[0:ROWT, t % 3, :], ACT.Copy).then_inc(xtok_ready, 1)
                    if g:
                        patch_sd(l, g - 1)
                patch_sd(l, NG - 1)
                act.wait_ge(pooled, l * NG + NG)
                act.activation(mterm[:, :], PS[:, 3, 0:NT], ACT.Copy).then_inc(mterm_ready, 1)

            def mixer(l):
                act.wait_ge(var_h, l * 2 + 2)
                act.activation(sdh[:, :], mvh[:, :, 1], ACT.Sqrt, bias=eps[0:TT, 1:2]).then_inc(sd_h, 1)
                act.wait_ge(tkT, l + 1)
                act.activation(tT[:, :, :], PS[0:HH, 2, 0:2 * NT].rearrange("p (h t) -> p h t", h=2), ACT.Copy)\
                    .then_inc(tT_ready, 1)
                act.wait_ge(acc_ready, l + 1)
                act.activation(uu[:, :, :], acc[:, :, :], ACT.Silu).then_inc(u_ready, 1)
                act.wait_ge(xz_ready, l * 2 + 2)
                act.activation(sz[:, :, :], PS[:, 4, 0:JC * NT].rearrange("p (j t) -> p j t", j=JC), ACT.Silu)\
                    .then_inc(z_ready, 1)
                act.wait_ge(mixw, l * 160 + 160)
                act.activation(negA[:, :, :], alog[:, :, :], ACT.Exp).then_inc(ea_ready, 1)
                act.wait_ge(ab_ready, l + 1)
                act.activation(ab[:, :, :], ab[:, :, :], ACT.Exp, scale=-1.0).then_inc(ex_done, 1)
                act.wait_ge(ex_done, l * 2 + 1)
                act.activation(ab[:, :, :], ab[:, :, :], ACT.Ln, bias=1.0).then_inc(ex_done, 1)
                act.wait_ge(na_ready, l + 1)
                act.wait_ge(sp_ready, l + 1)
                act.wait_ge(a1_zero, l + 1)
                for j in range(JC):
                    if j >= 2:
                        act.wait_ge(ysum, l * JC + j - 1)
                    for n in range(NS):
                        last = act.activation(a1[:, j % 2, n, :].rearrange("p (b t) -> p b t", t=L)[:, :, 1:],
                                              delta[:, j, :].rearrange("p (b t) -> p b t", t=L)[:, :, 1:],
                                              ACT.Identity, scale=negA[:, j, n:n + 1], bias=1.0)
                    last.then_inc(a1_ready, 1)
                act.wait_ge(og_ready, l + 1)
                act.activation(gH[:, :, :], PS[0:TT, 0:2, :], ACT.Copy).then_inc(gh_ready, 1)

            patches(0)
            mixer(0)
            act.wait_ge(lmv_done, TILES)
            act.activation(SD[:, 0:TILES], MV[:, 0:TILES, 1], ACT.Sqrt, bias=eps[:, 1:2]).then_inc(lsd_ready, 1)
            act.wait_ge(mrT, 1)
            act.activation(statT[:, :], PS[0:2 * TILES, 2, 0:P], ACT.Copy).then_inc(statT_ready, 1)
            act.wait_ge(statT_ready, 1)
            act.wait_ge(stats_out, 16)

            with act.Fori(0, E0 * NC) as n:
                for m in range(KC):
                    act.wait_ge(gu_ready, n * KC + m + 1)
                    act.wait_ge(sg_free, n * KC + m + 1)
                    act.activation(sg[:, m % 2, :], PS[:, 2 * (m % 2), 0:CN], ACT.Silu).then_inc(sg_ready, 1)

            patches(1)
            mixer(1)
            act.wait_ge(wb_ready, 1)
            act.activation(wbar[:, :], PS[:, 1, 0:E1], ACT.Copy, scale=1.0 / CH).then_inc(wb_sb, 1)
            act.wait_ge(g_ready, 2 + 2)
            for t in range(TILES):
                act.wait_ge(lt_ready, TILES + t + 1)
                act.activation(XN[:, t, :].rearrange("p (k n) -> p k n", n=P), router_banks(t)[:, :, 0:P], ACT.Copy)\
                    .then_inc(lt_free, 1)
            act.wait_ge(lmv_done, TILES + TILES)
            act.activation(SD[:, 0:TILES], MV[:, 0:TILES, 1], ACT.Sqrt, bias=eps[:, 1:2]).then_inc(lsd_ready, 1)
            act.wait_ge(rexp_in, 1)
            act.activation(R["e"][:, :, :], R["t"][:, :, :], ACT.Exp).then_inc(r_e, 1)
            act.wait_ge(r_pre, 2)
            act.activation(scT["tot"][:, :, :], PS[:, 3, 0:TILES * E1].rearrange("p (t e) -> p e t", e=E1), ACT.Copy)\
                .then_inc(r_tot, 1)
            act.wait_ge(nmr_ready, 1)
            for t in range(TILES):
                act.activation(XN[:, t, :], XN[:, t, :], ACT.Identity, scale=RS[:, t:t + 1], bias=nmr[:, t:t + 1])\
                    .then_inc(xnorm, 1)

            def x_hi(i, s):
                act.wait_ge(t_ready, i + 1)
                behind(act, g_up, i)
                act.activation(xtH[:, s, :, :], PS[:, s, :].rearrange("p (k n) -> p k n", n=P), ACT.Copy)\
                    .then_inc(xt_hi, 1)

            def silu(i, s):
                act.wait_ge(g_up, i + 1)
                behind(act, h_ready, i)
                act.activation(sgt[:, s, :], PS[:, 2 + s, 0:512:2], ACT.Silu).then_inc(sgt_ready, 1)

            def h_hi(i, s):
                act.wait_ge(th_ready, i + 1)
                behind(act, d_ready, i)
                act.activation(htH[:, s, :, :], PS[:, 4 + s, 0:2 * P].rearrange("p (k n) -> p k n", n=P), ACT.Copy)\
                    .then_inc(ht_hi, 1)

            def y_copy(i, s, turn):
                act.wait_ge(d_ready, i + 1)
                if turn is not None:
                    act.wait_ge(y_stored[s], turn * 16)
                act.activation(ysb[:, s, :], PS[:, 6 + s, :], ACT.Copy).then_inc(y_out, 1)

            def step(i, s, turn, first=False, last=False):
                if not last:
                    x_hi(i + 1, 1 - s)
                if not first:
                    h_hi(i - 1, 1 - s)
                silu(i, s)
                if not first:
                    y_copy(i - 1, 1 - s, turn)

            act.wait_ge(scattered, 16 * 2 * TILES)
            x_hi(0, 0)
            step(0, 0, None, first=True)
            step(1, 1, None)
            step(2, 0, None)
            step(3, 1, 1)
            with act.Fori(2, MT // 2 - 1) as g:
                step(g * 2, 0, g - 1)
                step(g * 2 + 1, 1, g)
            step(MT - 2, 0, MT // 2 - 2)
            step(MT - 1, 1, MT // 2 - 1, last=True)
            h_hi(MT - 1, 1)
            y_copy(MT - 1, 1, MT // 2 - 1)

            for t in range(TILES):
                act.wait_ge(g_loaded[t % GRING], 32 * (t // GRING + 1))
                if t >= 2:
                    act.wait_ge(gt_ready, t - 1)
                act.activation(gs[:, t % 2, :], g1[:, t % GRING, :], ACT.Copy, scale=score[:, 0, t:t + 1])\
                    .then_inc(gs_ready, 1)

        @block.vector
        def _(v):
            steps = [0]

            def link(ins):
                steps[0] += 1
                ins.then_inc(dve, 1)
                v.wait_ge(dve, steps[0])

            def count(ins):
                steps[0] += 1
                return ins.then_inc(dve, 1)

            link(v.memset(zero[:, :], 0.0))
            link(v.memset(eps[:, 0:1], 1e-6))
            link(v.memset(eps[:, 1:2], 1e-5))

            def patch_weights(l, g):
                sl = slice(g * GR, (g + 1) * GR)
                v.wait_ge(mv_done, l * NROW + (g + 1) * GR)
                v.wait_ge(sd_ready, l * NG + g + 1)
                link(v.reciprocal(RS[0:ROWT, sl], SD[0:ROWT, sl]))
                ins = v.tensor_tensor(RI[:, sl, :], RS[0:ROWT, sl].unsqueeze(2).broadcast_to((ROWT, GR, 3)),
                                      ind[:, :].unsqueeze(1).broadcast_to((ROWT, GR, 3)), ALU.mult)
                ins.then_inc(ri_ready, 1)
                v.wait_ge(ri_ready, l * 2 * NG + 2 * g + 1)
                v.tensor_tensor(RM[:, sl, :], RI[:, sl, :],
                                MV[0:ROWT, sl, 0].unsqueeze(2).broadcast_to((ROWT, GR, 3)), ALU.mult)\
                    .then_inc(ri_ready, 1)

            def patches(l):
                v.wait_ge(mixw, l * 160 + 160)
                v.tensor_copy(upM[:, :, :], upS[:, :, :]).then_inc(g_ready, 1)
                for g in range(NG):
                    for t in range(g * GR, (g + 1) * GR):
                        v.wait_ge(xtok_ready, l * NROW + t + 1)
                        v.bn_stats(ST6[0:ROWT, g % 2, t % GR, :], xtok[:, t % XR, :]).then_inc(st_done, 1)
                    v.wait_ge(st_done, l * NROW + (g + 1) * GR)
                    for t in range(g * GR, (g + 1) * GR):
                        v.bn_aggr(MV[0:ROWT, t, :], ST6[0:ROWT, g % 2, t % GR, :]).then_inc(mv_done, 1)
                    if g:
                        patch_weights(l, g - 1)
                patch_weights(l, NG - 1)
                v.wait_ge(mterm_ready, l + 1)
                for a in range(2):
                    v.tensor_tensor(pT[:, 2 * a:2 * a + 2, :],
                                    PS[:, 4 + a, 0:2 * NT].rearrange("p (k t) -> p k t", k=2),
                                    mterm[:, :].unsqueeze(1).broadcast_to((P, 2, NT)), ALU.subtract)\
                        .then_inc(p_ready, 1)

            def mixer(l):
                v.wait_ge(tok_ready, l + 1)
                link(v.tensor_tensor(tk[:, :, :], PS[0:TT, 0:2, 0:HID],
                                     vhid[:, 0:1, :].broadcast_to((TT, 2, HID)), ALU.add))
                for tt in range(2):
                    link(v.bn_stats(sth[:, tt, :], tk[:, tt, :]))
                    v.bn_aggr(mvh[:, tt, :], sth[:, tt, :]).then_inc(var_h, 1)
                v.wait_ge(var_h, l * 2 + 2)
                v.wait_ge(sd_h, l + 1)
                link(v.reciprocal(rsh[:, :], sdh[:, :]))
                for tt in range(2):
                    link(v.tensor_scalar(tk[:, tt, :], tk[:, tt, :], mvh[:, tt, 0:1], rsh[:, tt:tt + 1],
                                         ALU.subtract, ALU.mult))
                link(v.tensor_tensor(tk[:, :, :], tk[:, :, :], vhid[:, 1:2, :].broadcast_to((TT, 2, HID)), ALU.mult))
                v.tensor_tensor(tk[:, :, :], tk[:, :, :], vhid[:, 2:3, :].broadcast_to((TT, 2, HID)), ALU.add)\
                    .then_inc(tk_ready, 1)
                forget = lambda s: a1[:, s, :, :].rearrange("p n (b t) -> p (n b) t", t=L)[:, :, 0:1]
                link(v.memset(forget(0), 0.0))
                v.memset(forget(1), 0.0).then_inc(a1_zero, 1)
                v.wait_ge(xz_ready, l * 2 + 1)
                img = lambda ap: ap.rearrange("p (b t) -> p b t", t=L)
                for j in range(JC):
                    src = PS[:, 3, j * NT:(j + 1) * NT]
                    link(v.tensor_scalar(acc[:, j, :], src, vinn[:, j, 1:2], vinn[:, j, 3:4], ALU.mult, ALU.add))
                    link(v.scalar_tensor_tensor(img(acc[:, j, :])[:, :, 1:], img(src)[:, :, :L - 1], vinn[:, j, 0:1],
                                                img(acc[:, j, :])[:, :, 1:], ALU.mult, ALU.add))
                    last = v.scalar_tensor_tensor(img(acc[:, j, :])[:, :, :L - 1], img(src)[:, :, 1:], vinn[:, j, 2:3],
                                                  img(acc[:, j, :])[:, :, :L - 1], ALU.mult, ALU.add)
                    if j < JC - 1:
                        link(last)
                last.then_inc(acc_ready, 1)
                v.wait_ge(dbc_ready, l * 2 + 1)
                v.tensor_copy(bc[:, :], PS[0:2 * NS, 5, 0:NT]).then_inc(bc_ready, 1)
                v.wait_ge(dbc_ready, l * 2 + 2)
                v.tensor_copy(dl[:, :], PS[0:RANK, 6, 0:NT]).then_inc(dl_ready, 1)
                v.wait_ge(ea_ready, l + 1)
                v.tensor_scalar(negA[:, :, :], negA[:, :, :], -1.0, None, ALU.mult).then_inc(na_ready, 1)
                v.wait_ge(dt_ready, l + 1)
                for j in range(JC):
                    link(v.tensor_scalar(dx[:, j, :], PS[:, 7, j * NT:(j + 1) * NT], vinn[:, j, 4:5], None, ALU.add))
                v.scalar_tensor_tensor(ab[:, :, :], dx[:, :, :], -1.0, dx[:, :, :], ALU.mult, ALU.max)\
                    .then_inc(ab_ready, 1)
                v.wait_ge(ex_done, l * 2 + 2)
                v.scalar_tensor_tensor(delta[:, :, :], dx[:, :, :], 0.0, ab[:, :, :], ALU.max, ALU.add)\
                    .then_inc(sp_ready, 1)
                v.wait_ge(sp_ready, l + 1)
                v.wait_ge(u_ready, l + 1)
                v.tensor_tensor(du[:, :, :], delta[:, :, :], uu[:, :, :], ALU.mult).then_inc(du_ready, 1)
                v.wait_ge(bc_in, l * 16 + 16)
                v.wait_ge(a1_zero, l + 1)
                flat = lambda ap: ap.rearrange("p n t -> p (n t)")
                for j in range(JC):
                    if j >= 2:
                        v.wait_ge(ysum, l * JC + j - 1)
                        link(v.memset(forget(j % 2), 0.0))
                    v.wait_ge(a1_ready, l * JC + j + 1)
                    v.wait_ge(db_ready, l * JC + j + 1)
                    if j >= 1:
                        v.wait_ge(hc_ready, l * JC + j)
                    v.tensor_tensor_scan(flat(hs[:, :, :]), flat(a1[:, j % 2, :, :]), flat(db[:, j % 2, :, :]), 0.0,
                                         ALU.mult, ALU.add).then_inc(scanned, 1)
                    v.wait_ge(scanned, l * JC + j + 1)
                    v.tensor_tensor(a1[:, j % 2, :, :], hs[:, :, :], Bb[:, NS:, :], ALU.mult).then_inc(hc_ready, 1)
                v.wait_ge(hc_ready, (l + 1) * JC)
                v.wait_ge(ysum, (l + 1) * JC)
                for j in range(JC):
                    link(v.scalar_tensor_tensor(yy[:, j, :], uu[:, j, :], vinn[:, j, 5:6],
                                                PS[:, 2, j * NT:(j + 1) * NT], ALU.mult, ALU.add))
                v.wait_ge(z_ready, l + 1)
                v.tensor_tensor(yy[:, :, :], yy[:, :, :], sz[:, :, :], ALU.mult).then_inc(y_ready, 1)
                v.wait_ge(gh_ready, l + 1)
                v.tensor_tensor(gL[:, :, :], PS[0:TT, 0:2, :], gH[:, :, :].bitcast(f32), ALU.subtract)\
                    .then_inc(g_ready, 1)
                v.wait_ge(g_ready, l * 2 + 2)

            def add_upsampled(l, b):
                for half in range(2):
                    v.wait_ge(up_ready, l * 2 * B + 2 * b + half + 1)
                    dst = X[:, 2 * half:2 * half + 2, b * S:(b + 1) * S]
                    v.tensor_tensor(dst, dst, PS[:, 2 + 2 * half:4 + 2 * half, 0:S], ALU.add).then_inc(up_added, 1)

            def token_stats(l, q, src, at, read):
                v.bn_stats(ST6[:, (q // GR) % 2, q % GR, :], src).then_inc(read, 1)
                if q % GR == GR - 1:
                    v.wait_ge(read, q + 1)
                    for i in range(q + 1 - GR, q + 1):
                        v.bn_aggr(MV[:, at(i), :], ST6[:, (i // GR) % 2, i % GR, :]).then_inc(lmv_done, 1)

            def first_stats(q):
                v.wait_ge(lt_ready, q + 1)
                token_stats(0, q, PS[:, TB[q % len(TB)], :], lambda i: (i % E0) * EJ + i // E0, lt_free)

            patches(0)
            mixer(0)
            q = 0
            for b in range(B):
                add_upsampled(0, b)
                while q < TILES and images_before(E0 * P * (q // E0 + 1)) <= b:
                    first_stats(q)
                    q += 1
            while q < TILES:
                first_stats(q)
                q += 1
            v.wait_ge(lmv_done, TILES)
            v.wait_ge(lsd_ready, 1)
            v.reciprocal(MR[:, 0:TILES], SD[:, 0:TILES]).then_inc(mr_ready, 1)
            v.wait_ge(mr_ready, 1)
            v.tensor_tensor(MR[:, TILES:], MR[:, 0:TILES], MV[:, 0:TILES, 0], ALU.mult).then_inc(mr_ready, 1)

            v.wait_ge(stats_out, 16)
            for free, n in ((gu_free, 2), (sg_free, 2), (rm_free, 1), (dn_free, 1)):
                v.sem_inc(free, n)

            def normalise(n, r):
                v.wait_ge(rm_loaded, n * 16 + 16)
                e, c = n // NC, n % NC
                src = Xe[:, :, ds(e, 1), ds(c * CN, CN)].rearrange("p k e n -> p k (e n)") \
                    if not isinstance(n, int) else Xe[:, :, e, c * CN:(c + 1) * CN]
                v.tensor_tensor(xr[:, :, :], src, rmb[:, 0:1, :].broadcast_to((P, KC, CN)), ALU.mult)\
                    .then_inc(xr_done, 1)
                v.wait_ge(xr_done, n * 2 + 1)
                v.tensor_tensor(xr[:, :, :], xr[:, :, :], rmb[:, 1:2, :].broadcast_to((P, KC, CN)), ALU.subtract)\
                    .then_inc(xr_done, 1)
                v.wait_ge(xr_done, n * 2 + 2)
                v.sem_inc(rm_free, 1)
                if not isinstance(n, int) or n:
                    v.wait_ge(gu_ready, n * KC)
                v.tensor_copy(xnH[:, :, :], xr[:, :, :]).then_inc(it_step, 1)
                v.wait_ge(it_step, n * (2 * KC + 1) + 1)
                v.tensor_tensor(xnL[:, :, :], xr[:, :, :], xnH[:, :, :].bitcast(f32), ALU.subtract)\
                    .then_inc(xn_ready, 1)
                v.wait_ge(xn_ready, n + 1)

            def chunk(n, r, last=False):
                e, c = n // NC, n % NC
                for m in range(KC):
                    v.wait_ge(sg_ready, n * KC + m + 1)
                    v.tensor_tensor(sg[:, m % 2, :], sg[:, m % 2, :], PS[:, 2 * (m % 2) + 1, 0:CN], ALU.mult)\
                        .then_inc(gu_free, 1)
                    v.wait_ge(gu_free, n * KC + m + 3)
                    v.tensor_copy(itH[:, m, :], sg[:, m % 2, :]).then_inc(it_step, 1)
                    v.wait_ge(it_step, n * (2 * KC + 1) + (2 * m + 2))
                    v.tensor_tensor(itL[:, m, :], sg[:, m % 2, :], itH[:, m, :].bitcast(f32), ALU.subtract)\
                        .then_inc(it_step, 1)
                    v.wait_ge(it_step, n * (2 * KC + 1) + (2 * m + 3))
                    v.sem_inc(it_ready, 1)
                    v.sem_inc(sg_free, 1)
                if not last:
                    normalise(n + 1, 1 - r)
                v.wait_ge(dn_ready, n + 1)
                dst = Xe[:, :, ds(e, 1), ds(c * CN, CN)].rearrange("p k e n -> p k (e n)") \
                    if not isinstance(n, int) else Xe[:, :, e, c * CN:(c + 1) * CN]
                v.tensor_tensor(dst, dst, PS[:, 4:8, 0:CN], ALU.add).then_inc(dn_free, 1)

            normalise(0, 0)
            with v.Fori(0, E0 * NC // 2 - 1) as nn:
                for r in range(2):
                    chunk(nn * 2 + r, r)
            chunk(E0 * NC - 2, 0)
            chunk(E0 * NC - 1, 1, last=True)
            v.wait_ge(dn_free, E0 * NC + 1)

            patches(1)
            mixer(1)
            v.wait_ge(wb_sb, 1)
            v.wait_ge(upm, 16)
            link(v.tensor_copy(eyeR[:, :, 0:P], ident.unsqueeze(1).broadcast_to((P, KC, P))))
            v.tensor_tensor(rw, rw, wbar[:, :].unsqueeze(1).broadcast_to((P, KC, E1)), ALU.subtract)\
                .then_inc(rw_ready, 1)
            def router_tile(t):
                v.wait_ge(lt_free, TILES + t + 1)
                v.tensor_reduce(logits[:, t, :], router_banks(t)[:, :, P:P + E1].rearrange("p k e -> p e k"), AX.X,
                                ALU.add).then_inc(logits_ready, 1)
                token_stats(1, t, XN[:, t, :], lambda i: i, lst_done)

            t = 0
            for b in range(B):
                add_upsampled(1, b)
                while t < TILES and images_before(P * (t + 1)) <= b:
                    router_tile(t)
                    t += 1
            while t < TILES:
                router_tile(t)
                t += 1
            v.wait_ge(lmv_done, 2 * TILES)
            v.wait_ge(lsd_ready, 2)
            link(v.reciprocal(RS[:, 0:TILES], SD[:, 0:TILES]))
            v.scalar_tensor_tensor(nmr[:, :], MV[:, 0:TILES, 0], -1.0, RS[:, 0:TILES], ALU.mult, ALU.mult)\
                .then_inc(nmr_ready, 1)

            full = (P, TILES, E1)
            by_tile = lambda ap: ap.unsqueeze(2).broadcast_to(full)
            by_expert = lambda ap: ap.unsqueeze(1).broadcast_to(full)
            A = {n: ap[:, :, :] for n, ap in R.items()}
            Q = {n: ap[:, :] for n, ap in q36.items()}
            v.wait_ge(logits_ready, TILES)
            v.wait_ge(upm, 32)
            link(v.tensor_tensor(A["log"], logits[:, :, :],
                                 by_tile(RS[:, 0:TILES]), ALU.mult))
            link(v.tensor_reduce(Q["mx"], A["log"], AX.X, ALU.max))
            v.tensor_tensor(A["t"], A["log"], by_tile(Q["mx"]), ALU.subtract).then_inc(rexp_in, 1)
            v.wait_ge(r_e, 1)
            link(v.tensor_reduce(Q["sm"], A["e"], AX.X, ALU.add))
            link(v.reciprocal(Q["rs"], Q["sm"]))
            link(v.tensor_tensor(A["p"], A["e"], by_tile(Q["rs"]), ALU.mult))

            def best(m, onehot):
                link(v.tensor_reduce(m, A["p"], AX.X, ALU.max))
                link(v.tensor_tensor(A["t"], A["p"], by_tile(m), ALU.is_equal))
                link(v.tensor_tensor(A["t"], A["t"], by_expert(w8), ALU.mult))
                link(v.tensor_reduce(Q["k"], A["t"], AX.X, ALU.max))
                link(v.tensor_tensor(onehot, by_expert(w8), by_tile(Q["k"]), ALU.is_equal))

            best(Q["m1"], A["oh1"])
            link(v.scalar_tensor_tensor(A["p"], A["oh1"], -2.0, A["p"], ALU.mult, ALU.add))
            best(Q["m2"], A["oh2"])
            v.tensor_tensor(A["O"], A["oh1"], A["oh2"], ALU.add).then_inc(r_O, 1)
            link(v.tensor_tensor(Q["den"], Q["m1"], Q["m2"], ALU.add))
            link(v.reciprocal(Q["den"], Q["den"]))
            link(v.tensor_tensor(score[:, 0, :], Q["m1"], Q["den"], ALU.mult))
            link(v.tensor_tensor(score[:, 1, :], Q["m2"], Q["den"], ALU.mult))
            v.wait_ge(r_tot, 1)
            tot, inc, exc, cmp = (scT[n][:, :, :] for n in ("tot", "inc", "exc", "cmp"))
            nt, end, base = (e8[n][:, :] for n in ("nt", "end", "base"))
            flat = lambda ap: ap.rearrange("p e t -> p (e t)")
            link(v.tensor_tensor_scan(flat(inc), jmask, flat(tot), 0.0, ALU.mult, ALU.add))
            link(v.tensor_tensor(exc, inc, tot, ALU.subtract))
            link(v.tensor_tensor(cmp, inc[:, :, TILES - 1:TILES].broadcast_to((P, E1, TILES)),
                                 j128.unsqueeze(1).broadcast_to((P, E1, TILES)), ALU.is_gt))
            link(v.tensor_reduce(nt, cmp, AX.X, ALU.add))
            link(v.tensor_tensor_scan(end, one8, nt, 0.0, ALU.mult, ALU.add))
            link(v.tensor_tensor(base, end, nt, ALU.subtract))
            link(v.tensor_scalar(base, base, float(P), None, ALU.mult))
            link(v.tensor_scalar(tile_end[:, :], end, 1.0, None, ALU.max))
            link(v.tensor_tensor(tcmp[:, :, :], end[:, 0:E1 - 1].unsqueeze(1).broadcast_to((P, MT, E1 - 1)),
                                 iMT.unsqueeze(2).broadcast_to((P, MT, E1 - 1)), ALU.is_le))
            link(v.tensor_reduce(texp[:, :], tcmp[:, :, :], AX.X, ALU.add))
            link(v.tensor_copy(tile_expert[:, :], texp[:, :]))
            v.wait_ge(r_pre, 2)
            link(v.tensor_tensor(A["pe"], PS[:, 2, 0:TILES * E1].rearrange("p (t e) -> p t e", e=E1),
                                 exc.rearrange("p e t -> p t e"), ALU.add))
            link(v.tensor_tensor(A["pe"], A["pe"], by_expert(base), ALU.add))
            for k, oh in enumerate(("oh1", "oh2")):
                link(v.tensor_tensor(A["t"], A["pe"], A[oh], ALU.mult))
                link(v.tensor_reduce(Q["pf"], A["t"], AX.X, ALU.add))
                link(v.tensor_copy(pos[:, k, :], Q["pf"]))
                v.sem_inc(routed, 1)

            def x_lo(i, s):
                v.wait_ge(xt_hi, i + 1)
                v.tensor_tensor(xtL[:, s, :, :], PS[:, s, :].rearrange("p (k n) -> p k n", n=P),
                                xtH[:, s, :, :].bitcast(f32), ALU.subtract).then_inc(xt_ready, 1)

            def hidden(i, s):
                v.wait_ge(sgt_ready, i + 1)
                behind(v, th_ready, i)
                v.tensor_tensor(hh[:, s, :], sgt[:, s, :], PS[:, 2 + s, 1:512:2], ALU.mult).then_inc(h_ready, 1)

            def h_lo(i, s):
                v.wait_ge(ht_hi, i + 1)
                v.tensor_tensor(htL[:, s, :, :], PS[:, 4 + s, 0:2 * P].rearrange("p (k n) -> p k n", n=P),
                                htH[:, s, :, :].bitcast(f32), ALU.subtract).then_inc(ht_ready, 1)

            def step(i, s, first=False, last=False):
                if not last:
                    x_lo(i + 1, 1 - s)
                if not first:
                    h_lo(i - 1, 1 - s)
                hidden(i, s)

            v.wait_ge(scattered, 16 * 2 * TILES)
            x_lo(0, 0)
            step(0, 0, first=True)
            step(1, 1)
            with v.Fori(1, MT // 2 - 1) as g:
                for s in range(2):
                    step(g * 2 + s, s)
            step(MT - 2, 0)
            step(MT - 1, 1, last=True)
            h_lo(MT - 1, 1)

            def add_out(t):
                v.wait_ge(f_ready, t + 1)
                dst = X[:, :, t * P:(t + 1) * P]
                v.tensor_tensor(dst, dst, PS[:, t % 4, :].rearrange("p (k n) -> p k n", n=P), ALU.add)\
                    .then_inc(f_added, 1)

            for t in range(TILES):
                v.wait_ge(gs_ready, t + 1)
                if t >= 2:
                    v.wait_ge(f_ready, t - 1)
                v.scalar_tensor_tensor(gt[:, t % 2, :], g2[:, t % GRING, :], score[:, 1, t:t + 1], gs[:, t % 2, :],
                                       ALU.mult, ALU.add).then_inc(gt_ready, 1)
                if t:
                    add_out(t - 1)
            add_out(TILES - 1)


def bilinear():
    def axis(n):
        at = np.maximum((np.arange(n, dtype=np.float32) + np.float32(0.5)) * np.float32(3 / n) - np.float32(0.5), 0)
        i0 = np.minimum(np.floor(at).astype(np.int32), 2)
        i1 = np.minimum(i0 + 1, 2)
        w = at - i0.astype(np.float32)
        m = np.zeros((3, n), np.float32)
        for o in range(n):
            m[i0[o], o] += 1 - w[o]
            m[i1[o], o] += w[o]
        return m
    return np.einsum("ay,bx->abyx", axis(H), axis(W)).reshape(L, S)


def constants():
    mats = np.stack([np.eye(P), np.ones((P, P)), np.triu(np.ones((P, P)), 1)], 1).astype(np.float32)
    token = np.arange(ROWT)
    ind = (((token % W) // (W // 3))[:, None] == np.arange(3)).astype(np.float32) / (H // 3 * W // 3)
    up = np.zeros((IB, L, IB, S), np.float32)
    for b in range(IB):
        up[b, :, b] = bilinear()
    mask = np.ones((E1, TILES), np.float32)
    mask[:, 0] = 0
    row = np.concatenate([E1 - np.arange(E1), P * np.arange(TILES), np.arange(MT), mask.ravel()]).astype(np.float32)
    return {"c_mat": mats, "c_ind": ind, "c_up": up.reshape(TT, IB, S), "c_rout": np.tile(row, (P, 1))}


def kernel(**inputs):
    import concourse.bacc as bacc
    from concourse.bass_utils import run_bass_kernel_spmd

    def both(name):
        return [np.asarray(inputs[f"L{l}_conv_{name}"]) for l in range(2)]

    def rows(a, n):
        return a.reshape(n, a.shape[0] // n, *a.shape[1:]).swapaxes(0, 1)

    arrays = {"x": np.asarray(inputs["x"]).reshape(B, CH, S)}
    arrays |= constants()
    arrays["pe_W"] = np.stack([rows(a, KC) for a in both("pe_W")])
    arrays["vec_hid"] = np.stack([np.stack(v) for v in zip(both("pe_b"), both("ln_g"), both("ln_b"))])
    arrays["in_W"] = np.stack([rows(a, 2) for a in both("in_W")])
    arrays["vec_inner"] = np.stack([
        rows(np.concatenate([w.reshape(INNER, 3), cb[:, None], tb[:, None], d[:, None]], 1), JC)
        for w, cb, tb, d in zip(both("conv_w"), both("conv_b"), both("dt_b"), both("D_param"))])
    arrays["a_log"] = np.stack([rows(a, JC) for a in both("A_log")])
    arrays["xproj"] = np.stack([rows(a, JC) for a in both("xproj_W")])
    arrays["dt_W"] = np.stack(both("dt_W"))
    arrays["out_W"] = np.stack([rows(a, JC) for a in both("out_W")])
    gu0, dn0 = np.asarray(inputs["L0_ffn_gate_up_proj"]), np.asarray(inputs["L0_ffn_down_proj"])
    gu1, dn1 = np.asarray(inputs["L1_ffn_expert_gate_up"]), np.asarray(inputs["L1_ffn_expert_down"])

    def pieces(a, n):
        e, r, c = a.shape
        return a.reshape(e, n, r // (n * P), P, c).swapaxes(2, 3).reshape(e, n, P, PIECE)

    w0 = np.concatenate([pieces(gu0, KC), pieces(dn0, 2)], 1).reshape(NP0, P, PIECE)
    w1 = np.concatenate([pieces(gu1, 2), pieces(dn1, 1)], 1).reshape(NP1, P, PIECE)
    arrays["w_ffn"] = np.concatenate([w0, w1])
    arrays["router"] = rows(np.asarray(inputs["L1_ffn_router_gate"]).T, KC)

    nc = bacc.Bacc("TRN2", target_bir_lowering=False, num_devices=1)
    data, args = {}, []
    for name, a in arrays.items():
        a = np.ascontiguousarray(a)
        data[f"in_{name}"] = a
        args.append(nc.dram_tensor(f"in_{name}", a.shape, mybir.dt.from_np(a.dtype), kind="ExternalInput").ap())
    args.append(nc.dram_tensor("out_x", (B, CH, S), mybir.dt.float32, kind="ExternalOutput").ap())
    metaformer(nc, *args)
    r = run_bass_kernel_spmd(nc, [data], core_ids=[0])
    return r.results[0]["out_x"].reshape(B, CH, H, W)
```

```python
from contextlib import ExitStack

import concourse.bass as bass
import numpy as np
from concourse import mybir

P = 128
B, CH, H, W = 16, 512, 24, 12
S = H * W
T = B * S
KC = CH // P
HID, INNER, NS, RANK = 192, 384, 16, 48
HH = HID // 2
JC = INNER // P
L = 9
NT = B * L
TT = NT // 2
IB = B // 2
ROWT = S // 3
NROW = T // ROWT
XG = 8
GR = 4
NG = NROW // GR
XR = 14
LAG = XR - 3
XNG = 8
MIXW = 16 * 9
HT = NROW // 2
TILES = T // P
E0, I0 = 4, 512
E1, I1 = 8, 256
CN = 288
NC = T // E0 // CN
EJ = TILES // E0
PIECE = 1024
PE0 = KC * (2 * I0 + CH) // PIECE
PE1 = (KC * 2 * I1 + 2 * CH) // PIECE
NP0, NP1 = E0 * PE0, E1 * PE1
MT = 2 * TILES + E1
EARLY = 12
ROUND = 1.5 * 2 ** 23
HALF = T // 2
XSR = 8
GRING = 4
TB = (6, 7, 0)
RB = (6, 0)
RC = 256


def metaformer(nc, x, c_mat, c_ind, c_up, c_rout, pe_W, vec_hid, in_W, vec_inner, a_log, xproj, dt_W, out_W,
               w_ffn, router, out):
    f32, f32r, i32 = mybir.dt.float32, mybir.dt.float32r, mybir.dt.int32
    ALU, ACT, AX = mybir.AluOpType, mybir.ActivationFunctionType, mybir.AxisListType
    ds = bass.ds

    bc_dram = nc.dram_tensor("bc_dram", (2, 2 * NS, NT), f32, kind="Internal").ap()
    stat_dram = nc.dram_tensor("stat_dram", (2, E0, EJ * P), f32, kind="Internal").ap()
    w1_dram = nc.dram_tensor("w1_dram", (NP1, P, 2, PIECE), f32, kind="Internal").ap()
    xn_dram = nc.dram_tensor("xn_dram", (T, CH), f32, kind="Internal").ap()
    y_dram = nc.dram_tensor("y_dram", (MT * P, CH), f32, kind="Internal").ap()

    ctx = ExitStack()
    with ctx:
        def sb(name, shape, dt=f32, life=ctx):
            return life.enter_context(nc.sbuf_tensor("sb_" + name, shape, dt))

        def sem(name):
            return ctx.enter_context(nc.semaphore(name))

        X = sb("X", [P, KC, T])
        mats = sb("mats", [P, 3, P])
        ident, ones, triu = mats[:, 0, :], mats[:, 1, :], mats[:, 2, :]
        eps = sb("eps", [P, 2])
        ind = sb("ind", [ROWT, 3])
        raw = sb("raw", [P, 2, PIECE])
        MV = sb("MV", [P, NROW, 2])
        ST6 = sb("ST6", [P, 2, GR, 6])
        SD = sb("SD", [P, NROW])
        RS = sb("RS", [P, NROW])
        PS = ctx.enter_context(nc.psum_tensor("ps", [P, 8, 512], f32))

        mix = ExitStack()
        before = nc.sbuf_bytes_remaining
        score = sb("score", [P, 2, TILES], f32, mix)
        pos = sb("pos", [P, 2, TILES], i32, mix)
        source = sb("source", [P, MT], i32, mix)
        gather_at = sb("gather_at", [P, XSR], i32, mix)
        tile_expert = sb("tile_expert", [P, MT], i32, mix)
        tile_end = sb("tile_end", [P, E1], i32, mix)
        kept = before - nc.sbuf_bytes_remaining
        tables = ExitStack()
        R = {n: sb("R_" + n, [P, TILES, E1], f32, tables)
             for n in ("log", "e", "p", "oh1", "oh2", "t", "O", "pe")}
        q36 = {n: sb("q_" + n, [P, TILES], f32, tables) for n in ("mx", "sm", "rs", "m1", "m2", "k", "den", "pf")}
        scT = {n: sb("s_" + n, [P, E1, TILES], f32, tables) for n in ("tot", "inc", "exc", "cmp")}
        tables_end = nc.sbuf_bytes_remaining
        tables.close()
        gH = sb("gH", [TT, 2, CH], f32r, mix)
        gL = sb("gL", [TT, 2, CH], f32r, mix)
        upM = sb("upM", [TT, IB, S], f32r, mix)
        assert nc.sbuf_bytes_remaining <= tables_end
        MR = sb("MR", [P, 2 * TILES], f32, mix)
        statT = sb("statT", [2 * TILES, P], f32, mix)
        wbar = sb("wbar", [P, E1], f32, mix)
        body = ExitStack()
        pT = sb("pT", [P, KC, NT], f32, body)
        peW = sb("peW", [P, KC, HID], f32, body)
        vhid = sb("vhid", [TT, 3, HID], f32, body)
        inW = sb("inW", [HH, 2, 2 * INNER], f32, body)
        vinn = sb("vinn", [P, JC, 6], f32, body)
        alog = sb("alog", [P, JC, NS], f32, body)
        xpW = sb("xpW", [P, JC, RANK + 2 * NS], f32, body)
        dtW = sb("dtW", [RANK, INNER], f32, body)
        outW = sb("outW", [P, JC, CH], f32, body)
        tk = sb("tk", [TT, 2, HID], f32, body)
        mvh = sb("mvh", [TT, 2, 2], f32, body)
        sth = sb("sth", [TT, 2, 6], f32, body)
        sdh = sb("sdh", [TT, 2], f32, body)
        rsh = sb("rsh", [TT, 2], f32, body)
        tT = sb("tT", [HH, 2, NT], f32, body)
        acc = sb("acc", [P, JC, NT], f32, body)
        uu = sb("uu", [P, JC, NT], f32, body)
        sz = sb("sz", [P, JC, NT], f32, body)
        bc = sb("bc", [2 * NS, NT], f32, body)
        dl = sb("dl", [RANK, NT], f32, body)
        early = ExitStack()
        ptok = sb("ptok", [TT, 2, CH], f32, early)
        early.close()
        dx = sb("dx", [P, JC, NT], f32, body)
        ab = sb("ab", [P, JC, NT], f32, body)
        delta = sb("delta", [P, JC, NT], f32, body)
        du = dx
        negA = sb("negA", [P, JC, NS], f32, body)
        yy = sb("yy", [P, JC, NT], f32, body)
        patch = ExitStack()
        xtok = sb("xtok", [ROWT, XR, CH], f32, patch)
        RI = sb("RI", [ROWT, 2, HT * (TT + 3)], f32, patch)
        upS = sb("upS", [TT, IB, S], f32, patch)
        assert nc.sbuf_bytes_remaining >= 4 * PIECE * 4
        patch.close()
        scan_at = nc.sbuf_bytes_remaining
        hs = sb("hs", [P, NS, NT], f32, body)
        Bb = sb("Bb", [P, 2 * NS, NT], f32, body)
        a1 = sb("a1", [P, 2, NS, NT], f32, body)
        db = sb("db", [P, 2, NS, NT], f32, body)
        body.close()
        late = ExitStack()
        sb("gap_to_pieces", [P, (nc.sbuf_bytes_remaining - 4 * PIECE * 4) // 4], f32, late)
        pieces = sb("pieces", [P, 2, 2, PIECE], f32r, late)
        late.close()
        moe_in = ExitStack()
        XN = sb("XN", [P, TILES, CH], f32, moe_in)
        rout = sb("rout", [P, E1 + TILES + MT + E1 * TILES + P + TILES], f32, moe_in)
        row_s = sb("row_s", [P, 2, TILES], f32, moe_in)
        row_m = sb("row_m", [P, 2, TILES], f32, moe_in)
        found = sb("found", [P, 2, MT], f32, moe_in)
        e8 = {n: sb("e_" + n, [P, E1], f32, moe_in) for n in ("nt", "end", "base")}
        tcmp = sb("tcmp", [P, MT, E1 - 1], f32, moe_in)
        texp = sb("texp", [P, MT], f32, moe_in)
        nmr = sb("nmr", [P, TILES], f32, moe_in)
        eyeR = sb("eyeR", [P, KC, P + E1], f32, moe_in)
        rw = eyeR[:, :, P:]
        logits = sb("logits", [P, TILES, E1], f32, moe_in)
        moe_in_end = nc.sbuf_bytes_remaining
        moe_in.close()
        invert = ExitStack()
        oh_s = sb("oh_s", [P, 2, TILES, P], f32r, invert)
        oh_m = sb("oh_m", [P, 2, TILES, MT], f32r, invert)
        assert 2 * TILES * (P + MT) <= XNG * GR * CH
        invert.close()
        mix.close()
        ffn0 = ExitStack()
        w0 = [None, sb("w0_1", [P, 2, PE0 * PIECE], f32r, ffn0)]
        rmb = sb("rmb", [P, 2, CN], f32, ffn0)
        xr = sb("xr", [P, KC, CN], f32, ffn0)
        sg = sb("sg", [P, 2, CN], f32, ffn0)
        sb("gap_to_scan", [P, (nc.sbuf_bytes_remaining - scan_at) // 4], f32, ffn0)
        w0[0] = sb("w0_0", [P, 2, PE0 * PIECE], f32r, ffn0)
        xnH = sb("xnH", [P, KC, CN], f32r, ffn0)
        xnL = sb("xnL", [P, KC, CN], f32r, ffn0)
        itH = sb("itH", [P, KC, CN], f32r, ffn0)
        itL = sb("itL", [P, KC, CN], f32r, ffn0)
        ffn0.close()
        ffn1 = ExitStack()
        sb("gap_kept", [P, kept // 4], f32, ffn1)
        xs = sb("xs", [P, XSR, CH], f32, ffn1)
        xtH = sb("xtH", [P, 2, KC, P], f32r, ffn1)
        xtL = sb("xtL", [P, 2, KC, P], f32r, ffn1)
        sgt = sb("sgt", [P, 2, I1], f32, ffn1)
        hh = sb("hh", [P, 2, I1], f32, ffn1)
        htH = sb("htH", [P, 2, 2, P], f32r, ffn1)
        htL = sb("htL", [P, 2, 2, P], f32r, ffn1)
        ysb = sb("ysb", [P, 2, CH], f32, ffn1)
        g1 = sb("g1", [P, GRING, CH], f32, ffn1)
        g2 = sb("g2", [P, GRING, CH], f32, ffn1)
        gs = sb("gs", [P, 2, CH], f32, ffn1)
        gt = sb("gt", [P, 2, CH], f32, ffn1)
        W1B = 2 * 2 * PE1 * PIECE * 4
        assert moe_in_end >= W1B // 2 and nc.sbuf_bytes_remaining >= W1B
        sb("gap_to_weights", [P, (nc.sbuf_bytes_remaining - W1B) // 4], f32, ffn1)
        w1 = sb("w1", [P, 2, PE1, 2 * PIECE], f32r, ffn1)
        ffn1.close()

        Xe = X[:, :, :].rearrange("p k (t e) -> p k e t", e=E0)
        w8 = rout[:, 0:E1]
        j128 = rout[:, E1:E1 + TILES]
        iMT = rout[:, E1 + TILES:E1 + TILES + MT]
        jmask = rout[:, E1 + TILES + MT:E1 + TILES + MT + E1 * TILES]
        i128 = rout[:, -P - TILES:-TILES]
        number = rout[:, -TILES:]
        one8 = ones[:, 0:E1]

        consts = sem("consts")
        x_loaded = [sem(f"x_loaded_{g}") for g in range(XG)]
        mixw, upm = sem("mix_weights"), sem("up_matrix")
        tp_ready, xtok_ready = sem("tp_ready"), sem("xtok_ready")
        st_done, mv_done, sd_ready = sem("st_done"), sem("mv_done"), sem("sd_ready")
        ri_ready, pooled = sem("ri_ready"), sem("pooled")
        ptok_ready, ptok_T = sem("pooled_tokens"), sem("pooled_tokens_T")
        p_ready, tok_ready = sem("p_ready"), sem("tok_ready")
        var_h, sd_h, tk_ready, tkT = sem("var_h"), sem("sd_h"), sem("tk_ready"), sem("tkT")
        tT_ready, xz_ready, acc_ready = sem("tT_ready"), sem("xz_ready"), sem("acc_ready")
        u_ready, z_ready, dbc_ready = sem("u_ready"), sem("z_ready"), sem("dbc_ready")
        bc_ready, bc_out, bc_in, dl_ready = sem("bc_ready"), sem("bc_out"), sem("bc_in"), sem("dl_ready")
        dt_ready, ab_ready, ex_done, sp_ready = sem("dt_ready"), sem("ab_ready"), sem("ex_done"), sem("sp_ready")
        ea_ready, na_ready, du_ready = sem("ea_ready"), sem("na_ready"), sem("du_ready")
        db_ready, a1_ready, hc_ready, ysum = sem("db_ready"), sem("a1_ready"), sem("hc_ready"), sem("ysum")
        a1_zero, scanned = sem("a1_zero"), sem("scanned")
        y_ready, og_ready, gh_ready, g_ready = sem("y_ready"), sem("og_ready"), sem("gh_ready"), sem("g_ready")
        up_ready, up_added = sem("up_ready"), sem("up_added")
        lt_ready, lt_free, lst_done, lmv_done = sem("lt_ready"), sem("lt_free"), sem("lst_done"), sem("lmv_done")
        lsd_ready, mr_ready = sem("lsd_ready"), sem("mr_ready")
        mrT, statT_ready, stats_out = sem("mrT"), sem("statT_ready"), sem("stats_out")
        dve = sem("dve_step")
        raw_loaded, split_step = [sem(f"raw_loaded_{r}") for r in range(2)], sem("split_step")
        w0_ready = sem("w0_ready")
        rm_loaded, rm_free, xr_done = sem("rm_loaded"), sem("rm_free"), sem("xr_done")
        xn_ready = sem("xn_ready")
        gu_ready, gu_free, sg_ready, sg_free = sem("gu_ready"), sem("gu_free"), sem("sg_ready"), sem("sg_free")
        it_step, it_ready = sem("it_step"), sem("it_ready")
        dn_ready, dn_free = sem("dn_ready"), sem("dn_free")
        wb_ready, wb_sb, rw_ready = sem("wb_ready"), sem("wb_sb"), sem("rw_ready")
        logits_ready, r_e, r_O, r_pre, r_tot = (sem("logits_ready"), sem("router_exp"), sem("router_onehot"),
                                               sem("router_prefix"), sem("router_totals"))
        rexp_in, xnorm, nmr_ready = sem("rexp_in"), sem("xnorm"), sem("nmr_ready")
        xn_stored = [sem("xn_stored_first"), sem("xn_stored_last")]
        oh_s_ready, oh_m_ready, oh_numbered = sem("oh_s_ready"), sem("oh_m_ready"), sem("oh_numbered")
        inverted, source_ready = sem("inverted"), sem("source_ready")
        at_ready, gather_go = sem("at_ready"), sem("gather_go")
        w1_stored = [sem("w1_stored_0"), sem("w1_stored_1")]
        w1_loaded, w1_ready, slot_free = sem("w1_loaded"), sem("w1_ready"), sem("slot_free")
        xs_loaded = [sem(f"xs_loaded_{r}") for r in range(XSR)]
        t_ready, xt_hi, xt_ready = sem("t_ready"), sem("xt_hi"), sem("xt_ready")
        g_up, sgt_ready, h_ready = sem("g_up"), sem("sgt_ready"), sem("h_ready")
        th_ready, ht_hi, ht_ready = sem("th_ready"), sem("ht_hi"), sem("ht_ready")
        d_ready, y_out, y_stored = sem("d_ready"), sem("y_out"), [sem("y_stored_0"), sem("y_stored_1")]
        g_loaded = [sem(f"g_loaded_{r}") for r in range(GRING)]
        gs_ready, gt_ready = sem("gs_ready"), sem("gt_ready")
        f_ready, f_added, stored = sem("f_ready"), sem("f_added"), sem("stored")

        def behind(engine, signal, i):
            if not isinstance(i, int) or i >= 2:
                engine.wait_ge(signal, i - 1)

        def router_banks(t):
            return PS[:, RB[t % 2]:RB[t % 2] + 2, :].rearrange("p b (h n) -> p (b h) n", n=RC)

        def images_before(tokens):
            return -(-tokens // S)

        block = ctx.enter_context(nc.Block())

        @block.sync
        def _(sp):
            sp.dma_start(mats[:, :, :], c_mat).then_inc(consts, 16)
            sp.dma_start(ind[:, :], c_ind).then_inc(consts, 16)

            def load_mix_weights(l):
                for dst, src in ((peW[:, :, :], pe_W[l]), (inW[:, :, :], in_W[l]),
                                 (vinn[:, :, :], vec_inner[l]), (alog[:, :, :], a_log[l]),
                                 (xpW[:, :, :], xproj[l]), (dtW[:, :], dt_W[l]), (outW[:, :, :], out_W[l])):
                    sp.dma_start(dst, src).then_inc(mixw, 16)
                sp.dma_start(vhid[:, :, :], vec_hid[l:l + 1].broadcast_to((TT, 3, HID))).then_inc(mixw, 16)
                sp.dma_start(upS[:, :, :], c_up).then_inc(mixw, 16)

            def exchange(l):
                sp.wait_ge(bc_ready, l + 1)
                sp.dma_start(bc_dram[l], bc[:, :]).then_inc(bc_out, 16)
                sp.wait_ge(bc_out, l * 16 + 16)
                sp.wait_ge(p_ready, l * 2 + 2)
                sp.dma_start(Bb[:, :, :], bc_dram[l:l + 1].broadcast_to((P, 2 * NS, NT))).then_inc(bc_in, 16)

            for b in range(B):
                sp.dma_start(X[:, :, b * S:(b + 1) * S], x[b].rearrange("(k p) s -> p k s", p=P))\
                    .then_inc(x_loaded[b // (B // XG)], 16)
            load_mix_weights(0)
            exchange(0)
            sp.wait_ge(statT_ready, 1)
            sp.dma_start(stat_dram.rearrange("a e (j t) -> (a e j) t", t=P), statT[:, :]).then_inc(stats_out, 16)
            sp.wait_ge(stats_out, 16)
            with sp.Fori(0, E0) as e:
                for c in range(NC):
                    sp.wait_ge(rm_free, e * NC + c + 1)
                    sp.dma_start(rmb[:, :, :],
                                 stat_dram[:, ds(e, 1), c * CN:(c + 1) * CN].rearrange("a e n -> e a n")
                                 .broadcast_to((P, 2, CN))).then_inc(rm_loaded, 16)
            sp.wait_ge(dn_free, E0 * NC + 1)
            load_mix_weights(1)
            exchange(1)
            sp.wait_ge(y_ready, 2)
            sp.dma_start(rw, router).then_inc(upm, 16)
            sp.dma_start(rout[:, :], c_rout).then_inc(upm, 16)
            for g in range(TILES // GR):
                sp.wait_ge(xnorm, (g + 1) * GR)
                sp.dma_start(xn_dram[g * GR * P:(g + 1) * GR * P].rearrange("(t p) c -> p t c", p=P),
                             XN[:, g * GR:(g + 1) * GR, :]).then_inc(xn_stored[g // XNG], 16)
            for e in range(E1):
                if e == 0:
                    for r in range(2):
                        sp.wait_ge(w1_stored[r], 16 * (NP1 // 2))
                elif e == 1:
                    sp.wait_ge(t_ready, 1)
                else:
                    end = sp.value_load(tile_end[0:1, e - 2:e - 1], min_val=1, max_val=MT)
                    sp.wait_ge(d_ready, end)
                    sp.sem_inc(slot_free, 1)
                for q in range(PE1):
                    sp.dma_start(w1[:, 1 - e % 2, q, :].bitcast(f32),
                                 w1_dram[e * PE1 + q].rearrange("p a n -> p (a n)")).then_inc(w1_loaded, 16)
                sp.wait_ge(w1_loaded, 16 * PE1 * (e + 1))
                sp.sem_inc(w1_ready, 1)
            for b in range(B):
                sp.wait_ge(f_added, -(-S * (b + 1) // P))
                sp.dma_start(out[b].rearrange("(k p) s -> p k s", p=P), X[:, :, b * S:(b + 1) * S])\
                    .then_inc(stored, 16)
            sp.wait_ge(stored, 16 * B)

        @block.gpsimd
        def _(pool):
            def split(p, dst_h, dst_l):
                r = p % 2
                pool.wait_ge(raw_loaded[r], 16 * (p // 2 + 1))
                pool.tensor_copy(dst_h, raw[:, r, :]).then_inc(split_step, 1)
                pool.wait_ge(split_step, 2 * p + 1)
                pool.tensor_tensor(dst_l, raw[:, r, :], dst_h.bitcast(f32), ALU.subtract).then_inc(split_step, 1)
                pool.wait_ge(split_step, 2 * p + 2)
                if p + 2 < NP0 + NP1:
                    pool.dma_start(raw[:, r, :], w_ffn[p + 2]).then_inc(raw_loaded[r], 16)

            def split_store(n):
                if n >= 2:
                    pool.wait_ge(w1_stored[n % 2], 16 * (n // 2))
                split(NP0 + n, pieces[:, n % 2, 0, :], pieces[:, n % 2, 1, :])
                pool.dma_start(w1_dram[n], pieces[:, n % 2, :, :].bitcast(f32)).then_inc(w1_stored[n % 2], 16)

            def scan_inputs(l):
                pool.wait_ge(du_ready, l + 1)
                pool.wait_ge(bc_in, l * 16 + 16)
                for j in range(JC):
                    if j >= 2:
                        pool.wait_ge(scanned, l * JC + j - 1)
                    pool.tensor_tensor(db[:, j % 2, :, :], du[:, j:j + 1, :].broadcast_to((P, NS, NT)),
                                       Bb[:, 0:NS, :], ALU.mult).then_inc(db_ready, 1)

            pool.wait_ge(x_loaded[0], 16 * (B // XG))
            pool.dma_start(raw[:, 0, :], w_ffn[0]).then_inc(raw_loaded[0], 16)
            pool.dma_start(raw[:, 1, :], w_ffn[1]).then_inc(raw_loaded[1], 16)
            scan_inputs(0)
            pool.wait_ge(y_ready, 1)
            for e in range(E0):
                if e == 1:
                    pool.wait_ge(stats_out, 16)
                if e >= 2:
                    pool.wait_ge(dn_ready, (e - 1) * NC)
                for q in range(PE0):
                    p = e * PE0 + q
                    split(p, *(w0[e % 2][:, a, q * PIECE:(q + 1) * PIECE] for a in range(2)))
                pool.sem_inc(w0_ready, 1)
            pool.wait_ge(dn_ready, E0 * NC)
            for n in range(EARLY):
                split_store(n)
            for r in range(2):
                pool.wait_ge(w1_stored[r], 16 * (EARLY // 2))
            scan_inputs(1)
            pool.wait_ge(y_ready, 2)
            for n in range(EARLY, NP1):
                split_store(n)
            pool.wait_ge(upm, 32)
            for n in range(2 * E0):
                k, sl = n // E0, slice(n % E0 * EJ, (n % E0 + 1) * EJ)
                pool.wait_ge(oh_m_ready, n + 1)
                pool.tensor_tensor(oh_m[:, k, sl, :], oh_m[:, k, sl, :].bitcast(f32),
                                   number[:, sl].unsqueeze(2).broadcast_to((P, EJ, MT)), ALU.mult)\
                    .then_inc(oh_numbered, 1)
            y_t = y_dram.rearrange("(m p) c -> m p c", p=P)

            def gather(i, r):
                if not isinstance(i, int):
                    pool.wait_ge(t_ready, i - (XSR - 1))
                pool.tensor_copy(gather_at[:, r:r + 1], source[:, i:i + 1] if isinstance(i, int) else
                                 source[:, ds(i, 1)]).then_inc(at_ready, 1)
                pool.wait_ge(at_ready, i + 1)
                pool.sem_inc(gather_go, 1)
                pool.indirect_dma_start(xs[:, r, :], None, xn_dram,
                                        bass.IndirectOffsetOnAxis(ap=gather_at[:, r:r + 1], axis=0))\
                    .then_inc(xs_loaded[r], 16)

            def store(i, r):
                pool.wait_ge(y_out, i + 1)
                pool.dma_start(y_t[ds(i, 1)].rearrange("m p c -> p m c"), ysb[:, r:r + 1, :])\
                    .then_inc(y_stored[r], 16)

            pool.wait_ge(source_ready, 1)
            pool.wait_ge(xn_stored[0], 16 * XNG)
            pool.wait_ge(xn_stored[1], 16 * (TILES // GR - XNG))
            for i in range(XSR):
                gather(i, i)
            with pool.Fori(0, MT // XSR - 1) as g:
                for r in range(XSR):
                    gather(g * XSR + (r + XSR), r)
                    store(g * XSR + r, r % 2)
            for r in range(XSR):
                store(MT - XSR + r, r % 2)
            for r in range(2):
                pool.wait_ge(y_stored[r], 16 * (MT // 2))
            for t in range(TILES):
                if t >= GRING:
                    pool.wait_ge(gt_ready, t - GRING + 1)
                for k, g in enumerate((g1, g2)):
                    pool.indirect_dma_start(
                        g[:, t % GRING, :], None, y_dram, bass.IndirectOffsetOnAxis(ap=pos[:, k, t:t + 1], axis=0))\
                        .then_inc(g_loaded[t % GRING], 16)

        @block.tensor
        def _(pe):
            def pool_patches(l, t):
                h, i = t // HT, t % HT
                if t % GR == 0:
                    pe.wait_ge(ri_ready, l * NG + t // GR + 1)
                pe.matmul(PS[0:TT, 4 + h, :], RI[:, h, i * TT:(i + 1) * TT], xtok[:, t % XR, :],
                          start=i == 0, stop=i == HT - 1).then_inc(pooled, 1)

            def pooled_transposes(l, h):
                pe.wait_ge(ptok_ready, l * 2 + h + 1)
                for k in range(KC):
                    last = pe.transpose(PS[:, 6 + h, k * TT:(k + 1) * TT], ptok[:, h, k * P:(k + 1) * P],
                                        ident[0:TT, 0:TT])
                last.then_inc(ptok_T, 1)

            def patches(l):
                for t in range(NROW + LAG):
                    if t < NROW:
                        if l == 0:
                            if t % (NROW // XG) == 0:
                                pe.wait_ge(x_loaded[t // (NROW // XG)], 16 * (B // XG))
                        elif t == 0:
                            pe.wait_ge(dn_free, E0 * NC + 1)
                        if t >= 3:
                            pe.wait_ge(xtok_ready, l * NROW + t - 2)
                        for k in range(KC):
                            last = pe.transpose(PS[0:ROWT, t % 3, k * P:(k + 1) * P],
                                                X[:, k, t * ROWT:(t + 1) * ROWT], ident)
                        last.then_inc(tp_ready, 1)
                    if t >= LAG:
                        pool_patches(l, t - LAG)
                    if t == NROW + GR:
                        pooled_transposes(l, 0)
                pooled_transposes(l, 1)

            def mixer(l):
                pe.wait_ge(mixw, (l + 1) * MIXW)
                pe.wait_ge(p_ready, l * 2 + 2)
                for tt in range(2):
                    for k in range(KC):
                        last = pe.matmul(PS[0:TT, tt, 0:HID], pT[:, k, tt * TT:(tt + 1) * TT], peW[:, k, :],
                                         start=k == 0, stop=k == KC - 1)
                last.then_inc(tok_ready, 1)
                pe.wait_ge(tk_ready, l + 1)
                for tt in range(2):
                    for h in range(2):
                        last = pe.transpose(PS[0:HH, 2, h * NT + tt * TT:h * NT + (tt + 1) * TT],
                                            tk[:, tt, h * HH:(h + 1) * HH], ident[0:TT, 0:TT])
                last.then_inc(tkT, 1)
                pe.wait_ge(tT_ready, l + 1)
                pe.wait_ge(p_ready, l * 2 + 2)
                for m in range(2 * JC):
                    for h in range(2):
                        last = pe.matmul(PS[:, 3 + m // JC, (m % JC) * NT:(m % JC + 1) * NT],
                                         inW[:, h, m * P:(m + 1) * P], tT[:, h, :], start=h == 0, stop=h == 1)
                    if m % JC == JC - 1:
                        last.then_inc(xz_ready, 1)
                pe.wait_ge(u_ready, l + 1)
                for j in range(JC):
                    last = pe.matmul(PS[0:2 * NS, 5, 0:NT], xpW[:, j, RANK:], uu[:, j, :],
                                     start=j == 0, stop=j == JC - 1)
                last.then_inc(dbc_ready, 1)
                for j in range(JC):
                    last = pe.matmul(PS[0:RANK, 6, 0:NT], xpW[:, j, 0:RANK], uu[:, j, :],
                                     start=j == 0, stop=j == JC - 1)
                last.then_inc(dbc_ready, 1)
                pe.wait_ge(dl_ready, l + 1)
                for j in range(JC):
                    last = pe.matmul(PS[:, 7, j * NT:(j + 1) * NT], dtW[:, j * P:(j + 1) * P], dl[:, :],
                                     start=True, stop=True)
                last.then_inc(dt_ready, 1)
                for j in range(JC):
                    pe.wait_ge(hc_ready, l * JC + j + 1)
                    for n in range(NS):
                        last = pe.matmul(PS[:, 2, j * NT:(j + 1) * NT], ident, a1[:, j % 2, n, :],
                                         start=n == 0, stop=n == NS - 1)
                    last.then_inc(ysum, 1)
                pe.wait_ge(y_ready, l + 1)
                for tt in range(2):
                    for j in range(JC):
                        last = pe.matmul(PS[0:TT, tt, :], yy[:, j, tt * TT:(tt + 1) * TT], outW[:, j, :],
                                         start=j == 0, stop=j == JC - 1)
                last.then_inc(og_ready, 1)

            def upsample(l, b):
                for half in range(2):
                    if b:
                        pe.wait_ge(up_added, l * 2 * B + 2 * (b - 1) + half + 1)
                    for k in (2 * half, 2 * half + 1):
                        for g, first in ((gH, True), (gL, False)):
                            last = pe.matmul(PS[:, 2 + k, 0:S], g[:, b // IB, k * P:(k + 1) * P],
                                             upM[:, b % IB, :], start=first, stop=not first)
                    last.then_inc(up_ready, 1)

            def tile_transposes(l, q, view):
                if q >= len(TB):
                    pe.wait_ge(lt_free, l * TILES + q - len(TB) + 1)
                for k in range(KC):
                    last = pe.transpose(PS[:, TB[q % len(TB)], k * P:(k + 1) * P], view(k), ident)
                last.then_inc(lt_ready, 1)

            pe.wait_ge(consts, 32)
            patches(0)
            mixer(0)
            pe.wait_ge(g_ready, 2)
            q = 0
            for b in range(B):
                upsample(0, b)
                while q < TILES and images_before(E0 * P * (q // E0 + 1)) <= b:
                    pe.wait_ge(up_added, 2 * images_before(E0 * P * (q // E0 + 1)))
                    tile_transposes(0, q, lambda k: Xe[:, k, q % E0, (q // E0) * P:(q // E0 + 1) * P])
                    q += 1
            while q < TILES:
                pe.wait_ge(up_added, 2 * images_before(E0 * P * (q // E0 + 1)))
                tile_transposes(0, q, lambda k: Xe[:, k, q % E0, (q // E0) * P:(q // E0 + 1) * P])
                q += 1
            pe.wait_ge(mr_ready, 2)
            pe.transpose(PS[0:2 * TILES, 2, 0:P], MR[:, :], ident).then_inc(mrT, 1)

            def three(out_ap, wl, wh, xl, xh, start, stop):
                pe.matmul(out_ap, wh, xh, start=start, stop=False)
                pe.matmul(out_ap, wl, xh, start=False, stop=False)
                return pe.matmul(out_ap, wh, xl, start=False, stop=stop)

            pe.wait_ge(statT_ready, 1)
            with pe.Fori(0, E0 // 2) as ee:
                for s in range(2):
                    with pe.Fori(0, NC) as c:
                        n = ee * (2 * NC) + c + s * NC
                        pe.wait_ge(w0_ready, ee * 2 + s + 1)
                        pe.wait_ge(xn_ready, n + 1)
                        for m in range(KC):
                            pe.wait_ge(gu_free, n * KC + m + 1)
                            for u in range(2):
                                for k in range(KC):
                                    o = k * 2 * I0 + u * I0 + m * P
                                    last = three(PS[:, 2 * (m % 2) + u, 0:CN], w0[s][:, 1, o:o + P],
                                                 w0[s][:, 0, o:o + P], xnL[:, k, :], xnH[:, k, :],
                                                 k == 0, k == KC - 1)
                            last.then_inc(gu_ready, 1)
                        pe.wait_ge(dn_free, n + 1)
                        for k in range(KC):
                            pe.wait_ge(it_ready, n * KC + k + 1)
                            for h in range(KC):
                                o = KC * 2 * I0 + k * CH + h * P
                                last = three(PS[:, 4 + h, 0:CN], w0[s][:, 1, o:o + P], w0[s][:, 0, o:o + P],
                                             itL[:, k, :], itH[:, k, :], k == 0, k == KC - 1)
                        last.then_inc(dn_ready, 1)

            patches(1)
            mixer(1)
            pe.wait_ge(upm, 32)
            pe.wait_ge(gh_ready, 1 + 1)
            pe.wait_ge(g_ready, 2 + 2)
            for k in range(KC):
                last = pe.matmul(PS[:, 1, 0:E1], ones, rw[:, k, :], start=k == 0, stop=k == KC - 1)
            last.then_inc(wb_ready, 1)
            pe.wait_ge(rw_ready, 1)
            pe.wait_ge(g_ready, 2 + 2)

            def router_tile(t):
                pe.wait_ge(up_added, 2 * B + 2 * images_before(P * (t + 1)))
                if t >= 2:
                    pe.wait_ge(logits_ready, t - 1)
                for k in range(KC):
                    at = k % 2 * RC
                    last = pe.matmul(PS[:, RB[t % 2] + k // 2, at:at + P + E1], X[:, k, t * P:(t + 1) * P],
                                     eyeR[:, k, :], start=True, stop=True)
                last.then_inc(lt_ready, 1)

            t = 0
            for b in range(B):
                upsample(1, b)
                while t < TILES and images_before(P * (t + 1)) <= b:
                    router_tile(t)
                    t += 1
            while t < TILES:
                router_tile(t)
                t += 1
            pe.wait_ge(r_O, 1)
            O = R["O"][:, :, :].rearrange("p t e -> p (t e)")
            pe.matmul(PS[:, 2, 0:TILES * E1], triu, O, start=True, stop=True).then_inc(r_pre, 1)
            pe.matmul(PS[:, 3, 0:TILES * E1], ones, O, start=True, stop=True).then_inc(r_pre, 1)
            for k in range(2):
                for t in range(TILES):
                    if t % EJ == 0:
                        pe.wait_ge(oh_s_ready, k * E0 + t // EJ + 1)
                        pe.wait_ge(oh_numbered, k * E0 + t // EJ + 1)
                    last = pe.matmul(PS[:, 4, 0:MT], oh_s[:, k, t, :], oh_m[:, k, t, :],
                                     start=k == 0 and t == 0, stop=k == 1 and t == TILES - 1)
            last.then_inc(inverted, 1)
            pe.wait_ge(source_ready, 1)

            def transposes(i, turn, r, s):
                pe.wait_ge(xs_loaded[r], 16 * turn + 16)
                behind(pe, xt_ready, i)
                for k in range(KC):
                    last = pe.transpose(PS[:, s, k * P:(k + 1) * P], xs[:, r, k * P:(k + 1) * P], ident)
                last.then_inc(t_ready, 1)

            def slot_of(i):
                e = pe.value_load(tile_expert[0:1, i:i + 1] if isinstance(i, int) else tile_expert[0:1, ds(i, 1)],
                                  min_val=0, max_val=E1 - 1)
                return e, (e + 1) % 2

            def w1_chunk(slot, part, k):
                at = part * PIECE + k % 2 * 512
                return w1[:, ds(slot, 1), k // 2, at:at + 512]

            def gate_up(i, s, slot, ks):
                for k in ks:
                    wh = w1_chunk(slot, 0, k)
                    wl = w1_chunk(slot, 1, k)
                    pe.matmul(PS[:, 2 + s, :], xtH[:, s, k, :], wh, start=k == 0, stop=False)
                    pe.matmul(PS[:, 2 + s, :], xtL[:, s, k, :], wh, start=False, stop=False)
                    last = pe.matmul(PS[:, 2 + s, :], xtH[:, s, k, :], wl, start=False, stop=k == KC - 1)
                return last

            def hidden_transposes(i, s):
                pe.wait_ge(h_ready, i + 1)
                behind(pe, ht_ready, i)
                for k in range(2):
                    last = pe.transpose(PS[:, 4 + s, k * P:(k + 1) * P], hh[:, s, k * P:(k + 1) * P], ident)
                last.then_inc(th_ready, 1)

            def down(i, s, slot):
                pe.wait_ge(ht_ready, i + 1)
                behind(pe, y_out, i)
                for k in range(2):
                    wh = w1_chunk(slot, 0, KC + k)
                    wl = w1_chunk(slot, 1, KC + k)
                    pe.matmul(PS[:, 6 + s, :], htH[:, s, k, :], wh, start=k == 0, stop=False)
                    pe.matmul(PS[:, 6 + s, :], htL[:, s, k, :], wh, start=False, stop=False)
                    last = pe.matmul(PS[:, 6 + s, :], htH[:, s, k, :], wl, start=False, stop=k == 1)
                last.then_inc(d_ready, 1)

            def step(i, s, r_next, turn_next, first=False, last=False):
                if not last:
                    transposes(i + 1, turn_next, r_next, 1 - s)
                e, slot = slot_of(i)
                pe.wait_ge(w1_ready, e + 1)
                pe.wait_ge(xt_ready, i + 1)
                behind(pe, h_ready, i)
                gate_up(i, s, slot, (0, 1))
                if not first:
                    hidden_transposes(i - 1, 1 - s)
                gate_up(i, s, slot, (2, 3)).then_inc(g_up, 1)
                if not first:
                    _, before = slot_of(i - 1)
                    down(i - 1, 1 - s, before)

            transposes(0, 0, 0, 0)
            step(0, 0, 1, 0, first=True)
            for i in range(1, XSR):
                step(i, i % 2, (i + 1) % XSR, (i + 1) // XSR)
            with pe.Fori(1, MT // XSR - 1) as g:
                for r in range(XSR):
                    step(g * XSR + r, r % 2, (r + 1) % XSR, g + (r + 1) // XSR)
            for i in range(MT - XSR, MT):
                step(i, i % 2, (i + 1) % XSR, (i + 1) // XSR, last=i == MT - 1)
            hidden_transposes(MT - 1, 1)
            down(MT - 1, 1, slot_of(MT - 1)[1])

            for t in range(TILES):
                pe.wait_ge(gt_ready, t + 1)
                if t >= 4:
                    pe.wait_ge(f_added, t - 3)
                for k in range(KC):
                    last = pe.transpose(PS[:, t % 4, k * P:(k + 1) * P], gt[:, t % 2, k * P:(k + 1) * P], ident)
                last.then_inc(f_ready, 1)

        @block.scalar
        def _(act):
            def patch_sd(l, g):
                act.wait_ge(mv_done, l * NROW + GR * (g + 1))
                act.activation(SD[0:ROWT, g * GR:(g + 1) * GR], MV[0:ROWT, g * GR:(g + 1) * GR, 1], ACT.Sqrt,
                               bias=eps[0:ROWT, 0:1]).then_inc(sd_ready, 1)

            def patches(l):
                for g in range(NG):
                    for t in range(g * GR, (g + 1) * GR):
                        act.wait_ge(tp_ready, l * NROW + t + 1)
                        if t >= XR:
                            act.wait_ge(pooled, l * NROW + t - XR + 1)
                        act.activation(xtok[:, t % XR, :], PS[0:ROWT, t % 3, :], ACT.Copy).then_inc(xtok_ready, 1)
                    if g:
                        patch_sd(l, g - 1)
                patch_sd(l, NG - 1)
                for h in range(2):
                    act.wait_ge(ptok_T, l * 2 + h + 1)
                    act.activation(pT[:, :, h * TT:(h + 1) * TT],
                                   PS[:, 6 + h, 0:KC * TT].rearrange("p (k t) -> p k t", k=KC), ACT.Copy)\
                        .then_inc(p_ready, 1)

            def mixer(l):
                act.wait_ge(var_h, l * 2 + 2)
                act.activation(sdh[:, :], mvh[:, :, 1], ACT.Sqrt, bias=eps[0:TT, 1:2]).then_inc(sd_h, 1)
                act.wait_ge(tkT, l + 1)
                act.activation(tT[:, :, :], PS[0:HH, 2, 0:2 * NT].rearrange("p (h t) -> p h t", h=2), ACT.Copy)\
                    .then_inc(tT_ready, 1)
                act.wait_ge(acc_ready, l + 1)
                act.activation(uu[:, :, :], acc[:, :, :], ACT.Silu).then_inc(u_ready, 1)
                act.wait_ge(xz_ready, l * 2 + 2)
                act.activation(sz[:, :, :], PS[:, 4, 0:JC * NT].rearrange("p (j t) -> p j t", j=JC), ACT.Silu)\
                    .then_inc(z_ready, 1)
                act.wait_ge(mixw, (l + 1) * MIXW)
                act.activation(negA[:, :, :], alog[:, :, :], ACT.Exp).then_inc(ea_ready, 1)
                act.wait_ge(ab_ready, l + 1)
                act.activation(ab[:, :, :], ab[:, :, :], ACT.Exp, scale=-1.0).then_inc(ex_done, 1)
                act.wait_ge(ex_done, l * 2 + 1)
                act.activation(ab[:, :, :], ab[:, :, :], ACT.Ln, bias=1.0).then_inc(ex_done, 1)
                act.wait_ge(na_ready, l + 1)
                act.wait_ge(sp_ready, l + 1)
                act.wait_ge(a1_zero, l + 1)
                for j in range(JC):
                    if j >= 2:
                        act.wait_ge(ysum, l * JC + j - 1)
                    for n in range(NS):
                        last = act.activation(a1[:, j % 2, n, :].rearrange("p (b t) -> p b t", t=L)[:, :, 1:],
                                              delta[:, j, :].rearrange("p (b t) -> p b t", t=L)[:, :, 1:],
                                              ACT.Identity, scale=negA[:, j, n:n + 1], bias=1.0)
                    last.then_inc(a1_ready, 1)
                act.wait_ge(og_ready, l + 1)
                act.activation(gH[:, :, :], PS[0:TT, 0:2, :], ACT.Copy).then_inc(gh_ready, 1)

            patches(0)
            mixer(0)
            act.wait_ge(lmv_done, TILES)
            act.activation(SD[:, 0:TILES], MV[:, 0:TILES, 1], ACT.Sqrt, bias=eps[:, 1:2]).then_inc(lsd_ready, 1)
            act.wait_ge(mrT, 1)
            act.activation(statT[:, :], PS[0:2 * TILES, 2, 0:P], ACT.Copy).then_inc(statT_ready, 1)
            act.wait_ge(statT_ready, 1)
            act.wait_ge(stats_out, 16)

            with act.Fori(0, E0 * NC) as n:
                for m in range(KC):
                    act.wait_ge(gu_ready, n * KC + m + 1)
                    act.wait_ge(sg_free, n * KC + m + 1)
                    act.activation(sg[:, m % 2, :], PS[:, 2 * (m % 2), 0:CN], ACT.Silu).then_inc(sg_ready, 1)

            patches(1)
            mixer(1)
            act.wait_ge(wb_ready, 1)
            act.activation(wbar[:, :], PS[:, 1, 0:E1], ACT.Copy, scale=1.0 / CH).then_inc(wb_sb, 1)
            act.wait_ge(g_ready, 2 + 2)

            def finish(g):
                if g < TILES // GR:
                    act.wait_ge(lmv_done, TILES + (g + 1) * GR)
                    act.activation(SD[:, g * GR:(g + 1) * GR], MV[:, g * GR:(g + 1) * GR, 1], ACT.Sqrt,
                                   bias=eps[:, 1:2]).then_inc(lsd_ready, 1)
                if g:
                    act.wait_ge(nmr_ready, g)
                    for t in range((g - 1) * GR, g * GR):
                        act.activation(XN[:, t, :], XN[:, t, :], ACT.Identity, scale=RS[:, t:t + 1],
                                       bias=nmr[:, t:t + 1]).then_inc(xnorm, 1)

            for t in range(TILES):
                act.wait_ge(lt_ready, TILES + t + 1)
                act.activation(XN[:, t, :].rearrange("p (k n) -> p k n", n=P), router_banks(t)[:, :, 0:P], ACT.Copy)\
                    .then_inc(lt_free, 1)
                if t >= GR and t % GR == GR - 1:
                    finish(t // GR - 1)
            finish(TILES // GR - 1)
            act.wait_ge(rexp_in, 1)
            act.activation(R["e"][:, :, :], R["t"][:, :, :], ACT.Exp).then_inc(r_e, 1)
            finish(TILES // GR)
            act.wait_ge(r_pre, 2)
            act.activation(scT["tot"][:, :, :], PS[:, 3, 0:TILES * E1].rearrange("p (t e) -> p e t", e=E1), ACT.Copy)\
                .then_inc(r_tot, 1)

            def x_hi(i, s):
                act.wait_ge(t_ready, i + 1)
                behind(act, g_up, i)
                act.activation(xtH[:, s, :, :], PS[:, s, :].rearrange("p (k n) -> p k n", n=P), ACT.Copy)\
                    .then_inc(xt_hi, 1)

            def silu(i, s):
                act.wait_ge(g_up, i + 1)
                behind(act, h_ready, i)
                act.activation(sgt[:, s, :], PS[:, 2 + s, 0:512:2], ACT.Silu).then_inc(sgt_ready, 1)

            def h_hi(i, s):
                act.wait_ge(th_ready, i + 1)
                behind(act, d_ready, i)
                act.activation(htH[:, s, :, :], PS[:, 4 + s, 0:2 * P].rearrange("p (k n) -> p k n", n=P), ACT.Copy)\
                    .then_inc(ht_hi, 1)

            def y_copy(i, s, turn):
                act.wait_ge(d_ready, i + 1)
                if turn is not None:
                    act.wait_ge(y_stored[s], turn * 16)
                act.activation(ysb[:, s, :], PS[:, 6 + s, :], ACT.Copy).then_inc(y_out, 1)

            def step(i, s, turn, first=False, last=False):
                if not last:
                    x_hi(i + 1, 1 - s)
                if not first:
                    h_hi(i - 1, 1 - s)
                silu(i, s)
                if not first:
                    y_copy(i - 1, 1 - s, turn)

            act.wait_ge(source_ready, 1)
            x_hi(0, 0)
            step(0, 0, None, first=True)
            step(1, 1, None)
            step(2, 0, None)
            step(3, 1, 1)
            with act.Fori(2, MT // 2 - 1) as g:
                step(g * 2, 0, g - 1)
                step(g * 2 + 1, 1, g)
            step(MT - 2, 0, MT // 2 - 2)
            step(MT - 1, 1, MT // 2 - 1, last=True)
            h_hi(MT - 1, 1)
            y_copy(MT - 1, 1, MT // 2 - 1)

            for t in range(TILES):
                act.wait_ge(g_loaded[t % GRING], 32 * (t // GRING + 1))
                if t >= 2:
                    act.wait_ge(gt_ready, t - 1)
                act.activation(gs[:, t % 2, :], g1[:, t % GRING, :], ACT.Copy, scale=score[:, 0, t:t + 1])\
                    .then_inc(gs_ready, 1)

        @block.vector
        def _(v):
            steps = [0]

            def link(ins):
                steps[0] += 1
                ins.then_inc(dve, 1)
                v.wait_ge(dve, steps[0])

            def count(ins):
                steps[0] += 1
                return ins.then_inc(dve, 1)

            link(v.memset(eps[:, 0:1], 1e-6))
            link(v.memset(eps[:, 1:2], 1e-5))

            def patch_weights(l, g):
                sl = slice(g * GR, (g + 1) * GR)
                v.wait_ge(mv_done, l * NROW + (g + 1) * GR)
                v.wait_ge(sd_ready, l * NG + g + 1)
                link(v.reciprocal(RS[0:ROWT, sl], SD[0:ROWT, sl]))
                h, i = g * GR // HT, g * GR % HT
                own = RI[:, h, :].rearrange("p (i c) -> p i c", c=TT + 3)[:, i:i + GR, 0:3]
                v.tensor_tensor(own, RS[0:ROWT, sl].unsqueeze(2).broadcast_to((ROWT, GR, 3)),
                                ind[:, :].unsqueeze(1).broadcast_to((ROWT, GR, 3)), ALU.mult).then_inc(ri_ready, 1)

            def centre_pooled(l, h):
                v.wait_ge(pooled, l * NROW + (h + 1) * HT)
                link(v.bn_stats(sth[:, h, :], PS[0:TT, 4 + h, :]))
                link(v.bn_aggr(mvh[:, h, :], sth[:, h, :]))
                v.tensor_scalar(ptok[:, h, :], PS[0:TT, 4 + h, :], mvh[:, h, 0:1], None, ALU.subtract)\
                    .then_inc(ptok_ready, 1)

            def patches(l):
                v.wait_ge(consts, 32)
                for g in range(NG):
                    if g in (0, NG // 4):
                        link(v.memset(RI[:, 4 * g // NG, :], 0.0))
                    if g == NG - 2:
                        v.wait_ge(mixw, (l + 1) * MIXW)
                        v.tensor_copy(upM[:, :, :], upS[:, :, :]).then_inc(g_ready, 1)
                    for t in range(g * GR, (g + 1) * GR):
                        v.wait_ge(xtok_ready, l * NROW + t + 1)
                        v.bn_stats(ST6[0:ROWT, g % 2, t % GR, :], xtok[:, t % XR, :]).then_inc(st_done, 1)
                    v.wait_ge(st_done, l * NROW + (g + 1) * GR)
                    for t in range(g * GR, (g + 1) * GR):
                        v.bn_aggr(MV[0:ROWT, t, :], ST6[0:ROWT, g % 2, t % GR, :]).then_inc(mv_done, 1)
                    if g:
                        patch_weights(l, g - 1)
                patch_weights(l, NG - 1)
                centre_pooled(l, 0)
                centre_pooled(l, 1)

            def mixer(l):
                v.wait_ge(tok_ready, l + 1)
                link(v.tensor_tensor(tk[:, :, :], PS[0:TT, 0:2, 0:HID],
                                     vhid[:, 0:1, :].broadcast_to((TT, 2, HID)), ALU.add))
                for tt in range(2):
                    link(v.bn_stats(sth[:, tt, :], tk[:, tt, :]))
                    v.bn_aggr(mvh[:, tt, :], sth[:, tt, :]).then_inc(var_h, 1)
                v.wait_ge(var_h, l * 2 + 2)
                v.wait_ge(sd_h, l + 1)
                link(v.reciprocal(rsh[:, :], sdh[:, :]))
                for tt in range(2):
                    link(v.tensor_scalar(tk[:, tt, :], tk[:, tt, :], mvh[:, tt, 0:1], rsh[:, tt:tt + 1],
                                         ALU.subtract, ALU.mult))
                link(v.tensor_tensor(tk[:, :, :], tk[:, :, :], vhid[:, 1:2, :].broadcast_to((TT, 2, HID)), ALU.mult))
                v.tensor_tensor(tk[:, :, :], tk[:, :, :], vhid[:, 2:3, :].broadcast_to((TT, 2, HID)), ALU.add)\
                    .then_inc(tk_ready, 1)
                v.wait_ge(xz_ready, l * 2 + 1)
                img = lambda ap: ap.rearrange("p (b t) -> p b t", t=L)
                for j in range(JC):
                    src = PS[:, 3, j * NT:(j + 1) * NT]
                    link(v.tensor_scalar(acc[:, j, :], src, vinn[:, j, 1:2], vinn[:, j, 3:4], ALU.mult, ALU.add))
                    link(v.scalar_tensor_tensor(img(acc[:, j, :])[:, :, 1:], img(src)[:, :, :L - 1], vinn[:, j, 0:1],
                                                img(acc[:, j, :])[:, :, 1:], ALU.mult, ALU.add))
                    last = v.scalar_tensor_tensor(img(acc[:, j, :])[:, :, :L - 1], img(src)[:, :, 1:], vinn[:, j, 2:3],
                                                  img(acc[:, j, :])[:, :, :L - 1], ALU.mult, ALU.add)
                    if j < JC - 1:
                        link(last)
                last.then_inc(acc_ready, 1)
                v.wait_ge(dbc_ready, l * 2 + 1)
                v.tensor_copy(bc[:, :], PS[0:2 * NS, 5, 0:NT]).then_inc(bc_ready, 1)
                v.wait_ge(dbc_ready, l * 2 + 2)
                v.tensor_copy(dl[:, :], PS[0:RANK, 6, 0:NT]).then_inc(dl_ready, 1)
                v.wait_ge(ea_ready, l + 1)
                v.tensor_scalar(negA[:, :, :], negA[:, :, :], -1.0, None, ALU.mult).then_inc(na_ready, 1)
                v.wait_ge(dt_ready, l + 1)
                for j in range(JC):
                    link(v.tensor_scalar(dx[:, j, :], PS[:, 7, j * NT:(j + 1) * NT], vinn[:, j, 4:5], None, ALU.add))
                v.scalar_tensor_tensor(ab[:, :, :], dx[:, :, :], -1.0, dx[:, :, :], ALU.mult, ALU.max)\
                    .then_inc(ab_ready, 1)
                forget = lambda s: a1[:, s, :, :].rearrange("p n (b t) -> p (n b) t", t=L)[:, :, 0:1]
                link(v.memset(forget(0), 0.0))
                v.memset(forget(1), 0.0).then_inc(a1_zero, 1)
                v.wait_ge(ex_done, l * 2 + 2)
                v.scalar_tensor_tensor(delta[:, :, :], dx[:, :, :], 0.0, ab[:, :, :], ALU.max, ALU.add)\
                    .then_inc(sp_ready, 1)
                v.wait_ge(sp_ready, l + 1)
                v.wait_ge(u_ready, l + 1)
                v.tensor_tensor(du[:, :, :], delta[:, :, :], uu[:, :, :], ALU.mult).then_inc(du_ready, 1)
                v.wait_ge(bc_in, l * 16 + 16)
                v.wait_ge(a1_zero, l + 1)
                flat = lambda ap: ap.rearrange("p n t -> p (n t)")
                for j in range(JC):
                    if j >= 2:
                        v.wait_ge(ysum, l * JC + j - 1)
                        link(v.memset(forget(j % 2), 0.0))
                    v.wait_ge(a1_ready, l * JC + j + 1)
                    v.wait_ge(db_ready, l * JC + j + 1)
                    if j >= 1:
                        v.wait_ge(hc_ready, l * JC + j)
                    v.tensor_tensor_scan(flat(hs[:, :, :]), flat(a1[:, j % 2, :, :]), flat(db[:, j % 2, :, :]), 0.0,
                                         ALU.mult, ALU.add).then_inc(scanned, 1)
                    v.wait_ge(scanned, l * JC + j + 1)
                    v.tensor_tensor(a1[:, j % 2, :, :], hs[:, :, :], Bb[:, NS:, :], ALU.mult).then_inc(hc_ready, 1)
                v.wait_ge(hc_ready, (l + 1) * JC)
                v.wait_ge(ysum, (l + 1) * JC)
                for j in range(JC):
                    link(v.scalar_tensor_tensor(yy[:, j, :], uu[:, j, :], vinn[:, j, 5:6],
                                                PS[:, 2, j * NT:(j + 1) * NT], ALU.mult, ALU.add))
                v.wait_ge(z_ready, l + 1)
                v.tensor_tensor(yy[:, :, :], yy[:, :, :], sz[:, :, :], ALU.mult).then_inc(y_ready, 1)
                v.wait_ge(gh_ready, l + 1)
                v.tensor_tensor(gL[:, :, :], PS[0:TT, 0:2, :], gH[:, :, :].bitcast(f32), ALU.subtract)\
                    .then_inc(g_ready, 1)
                v.wait_ge(g_ready, l * 2 + 2)

            def add_upsampled(l, b):
                for half in range(2):
                    v.wait_ge(up_ready, l * 2 * B + 2 * b + half + 1)
                    dst = X[:, 2 * half:2 * half + 2, b * S:(b + 1) * S]
                    v.tensor_tensor(dst, dst, PS[:, 2 + 2 * half:4 + 2 * half, 0:S], ALU.add).then_inc(up_added, 1)

            def token_stats(l, q, src, at, read):
                v.bn_stats(ST6[:, (q // GR) % 2, q % GR, :], src).then_inc(read, 1)
                if q % GR == GR - 1:
                    v.wait_ge(read, q + 1)
                    for i in range(q + 1 - GR, q + 1):
                        v.bn_aggr(MV[:, at(i), :], ST6[:, (i // GR) % 2, i % GR, :]).then_inc(lmv_done, 1)

            def first_stats(q):
                v.wait_ge(lt_ready, q + 1)
                token_stats(0, q, PS[:, TB[q % len(TB)], :], lambda i: (i % E0) * EJ + i // E0, lt_free)

            patches(0)
            mixer(0)
            q = 0
            for b in range(B):
                add_upsampled(0, b)
                while q < TILES and images_before(E0 * P * (q // E0 + 1)) <= b:
                    first_stats(q)
                    q += 1
            while q < TILES:
                first_stats(q)
                q += 1
            v.wait_ge(lmv_done, TILES)
            v.wait_ge(lsd_ready, 1)
            v.reciprocal(MR[:, 0:TILES], SD[:, 0:TILES]).then_inc(mr_ready, 1)
            v.wait_ge(mr_ready, 1)
            v.tensor_tensor(MR[:, TILES:], MR[:, 0:TILES], MV[:, 0:TILES, 0], ALU.mult).then_inc(mr_ready, 1)

            v.wait_ge(stats_out, 16)
            for free, n in ((gu_free, 2), (sg_free, 2), (rm_free, 1), (dn_free, 1)):
                v.sem_inc(free, n)

            def tokens(n):
                e, c = n // NC, n % NC
                return Xe[:, :, e, c * CN:(c + 1) * CN] if isinstance(n, int) else \
                    Xe[:, :, ds(e, 1), ds(c * CN, CN)].rearrange("p k e n -> p k (e n)")

            def scale(n):
                v.wait_ge(rm_loaded, n * 16 + 16)
                v.tensor_tensor(xr[:, :, :], tokens(n), rmb[:, 0:1, :].broadcast_to((P, KC, CN)), ALU.mult)\
                    .then_inc(xr_done, 1)
                v.wait_ge(xr_done, n * 2 + 1)

            def shift(n):
                v.tensor_tensor(xr[:, :, :], xr[:, :, :], rmb[:, 1:2, :].broadcast_to((P, KC, CN)), ALU.subtract)\
                    .then_inc(xr_done, 1)
                v.wait_ge(xr_done, n * 2 + 2)
                v.sem_inc(rm_free, 1)

            def split(n):
                if not isinstance(n, int) or n:
                    v.wait_ge(gu_ready, n * KC)
                v.tensor_copy(xnH[:, :, :], xr[:, :, :]).then_inc(it_step, 1)
                v.wait_ge(it_step, n * (2 * KC + 1) + 1)
                v.tensor_tensor(xnL[:, :, :], xr[:, :, :], xnH[:, :, :].bitcast(f32), ALU.subtract)\
                    .then_inc(xn_ready, 1)
                v.wait_ge(xn_ready, n + 1)

            def chunk(n, last=False):
                for m in range(KC):
                    v.wait_ge(sg_ready, n * KC + m + 1)
                    v.tensor_tensor(sg[:, m % 2, :], sg[:, m % 2, :], PS[:, 2 * (m % 2) + 1, 0:CN], ALU.mult)\
                        .then_inc(gu_free, 1)
                    v.wait_ge(gu_free, n * KC + m + 3)
                    v.tensor_copy(itH[:, m, :], sg[:, m % 2, :]).then_inc(it_step, 1)
                    v.wait_ge(it_step, n * (2 * KC + 1) + (2 * m + 2))
                    v.tensor_tensor(itL[:, m, :], sg[:, m % 2, :], itH[:, m, :].bitcast(f32), ALU.subtract)\
                        .then_inc(it_step, 1)
                    v.wait_ge(it_step, n * (2 * KC + 1) + (2 * m + 3))
                    v.sem_inc(it_ready, 1)
                    v.sem_inc(sg_free, 1)
                    if m == 0 and not last:
                        scale(n + 1)
                    if m == 1 and not last:
                        shift(n + 1)
                if not last:
                    split(n + 1)
                v.wait_ge(dn_ready, n + 1)
                dst = tokens(n)
                v.tensor_tensor(dst, dst, PS[:, 4:8, 0:CN], ALU.add).then_inc(dn_free, 1)

            scale(0)
            shift(0)
            split(0)
            with v.Fori(0, E0 * NC - 1) as n:
                chunk(n)
            chunk(E0 * NC - 1, last=True)
            v.wait_ge(dn_free, E0 * NC + 1)

            patches(1)
            mixer(1)
            v.wait_ge(wb_sb, 1)
            v.wait_ge(upm, 32)
            link(v.tensor_copy(eyeR[:, :, 0:P], ident.unsqueeze(1).broadcast_to((P, KC, P))))
            v.tensor_tensor(rw, rw, wbar[:, :].unsqueeze(1).broadcast_to((P, KC, E1)), ALU.subtract)\
                .then_inc(rw_ready, 1)
            def finish(g):
                sl = slice(g * GR, (g + 1) * GR)
                v.wait_ge(lsd_ready, g + 2)
                link(v.reciprocal(RS[:, sl], SD[:, sl]))
                v.scalar_tensor_tensor(nmr[:, sl], MV[:, sl, 0], -1.0, RS[:, sl], ALU.mult, ALU.mult)\
                    .then_inc(nmr_ready, 1)

            def router_tile(t):
                v.wait_ge(lt_free, TILES + t + 1)
                v.tensor_reduce(logits[:, t, :], router_banks(t)[:, :, P:P + E1].rearrange("p k e -> p e k"), AX.X,
                                ALU.add).then_inc(logits_ready, 1)
                token_stats(1, t, XN[:, t, :], lambda i: i, lst_done)
                if t >= GR and t % GR == GR - 1:
                    finish(t // GR - 1)

            t = 0
            for b in range(B):
                add_upsampled(1, b)
                while t < TILES and images_before(P * (t + 1)) <= b:
                    router_tile(t)
                    t += 1
            while t < TILES:
                router_tile(t)
                t += 1
            finish(TILES // GR - 1)

            full = (P, TILES, E1)
            by_tile = lambda ap: ap.unsqueeze(2).broadcast_to(full)
            by_expert = lambda ap: ap.unsqueeze(1).broadcast_to(full)
            A = {n: ap[:, :, :] for n, ap in R.items()}
            Q = {n: ap[:, :] for n, ap in q36.items()}
            v.wait_ge(logits_ready, TILES)
            v.wait_ge(upm, 32)
            link(v.tensor_tensor(A["log"], logits[:, :, :],
                                 by_tile(RS[:, 0:TILES]), ALU.mult))
            link(v.tensor_reduce(Q["mx"], A["log"], AX.X, ALU.max))
            v.tensor_tensor(A["t"], A["log"], by_tile(Q["mx"]), ALU.subtract).then_inc(rexp_in, 1)
            v.wait_ge(r_e, 1)
            link(v.tensor_reduce(Q["sm"], A["e"], AX.X, ALU.add))
            link(v.reciprocal(Q["rs"], Q["sm"]))
            link(v.tensor_tensor(A["p"], A["e"], by_tile(Q["rs"]), ALU.mult))

            def best(m, onehot):
                link(v.tensor_reduce(m, A["p"], AX.X, ALU.max))
                link(v.tensor_tensor(A["t"], A["p"], by_tile(m), ALU.is_equal))
                link(v.tensor_tensor(A["t"], A["t"], by_expert(w8), ALU.mult))
                link(v.tensor_reduce(Q["k"], A["t"], AX.X, ALU.max))
                link(v.tensor_tensor(onehot, by_expert(w8), by_tile(Q["k"]), ALU.is_equal))

            best(Q["m1"], A["oh1"])
            link(v.scalar_tensor_tensor(A["p"], A["oh1"], -2.0, A["p"], ALU.mult, ALU.add))
            best(Q["m2"], A["oh2"])
            v.tensor_tensor(A["O"], A["oh1"], A["oh2"], ALU.add).then_inc(r_O, 1)
            link(v.tensor_tensor(Q["den"], Q["m1"], Q["m2"], ALU.add))
            link(v.reciprocal(Q["den"], Q["den"]))
            link(v.tensor_tensor(score[:, 0, :], Q["m1"], Q["den"], ALU.mult))
            link(v.tensor_tensor(score[:, 1, :], Q["m2"], Q["den"], ALU.mult))
            v.wait_ge(r_tot, 1)
            tot, inc, exc, cmp = (scT[n][:, :, :] for n in ("tot", "inc", "exc", "cmp"))
            nt, end, base = (e8[n][:, :] for n in ("nt", "end", "base"))
            flat = lambda ap: ap.rearrange("p e t -> p (e t)")
            link(v.tensor_tensor_scan(flat(inc), jmask, flat(tot), 0.0, ALU.mult, ALU.add))
            link(v.tensor_tensor(exc, inc, tot, ALU.subtract))
            link(v.tensor_tensor(cmp, inc[:, :, TILES - 1:TILES].broadcast_to((P, E1, TILES)),
                                 j128.unsqueeze(1).broadcast_to((P, E1, TILES)), ALU.is_gt))
            link(v.tensor_reduce(nt, cmp, AX.X, ALU.add))
            link(v.tensor_scalar(nt, nt, 1.0, None, ALU.max))
            link(v.tensor_tensor_scan(end, one8, nt, 0.0, ALU.mult, ALU.add))
            link(v.tensor_tensor(base, end, nt, ALU.subtract))
            link(v.tensor_scalar(base, base, float(P), None, ALU.mult))
            v.wait_ge(r_pre, 2)
            link(v.tensor_tensor(A["pe"], PS[:, 2, 0:TILES * E1].rearrange("p (t e) -> p t e", e=E1),
                                 exc.rearrange("p e t -> p t e"), ALU.add))
            link(v.tensor_tensor(A["pe"], A["pe"], by_expert(base), ALU.add))
            for k, oh in enumerate(("oh1", "oh2")):
                link(v.tensor_tensor(A["t"], A["pe"], A[oh], ALU.mult))
                link(v.tensor_reduce(Q["pf"], A["t"], AX.X, ALU.add))
                link(v.tensor_copy(pos[:, k, :], Q["pf"]))
                link(v.tensor_scalar(row_m[:, k, :], Q["pf"], 1.0 / P, (1 - P) / (2.0 * P), ALU.mult, ALU.add))
                link(v.tensor_scalar(row_m[:, k, :], row_m[:, k, :], ROUND, None, ALU.add))
                link(v.tensor_scalar(row_m[:, k, :], row_m[:, k, :], ROUND, None, ALU.subtract))
                link(v.scalar_tensor_tensor(row_s[:, k, :], row_m[:, k, :], -float(P), Q["pf"], ALU.mult, ALU.add))
            v.wait_ge(xn_stored[0], 16 * XNG)
            for n in range(2 * E0):
                k, sl = n // E0, slice(n % E0 * EJ, (n % E0 + 1) * EJ)
                for oh, index, row, size, signal in ((oh_m, iMT, row_m, MT, oh_m_ready),
                                                     (oh_s, i128, row_s, P, oh_s_ready)):
                    v.tensor_tensor(oh[:, k, sl, :], index.unsqueeze(1).broadcast_to((P, EJ, size)),
                                    row[:, k, sl].unsqueeze(2).broadcast_to((P, EJ, size)), ALU.is_equal)\
                        .then_inc(signal, 1)
            link(v.tensor_copy(tile_end[:, :], end))
            link(v.tensor_tensor(tcmp[:, :, :], end[:, 0:E1 - 1].unsqueeze(1).broadcast_to((P, MT, E1 - 1)),
                                 iMT.unsqueeze(2).broadcast_to((P, MT, E1 - 1)), ALU.is_le))
            link(v.tensor_reduce(texp[:, :], tcmp[:, :, :], AX.X, ALU.add))
            link(v.tensor_copy(tile_expert[:, :], texp[:, :]))
            v.wait_ge(inverted, 1)
            link(v.tensor_scalar(found[:, 0, :], PS[:, 4, 0:MT], 0.0, None, ALU.is_gt))
            link(v.scalar_tensor_tensor(found[:, 1, :], PS[:, 4, 0:MT], float(HALF), found[:, 0, :],
                                        ALU.add, ALU.subtract))
            v.tensor_copy(source[:, :], found[:, 1, :]).then_inc(source_ready, 1)
            v.wait_ge(source_ready, 1)

            def x_lo(i, s):
                v.wait_ge(xt_hi, i + 1)
                v.tensor_tensor(xtL[:, s, :, :], PS[:, s, :].rearrange("p (k n) -> p k n", n=P),
                                xtH[:, s, :, :].bitcast(f32), ALU.subtract).then_inc(xt_ready, 1)

            def hidden(i, s):
                v.wait_ge(sgt_ready, i + 1)
                behind(v, th_ready, i)
                v.tensor_tensor(hh[:, s, :], sgt[:, s, :], PS[:, 2 + s, 1:512:2], ALU.mult).then_inc(h_ready, 1)

            def h_lo(i, s):
                v.wait_ge(ht_hi, i + 1)
                v.tensor_tensor(htL[:, s, :, :], PS[:, 4 + s, 0:2 * P].rearrange("p (k n) -> p k n", n=P),
                                htH[:, s, :, :].bitcast(f32), ALU.subtract).then_inc(ht_ready, 1)

            def step(i, s, first=False, last=False):
                if not last:
                    x_lo(i + 1, 1 - s)
                if not first:
                    h_lo(i - 1, 1 - s)
                hidden(i, s)

            x_lo(0, 0)
            step(0, 0, first=True)
            step(1, 1)
            with v.Fori(1, MT // 2 - 1) as g:
                for s in range(2):
                    step(g * 2 + s, s)
            step(MT - 2, 0)
            step(MT - 1, 1, last=True)
            h_lo(MT - 1, 1)

            def add_out(t):
                v.wait_ge(f_ready, t + 1)
                dst = X[:, :, t * P:(t + 1) * P]
                v.tensor_tensor(dst, dst, PS[:, t % 4, :].rearrange("p (k n) -> p k n", n=P), ALU.add)\
                    .then_inc(f_added, 1)

            for t in range(TILES):
                v.wait_ge(gs_ready, t + 1)
                if t >= 2:
                    v.wait_ge(f_ready, t - 1)
                v.scalar_tensor_tensor(gt[:, t % 2, :], g2[:, t % GRING, :], score[:, 1, t:t + 1], gs[:, t % 2, :],
                                       ALU.mult, ALU.add).then_inc(gt_ready, 1)
                if t:
                    add_out(t - 1)
            add_out(TILES - 1)


def bilinear():
    def axis(n):
        at = np.maximum((np.arange(n, dtype=np.float32) + np.float32(0.5)) * np.float32(3 / n) - np.float32(0.5), 0)
        i0 = np.minimum(np.floor(at).astype(np.int32), 2)
        i1 = np.minimum(i0 + 1, 2)
        w = at - i0.astype(np.float32)
        m = np.zeros((3, n), np.float32)
        for o in range(n):
            m[i0[o], o] += 1 - w[o]
            m[i1[o], o] += w[o]
        return m
    return np.einsum("ay,bx->abyx", axis(H), axis(W)).reshape(L, S)


def constants():
    mats = np.stack([np.eye(P), np.ones((P, P)), np.triu(np.ones((P, P)), 1)], 1).astype(np.float32)
    token = np.arange(ROWT)
    ind = (((token % W) // (W // 3))[:, None] == np.arange(3)).astype(np.float32) / (H // 3 * W // 3)
    up = np.zeros((IB, L, IB, S), np.float32)
    for b in range(IB):
        up[b, :, b] = bilinear()
    mask = np.ones((E1, TILES), np.float32)
    mask[:, 0] = 0
    row = np.concatenate([E1 - np.arange(E1), P * np.arange(TILES), np.arange(MT), mask.ravel(), np.arange(P)])
    token = P * np.arange(TILES) + np.arange(P)[:, None]
    number = token - HALF + (token >= HALF)
    rout = np.concatenate([np.tile(row, (P, 1)), number], 1).astype(np.float32)
    return {"c_mat": mats, "c_ind": ind, "c_up": up.reshape(TT, IB, S), "c_rout": rout}


def kernel(**inputs):
    import concourse.bacc as bacc
    from concourse.bass_utils import run_bass_kernel_spmd

    def both(name):
        return [np.asarray(inputs[f"L{l}_conv_{name}"]) for l in range(2)]

    def rows(a, n):
        return a.reshape(n, a.shape[0] // n, *a.shape[1:]).swapaxes(0, 1)

    arrays = {"x": np.asarray(inputs["x"]).reshape(B, CH, S)}
    arrays |= constants()
    arrays["pe_W"] = np.stack([rows(a, KC) for a in both("pe_W")])
    arrays["vec_hid"] = np.stack([np.stack(v) for v in zip(both("pe_b"), both("ln_g"), both("ln_b"))])
    arrays["in_W"] = np.stack([rows(a, 2) for a in both("in_W")])
    arrays["vec_inner"] = np.stack([
        rows(np.concatenate([w.reshape(INNER, 3), cb[:, None], tb[:, None], d[:, None]], 1), JC)
        for w, cb, tb, d in zip(both("conv_w"), both("conv_b"), both("dt_b"), both("D_param"))])
    arrays["a_log"] = np.stack([rows(a, JC) for a in both("A_log")])
    arrays["xproj"] = np.stack([rows(a, JC) for a in both("xproj_W")])
    arrays["dt_W"] = np.stack(both("dt_W"))
    arrays["out_W"] = np.stack([rows(a, JC) for a in both("out_W")])
    gu0, dn0 = np.asarray(inputs["L0_ffn_gate_up_proj"]), np.asarray(inputs["L0_ffn_down_proj"])
    gu1, dn1 = np.asarray(inputs["L1_ffn_expert_gate_up"]), np.asarray(inputs["L1_ffn_expert_down"])

    def pieces(a, n):
        e, r, c = a.shape
        return a.reshape(e, n, r // (n * P), P, c).swapaxes(2, 3).reshape(e, n, P, PIECE)

    w0 = np.concatenate([pieces(gu0, KC), pieces(dn0, 2)], 1).reshape(NP0, P, PIECE)
    w1 = np.concatenate([pieces(gu1, 2), pieces(dn1, 1)], 1).reshape(NP1, P, PIECE)
    arrays["w_ffn"] = np.concatenate([w0, w1])
    arrays["router"] = rows(np.asarray(inputs["L1_ffn_router_gate"]).T, KC)

    nc = bacc.Bacc("TRN2", target_bir_lowering=False, num_devices=1)
    data, args = {}, []
    for name, a in arrays.items():
        a = np.ascontiguousarray(a)
        data[f"in_{name}"] = a
        args.append(nc.dram_tensor(f"in_{name}", a.shape, mybir.dt.from_np(a.dtype), kind="ExternalInput").ap())
    args.append(nc.dram_tensor("out_x", (B, CH, S), mybir.dt.float32, kind="ExternalOutput").ap())
    metaformer(nc, *args)
    r = run_bass_kernel_spmd(nc, [data], core_ids=[0])
    return r.results[0]["out_x"].reshape(B, CH, H, W)
```
